# Optimizing a Trainium2 kernel written in Bass

```python
import numpy as np
import jax
import jax.numpy as jnp

def _softmax(x, axis=-1):
    return jax.nn.softmax(x, axis=axis)
def _gelu(x):
    return jax.nn.gelu(x, approximate=True)
def _silu(x):
    return jax.nn.silu(x)
def _sigmoid(x):
    return jax.nn.sigmoid(x)
def _layernorm(x, axis=-1, eps=1e-5):
    m = jnp.mean(x, axis=axis, keepdims=True)
    v = jnp.var(x, axis=axis, keepdims=True)
    return (x - m) / jnp.sqrt(v + eps)
def _scatter_add(tgt, idx, src, axis=0):
    return tgt.at[idx].add(src)
def _segment_sum(src, seg, n):
    return jax.ops.segment_sum(src, seg, n)

kernel_name = 'mk_conv_attn_hybrid_d2_conv_nchw512_59d656'

def setup_inputs(seed: int = 0):
    np.random.seed(seed)
    _w = jnp.asarray
    def _rec_inputs():
        import jax
        import jax.numpy as jnp
        _gk = jax.random.key(seed)
        x = -0.0002928 + 1 * jax.random.normal(jax.random.fold_in(_gk, 1), (8, 512, 32, 32), jnp.float32)
        return x
    x = _rec_inputs()
    def _L0_conv_setup():
        import jax, jax.numpy as jnp
        import numpy as np
        import math
        N_GROUPS = 32
        N_HEADS = 8
        EPS = 1e-05

        def _group_norm(x, w, b):
            B, C, L = x.shape
            xg = x.reshape(B, N_GROUPS, C // N_GROUPS, L)
            mean = jnp.mean(xg, axis=(2, 3), keepdims=True)
            var = jnp.var(xg, axis=(2, 3), keepdims=True)
            xn = ((xg - mean) * jax.lax.rsqrt(var + EPS)).reshape(B, C, L)
            return xn * w[None, :, None] + b[None, :, None]
        key = jax.random.key(seed)
        ks = jax.random.split(key, 6)
        B, C, Hs, Ws = (8, 512, 32, 32)
        x = jax.random.normal(ks[0], (B, C, Hs, Ws), dtype=jnp.float32)
        gn_w = jnp.ones((C,), dtype=jnp.float32)
        gn_b = jnp.zeros((C,), dtype=jnp.float32)
        w_qkv = jax.random.normal(ks[1], (3 * C, C), dtype=jnp.float32) * 0.02
        b_qkv = jax.random.normal(ks[2], (3 * C,), dtype=jnp.float32) * 0.02
        w_proj = jax.random.normal(ks[3], (C, C), dtype=jnp.float32) * 0.02
        b_proj = jax.random.normal(ks[4], (C,), dtype=jnp.float32) * 0.02
        return {'x': x, 'gn_w': gn_w, 'gn_b': gn_b, 'w_qkv': w_qkv, 'b_qkv': b_qkv, 'w_proj': w_proj, 'b_proj': b_proj}
    _L0_conv_all = _L0_conv_setup()
    _L0_conv_in = {k: v for k, v in _L0_conv_all.items() if k in ('gn_w', 'gn_b', 'w_qkv', 'b_qkv', 'w_proj', 'b_proj', )}
    del _L0_conv_all

    def _L1_attn_setup():
        import jax, jax.numpy as jnp
        import numpy as np
        B, T, D, H = (4, 8192, 512, 8)
        HD = D // H
        key = jax.random.key(seed)
        k0, k1, k2 = jax.random.split(key, 3)
        std = 1.0 / np.sqrt(D)
        return {'x': jax.random.normal(k0, (B, T, D), dtype=jnp.float32), 'W_qkv': jax.random.normal(k1, (3 * D, D), dtype=jnp.float32) * std, 'b_qkv': jnp.zeros((3 * D,), dtype=jnp.float32), 'W_out': jax.random.normal(k2, (D, D), dtype=jnp.float32) * std, 'b_out': jnp.zeros((D,), dtype=jnp.float32)}
    _L1_attn_all = _L1_attn_setup()
    _L1_attn_in = {k: v for k, v in _L1_attn_all.items() if k in ('W_qkv', 'b_qkv', 'W_out', 'b_out', )}
    del _L1_attn_all

    def _L1_ffn_setup():
        import jax, jax.numpy as jnp
        import numpy as np
        BLOCK = 64
        NF4_TABLE = jnp.array([-1.0, -0.6961928009986877, -0.5250730514526367, -0.39491748809814453, -0.28444138169288635, -0.18477343022823334, -0.09105003625154495, 0.0, 0.07958029955625534, 0.16093020141124725, 0.24611230194568634, 0.33791524171829224, 0.44070982933044434, 0.5626170039176941, 0.7229568362236023, 1.0], dtype=jnp.float32)

        def _dequant_nf4(qidx, scales):
            w = NF4_TABLE[qidx].reshape(-1, BLOCK) * scales[:, None]
            return w.reshape(qidx.shape)
        key = jax.random.key(seed)
        k1, k2, k3, k4 = jax.random.split(key, 4)
        x = jax.random.normal(k1, (4, 8192, 512), dtype=jnp.float32)
        qidx = jax.random.randint(k2, (512, 512), 0, 16, dtype=jnp.int32)
        scales = jax.random.uniform(k3, (4096,), dtype=jnp.float32)
        W = jax.random.normal(k4, (512, 512), dtype=jnp.float32) * (1.0 / np.sqrt(512.0))
        return {'x': x, 'qidx': qidx, 'scales': scales, 'W': W}
    _L1_ffn_all = _L1_ffn_setup()
    _L1_ffn_in = {k: v for k, v in _L1_ffn_all.items() if k in ('qidx', 'scales', 'W', )}
    del _L1_ffn_all

    return {
        "x": x,
        "L0_conv_gn_w": _L0_conv_in["gn_w"],
        "L0_conv_gn_b": _L0_conv_in["gn_b"],
        "L0_conv_w_qkv": _L0_conv_in["w_qkv"],
        "L0_conv_b_qkv": _L0_conv_in["b_qkv"],
        "L0_conv_w_proj": _L0_conv_in["w_proj"],
        "L0_conv_b_proj": _L0_conv_in["b_proj"],
        "L1_attn_W_qkv": _L1_attn_in["W_qkv"],
        "L1_attn_b_qkv": _L1_attn_in["b_qkv"],
        "L1_attn_W_out": _L1_attn_in["W_out"],
        "L1_attn_b_out": _L1_attn_in["b_out"],
        "L1_ffn_qidx": _L1_ffn_in["qidx"],
        "L1_ffn_scales": _L1_ffn_in["scales"],
        "L1_ffn_W": _L1_ffn_in["W"],
    }

def reference(x, L0_conv_gn_w, L0_conv_gn_b, L0_conv_w_qkv, L0_conv_b_qkv, L0_conv_w_proj, L0_conv_b_proj, L1_attn_W_qkv, L1_attn_b_qkv, L1_attn_W_out, L1_attn_b_out, L1_ffn_qidx, L1_ffn_scales, L1_ffn_W):
    import jax
    import jax.numpy as jnp
    def _L0_conv_ref(x, gn_w, gn_b, w_qkv, b_qkv, w_proj, b_proj):
        import jax, jax.numpy as jnp
        import numpy as np
        import math
        N_GROUPS = 32
        N_HEADS = 8
        EPS = 1e-05

        def _group_norm(x, w, b):
            B, C, L = x.shape
            xg = x.reshape(B, N_GROUPS, C // N_GROUPS, L)
            mean = jnp.mean(xg, axis=(2, 3), keepdims=True)
            var = jnp.var(xg, axis=(2, 3), keepdims=True)
            xn = ((xg - mean) * jax.lax.rsqrt(var + EPS)).reshape(B, C, L)
            return xn * w[None, :, None] + b[None, :, None]
        B, C, Hs, Ws = x.shape
        L = Hs * Ws
        xf = x.reshape(B, C, L)
        xn = _group_norm(xf, gn_w, gn_b)
        qkv = jnp.einsum('oc,bcl->bol', w_qkv, xn) + b_qkv[None, :, None]
        ch = C // N_HEADS
        qkv = qkv.reshape(B * N_HEADS, 3 * ch, L)
        q, k, v = (qkv[:, :ch], qkv[:, ch:2 * ch], qkv[:, 2 * ch:])
        scale = 1.0 / math.sqrt(math.sqrt(ch))
        weight = jnp.einsum('bct,bcs->bts', q * scale, k * scale)
        weight = jax.nn.softmax(weight.astype(jnp.float32), axis=1).astype(weight.dtype)
        a = jnp.einsum('bts,bcs->bct', weight, v)
        a = a.reshape(B, C, L)
        h = jnp.einsum('oc,bcl->bol', w_proj, a) + b_proj[None, :, None]
        return (xf + h).reshape(B, C, Hs, Ws)

    def _L1_attn_ref(x, W_qkv, b_qkv, W_out, b_out):
        import jax, jax.numpy as jnp
        import numpy as np
        B, T, D, H = (4, 8192, 512, 8)
        HD = D // H
        b, t, d = x.shape
        qkv = x @ W_qkv.T + b_qkv
        q, k, v = jnp.split(qkv, 3, axis=-1)

        def to_heads(u):
            return u.reshape(b, t, H, HD).transpose(0, 2, 1, 3)
        q, k, v = (to_heads(q), to_heads(k), to_heads(v))
        k = jax.nn.softmax(k, axis=-2)
        context = jnp.einsum('bhtd,bhtv->bhdv', k, v)
        out = jnp.einsum('bhtd,bhdv->bhtv', q, context)
        out = out.transpose(0, 2, 1, 3).reshape(b, t, d)
        return out @ W_out.T + b_out

    def _L1_ffn_ref(x, qidx, scales, W):
        import jax, jax.numpy as jnp
        import numpy as np
        BLOCK = 64
        NF4_TABLE = jnp.array([-1.0, -0.6961928009986877, -0.5250730514526367, -0.39491748809814453, -0.28444138169288635, -0.18477343022823334, -0.09105003625154495, 0.0, 0.07958029955625534, 0.16093020141124725, 0.24611230194568634, 0.33791524171829224, 0.44070982933044434, 0.5626170039176941, 0.7229568362236023, 1.0], dtype=jnp.float32)

        def _dequant_nf4(qidx, scales):
            w = NF4_TABLE[qidx].reshape(-1, BLOCK) * scales[:, None]
            return w.reshape(qidx.shape)
        w_lora = _dequant_nf4(qidx, scales)
        y = jnp.einsum('bsd,od->bso', x, w_lora)
        out = jnp.einsum('bsd,od->bso', y, W)
        return out

    def _gn(v, G=32, eps=1e-5):
        B_, C_, H_, W_ = v.shape
        g = v.reshape(B_, G, C_ // G, H_, W_)
        m = jnp.mean(g, axis=(2, 3, 4), keepdims=True)
        s = jnp.var(g, axis=(2, 3, 4), keepdims=True)
        return ((g - m) / jnp.sqrt(s + eps)).reshape(v.shape)

    def _ln_c(v, eps=1e-6):
        m = jnp.mean(v, axis=1, keepdims=True)
        s = jnp.var(v, axis=1, keepdims=True)
        return (v - m) / jnp.sqrt(s + eps)

    def _ln_t(v, eps=1e-5):
        m = jnp.mean(v, axis=-1, keepdims=True)
        s = jnp.var(v, axis=-1, keepdims=True)
        return (v - m) / jnp.sqrt(s + eps)

    def _to_tokens(v):
        B_, C_, H_, W_ = v.shape
        return v.reshape(B_, C_, H_ * W_).transpose(0, 2, 1)
    def _from_tokens(t, like):
        B_, C_, H_, W_ = like.shape
        return t.transpose(0, 2, 1).reshape(B_, C_, H_, W_)

    x = _L0_conv_ref(x, L0_conv_gn_w, L0_conv_gn_b, L0_conv_w_qkv, L0_conv_b_qkv, L0_conv_w_proj, L0_conv_b_proj)
    t = _to_tokens(x)
    t = t + _L1_attn_ref(_ln_t(t), L1_attn_W_qkv, L1_attn_b_qkv, L1_attn_W_out, L1_attn_b_out)
    t = t + _L1_ffn_ref(_ln_t(t), L1_ffn_qidx, L1_ffn_scales, L1_ffn_W)
    x = _from_tokens(t, x)
    return x


_drawn_inputs = setup_inputs


def setup_inputs(seed=0):
    import zlib

    import numpy as np

    out = dict(_drawn_inputs(seed))
    spreads = {'L0_conv_gn_w': (1.0, 0.2),
     'L0_conv_gn_b': (0.0, 0.1),
     'L1_attn_b_qkv': (0.0, 0.1),
     'L1_attn_b_out': (0.0, 0.1)}
    factors = {}
    for name, (base, spread) in spreads.items():
        noise = np.random.default_rng([zlib.crc32(name.encode()), seed]).standard_normal(out[name].shape)
        drawn = base * np.exp(spread * noise) if base else spread * noise
        out[name] = jnp.asarray(drawn.astype(out[name].dtype))
    for name, factor in factors.items():
        out[name] = (out[name] * factor).astype(out[name].dtype)
    return out
```

```python
from contextlib import ExitStack

import concourse.bass as bass
from concourse import mybir

F32 = mybir.dt.float32
F32R = mybir.dt.float32r
I32 = mybir.dt.int32
ALU = mybir.AluOpType
ACT = mybir.ActivationFunctionType
AX_X = mybir.AxisListType.X

P = 128
B, C, L = 8, 512, 1024
CH = C // P
HEADS = 8
HD = C // HEADS
PAIRS = HEADS // 2
HALF = 512
SC = L // P
UNITS = PAIRS * SC
GROUPS = 32
GN_EPS = 1e-5
LN_EPS = 1e-5
HI, LO = 0, 1
SPLITS = ((HI, HI), (HI, LO), (LO, HI))
NF4 = (-1.0, -0.6961928009986877, -0.5250730514526367, -0.39491748809814453, -0.28444138169288635,
       -0.18477343022833334, -0.09105003625154495, 0.0, 0.07958029955625534, 0.16093020141124725,
       0.24611230194568634, 0.33791524171829224, 0.44070982933044434, 0.5626170039176941,
       0.7229568362236023, 1.0)

QK_ORDER = [("Q", 0, 0), ("K", 0, 0), ("Q", 0, 1), ("K", 0, 1), ("K", 1, 0), ("Q", 1, 0), ("Q", 1, 1), ("K", 1, 1),
            ("Q", 2, 0), ("K", 2, 0), ("Q", 2, 1), ("K", 2, 1), ("Q", 3, 0), ("K", 3, 0), ("Q", 3, 1), ("K", 3, 1)]


def QK(kind, pair, half, rel=0):
    return ("QK", rel, QK_ORDER.index((kind, pair, half)))


def V(s, rel=0):
    return ("V", rel, s)


def H(j):
    return ("H", -1, j)


WHOLE = (0, 1)
FILL = {
    0: [(QK("K", 0, 1), WHOLE), (V(3), WHOLE)],
    1: [(V(4), WHOLE), (V(5), WHOLE)],
    2: [(V(6), WHOLE), (H(0), WHOLE)],
    3: [(V(7), WHOLE), (H(1), WHOLE)],
    4: [(QK("K", 1, 0), WHOLE), (H(2), WHOLE)],
    5: [(QK("Q", 1, 0), WHOLE), (H(3), WHOLE)],
    6: [(QK("Q", 1, 1), WHOLE), (H(4), WHOLE), (H(5), WHOLE)],
    7: [(H(6), WHOLE), (H(7), WHOLE)],
    8 * 3: [(QK("K", 3, 1), WHOLE)],
    8 * 3 + 4: [(QK("Q", 0, 0, 1), WHOLE)],
    8 * 3 + 5: [(QK("K", 0, 0, 1), WHOLE)],
    8 * 3 + 6: [(QK("Q", 0, 1, 1), WHOLE), (V(0, 1), WHOLE)],
    8 * 3 + 7: [(V(1, 1), WHOLE), (V(2, 1), WHOLE)],
}
for _p in (1, 2):
    FILL[8 * _p] = [(QK("K", _p, 1), (0,))]
    FILL[8 * _p + 1] = [(QK("K", _p, 1), (1,))]
    FILL[8 * _p + 2] = [(QK("Q", _p + 1, 0), (0,))]
    FILL[8 * _p + 3] = [(QK("Q", _p + 1, 0), (1,))]
    FILL[8 * _p + 4] = [(QK("K", _p + 1, 0), WHOLE)]
    FILL[8 * _p + 5] = [(QK("Q", _p + 1, 1), (0,))]
    FILL[8 * _p + 6] = [(QK("Q", _p + 1, 1), (1,))]
G1, G2 = ("G", 1, 0), ("G", 1, 1)
FILL[8 * 2 + 2].append((G1, WHOLE))
FILL[8 * 2 + 4].append((G2, WHOLE))
TILES = [t for k in range(UNITS) for t, parts in FILL.get(k, []) if 1 in parts]
NEXT_QKV = [t for k in range(24, UNITS) for t, _ in FILL.get(k, []) if t[1] == 1]
GN_STATS = {9: 0, 11: 1, 13: 2, 15: 3}
GN_AGGREGATE, GN_POWER, GN_AFFINE = 16, 21, 22
GN_SCALE = {24: (0, 1), 26: (2, 3)}
GN_LO = {25: (0, 1), 27: (2, 3)}


def exists(tile, b):
    if not isinstance(b, int):
        return True
    return {-1: tile[1] == 1, 0: tile[1] != -1, B - 1: tile[1] != 1, B: tile[1] == -1}.get(b, True)


def bank_of(tile):
    return TILES.index(tile) % 2


def bank_user_before(tile, b):
    n = TILES.index(tile)
    for m in range(n - 2, n - 2 * len(TILES), -2):
        prev, prev_b = TILES[m % len(TILES)], b + m // len(TILES)
        if isinstance(prev_b, int) and prev_b < -1:
            return None
        if exists(prev, prev_b):
            return prev, prev_b + prev[1]
    return None


assert len(TILES) % 2 == 0


def layer0(nc, sem, x, w_qk_t, w_v_t, w_proj_t, b_v, vectors, group_mean, t_dram):
    ctx = ExitStack()

    def sb(name, shape, dt=F32):
        return ctx.enter_context(nc.sbuf_tensor(name, shape, dt))

    with ctx:
        wqk = sb("wqk", [P, 2, CH, 2 * C], F32R)
        wv = sb("wv", [P, 2, CH, C], F32R)
        wp = sb("wp", [P, 2, CH, C], F32R)
        x_ring = sb("x_ring", [P, 2, L])
        xn = sb("xn", [P, 2, CH, L], F32R)
        qq = sb("qq", [P, 2, 2, L], F32R)
        kk = sb("kk", [P, 2, 2, L], F32R)
        v_sb = sb("v_sb", [P, SC, C])
        vs = sb("vs", [P, 2, 2 * HD])
        probs = sb("probs", [P, 2, 2, L])
        a_sb = sb("a_sb", [P, 2, CH, L], F32R)
        bv_rows = sb("bv_rows", [P, C])
        bias = sb("bias", [P, 5, CH])
        BQ, BK, BP, GW, GB = range(5)
        bq_scaled = sb("bq_scaled", [P, CH])
        gmat = sb("gmat", [P, P])
        neg_half = sb("neg_half", [P, CH])
        neg_max = sb("neg_max", [P, 2, 2])
        row_sum = sb("row_sum", [P, 2, 2])
        inv_sum = sb("inv_sum", [P, 2, 2])
        st = sb("st", [P, CH, 2, 6])
        mv = sb("mv", [P, CH, 2])
        g_mean = sb("g_mean", [P, CH])
        dev = sb("dev", [P, CH])
        dev2 = sb("dev2", [P, CH])
        spread = sb("spread", [P, CH])
        var_eps = sb("var_eps", [P, CH])
        rstd = sb("rstd", [P, CH])
        g_scale = sb("g_scale", [P, CH])
        g_tmp = sb("g_tmp", [P, CH])
        g_shift = sb("g_shift", [P, CH])
        stage = probs[:, :, :, :].rearrange("p a b l -> p (a b l)")

        s_ps = [ctx.enter_context(nc.psum_tensor(f"scores{h}", [P, L], F32)) for h in range(2)]
        pv_ps = ctx.enter_context(nc.psum_tensor("pv_ps", [P, L], F32))
        fill_ps = [ctx.enter_context(nc.psum_tensor(f"fill{i}", [P, HALF], F32)) for i in range(2)]

        const_loaded, weights_loaded, weights_split = sem("const_loaded"), sem("weights_loaded"), sem("weights_split")
        weights_hi = sem("weights_hi")
        const_made = sem("const_made")
        stats_loaded = [sem(f"stats_loaded{i}") for i in range(2)]
        norm_loaded = [sem(f"norm_loaded{i}") for i in range(2)]
        res_loaded = [sem(f"res_loaded{i}") for i in range(2)]
        stats_done, gn_aggregated, gn_chain = sem("stats_done"), sem("gn_aggregated"), sem("gn_chain")
        gn_power_in, gn_power_out, gn_affine = sem("gn_power_in"), sem("gn_power_out"), sem("gn_affine")
        x_scaled, xn_hi_done, xn_done = sem("x_scaled"), sem("xn_hi_done"), sem("xn_done")
        ready = {k: sem(f"{k}_tile_ready") for k in ("QK", "V", "H", "G")}
        evacuated = {k: sem(f"{k}_tile_evacuated") for k in ("QK", "V", "H", "G")}
        qk_hi_done = sem("qk_hi_done")
        k_copied = [sem(f"k_copied{h}") for h in range(2)]
        scores_ready = [sem(f"scores_ready{h}") for h in range(2)]
        max_ready = [sem(f"max_ready{h}") for h in range(2)]
        exp_done = [sem(f"exp_done{h}") for h in range(2)]
        inv_ready, vs_ready, pv_done = sem("inv_ready"), sem("vs_ready"), sem("pv_done")
        a_hi_done, a_done = sem("a_hi_done"), sem("a_done")
        t_stored = [sem(f"t_stored{i}") for i in range(2)]

        per_batch = {"QK": 16, "V": 8, "H": 8, "G": 2}

        def count(tile, b):
            return per_batch[tile[0]] * b + tile[2] + 1

        def wait(eng, s, value):
            if not isinstance(value, int) or value > 0:
                eng.wait_ge(s, value)

        def body_loop(eng, body):
            body(0)
            with eng.Fori(1, B - 1) as b:
                body(b)
            body(B - 1)

        block = ctx.enter_context(nc.Block())

        @block.sync
        def _(sp):
            def load_stats(b, i):
                if i >= 2:
                    sp.wait_ge(stats_done, CH * b + i - 1)
                elif isinstance(b, int) and b == 1:
                    sp.wait_ge(xn_done, i + 3)
                elif not isinstance(b, int) or b > 1:
                    sp.wait_ge(t_stored[i], 32 * (b - 1))
                sp.dma_start(x_ring[:, i % 2, :], x[b, i * P:(i + 1) * P, :]).then_inc(stats_loaded[i % 2], 16)

            def load_norm(b, i):
                if i >= 2:
                    sp.wait_ge(xn_done, CH * b + i - 1)
                else:
                    sp.wait_ge(stats_done, CH * b + i + 3)
                sp.dma_start(x_ring[:, i % 2, :], x[b, i * P:(i + 1) * P, :]).then_inc(norm_loaded[i % 2], 16)

            def load_residual(b, i):
                if i >= 2:
                    sp.wait_ge(t_stored[i % 2], 32 * b + 16)
                else:
                    sp.wait_ge(xn_done, CH * (b + 1) + i + 3)
                sp.dma_start(x_ring[:, i % 2, :], x[b, i * P:(i + 1) * P, :]).then_inc(res_loaded[i % 2], 16)

            def store_t(b, o):
                sp.wait_ge(evacuated["H"], 8 * b + 2 * o + 2)
                sp.dma_start(t_dram[b, o * P:(o + 1) * P, :], x_ring[:, o % 2, :]).then_inc(t_stored[o % 2], 16)

            def copy_k(b, pair, half):
                sp.wait_ge(evacuated["QK"], count(QK("K", pair, half), b))
                cols = slice(half * HALF, (half + 1) * HALF)
                sp.dma_start(kk[64:128, 0, :, cols].bitcast(F32), kk[0:64, 0, :, cols].bitcast(F32)).then_inc(k_copied[half], 16)
                sp.dma_start(kk[0:64, 1, :, cols].bitcast(F32), kk[64:128, 1, :, cols].bitcast(F32)).then_inc(k_copied[half], 16)

            sp.dma_start(stage[:, :].rearrange("p (c n) -> p c n", c=CH),
                         w_qk_t.rearrange("(c p) n -> p c n", p=P)).then_inc(weights_loaded, 16)
            sp.dma_start(gmat[:, :], group_mean).then_inc(const_loaded, 16)
            sp.dma_start(bv_rows[:, :], b_v.partition_broadcast(P)).then_inc(const_loaded, 16)
            sp.dma_start(bias[:, :, :], vectors).then_inc(const_loaded, 16)
            for i in range(CH):
                load_stats(0, i)
            sp.wait_ge(weights_split, 2)
            sp.dma_start(stage[:, 0:CH * C].rearrange("p (c n) -> p c n", c=CH),
                         w_v_t.rearrange("(c p) n -> p c n", p=P)).then_inc(weights_loaded, 16)
            sp.dma_start(stage[:, CH * C:].rearrange("p (c n) -> p c n", c=CH),
                         w_proj_t.rearrange("(c p) n -> p c n", p=P)).then_inc(weights_loaded, 16)
            for i in range(CH):
                load_norm(0, i)
            copy_k(0, 0, 0)

            def body(b):
                first, last = isinstance(b, int) and b == 0, isinstance(b, int) and b == B - 1
                copy_k(b, 0, 1)
                if not first:
                    load_residual(b - 1, 0)
                    load_residual(b - 1, 1)
                    store_t(b - 1, 0)
                copy_k(b, 1, 0)
                if not first:
                    load_residual(b - 1, 2)
                    store_t(b - 1, 1)
                    load_residual(b - 1, 3)
                    store_t(b - 1, 2)
                    store_t(b - 1, 3)
                if not last:
                    load_stats(b + 1, 0)
                    load_stats(b + 1, 1)
                copy_k(b, 1, 1)
                if not last:
                    load_stats(b + 1, 2)
                    load_stats(b + 1, 3)
                copy_k(b, 2, 0)
                copy_k(b, 2, 1)
                if not last:
                    load_norm(b + 1, 0)
                    load_norm(b + 1, 1)
                copy_k(b, 3, 0)
                copy_k(b, 3, 1)
                if not last:
                    load_norm(b + 1, 2)
                    load_norm(b + 1, 3)
                    copy_k(b + 1, 0, 0)

            body_loop(sp, body)
            for o in range(CH):
                if o >= 2:
                    sp.wait_ge(t_stored[o % 2], 32 * (B - 1) + 16)
                else:
                    sp.wait_ge(t_stored[o % 2], 32 * (B - 1))
                sp.dma_start(x_ring[:, o % 2, :], x[B - 1, o * P:(o + 1) * P, :]).then_inc(res_loaded[o % 2], 16)
                if o >= 1:
                    store_t(B - 1, o - 1)
            store_t(B - 1, CH - 1)
            for i in range(2):
                sp.wait_ge(t_stored[i], 32 * B)

        @block.tensor
        def _(pe):
            def split_product(out, stationary, moving, parts, n=CH):
                steps = [(c, a, m) for c in range(n) for a, m in SPLITS]
                cut = len(steps) // 2
                for part in parts:
                    for k in range(part * cut, (part + 1) * cut):
                        c, a, m = steps[k]
                        mm = pe.matmul(out, stationary(a, c), moving(m, c), start=(k == 0), stop=(k == len(steps) - 1))
                return mm

            def tile(t, b, parts):
                kind, rel, n = t
                out = fill_ps[bank_of(t)]
                if 0 in parts:
                    before = bank_user_before(t, b)
                    if before:
                        wait(pe, evacuated[before[0][0]], count(*before))
                    if kind in ("QK", "V") and rel == 1:
                        pe.wait_ge(xn_done, CH * (b + 2))
                    if kind == "H" and n == 0:
                        pe.wait_ge(a_done, PAIRS * b)
                if kind == "QK":
                    which, pair, half = QK_ORDER[n]
                    col = (pair if which == "Q" else PAIRS + pair) * P
                    mm = split_product(out[:, :], lambda a, c: wqk[:, a, c, col:col + P],
                                       lambda m, c: xn[:, m, c, half * HALF:(half + 1) * HALF], parts)
                elif kind == "V":
                    mm = split_product(out[:, :], lambda a, c: xn[:, a, c, n * P:(n + 1) * P],
                                       lambda m, c: wv[:, m, c, :], parts)
                elif kind == "H":
                    o, half = n // 2, n % 2
                    mm = split_product(out[:, :], lambda a, c: wp[:, a, c, o * P:(o + 1) * P],
                                       lambda m, c: a_sb[:, m, c, half * HALF:(half + 1) * HALF], parts)
                else:
                    pe.wait_ge(gn_aggregated, 2 * (b + 1) + n + 1)
                    mm = pe.matmul(out[:, 0:CH], gmat[:, :], mv[:, :, 0] if n == 0 else spread[:, :],
                                   start=True, stop=True)
                if 1 in parts:
                    mm.then_inc(ready[kind], 1)

            def scores(b, k):
                pair, s = k // SC, k % SC
                g = UNITS * b + k
                if s == 0:
                    pe.wait_ge(evacuated["QK"], count(QK("Q", pair, 1), b))
                if s % 4 == 0:
                    pe.wait_ge(k_copied[s // 4], 32 * (PAIRS * b + pair + 1))
                for h in range(2):
                    wait(pe, exp_done[h], g)
                    for half in range(2):
                        for part in (HI, LO):
                            mm = pe.matmul(s_ps[h][:, half * HALF:(half + 1) * HALF],
                                           kk[:, h, part, s * P:(s + 1) * P],
                                           qq[:, pair % 2, h, half * HALF:(half + 1) * HALF],
                                           start=(part == HI), stop=(part == LO))
                    mm.then_inc(scores_ready[h], 1)

            def values(b, k):
                s = k % SC
                pe.wait_ge(vs_ready, UNITS * b + k + 1)
                if s == 0:
                    wait(pe, a_done, PAIRS * b + k // SC)
                for half in range(2):
                    for h in range(2):
                        mm = pe.matmul(pv_ps[64 * h:64 * h + 64, half * HALF:(half + 1) * HALF],
                                       vs[:, k % 2, h * HD:(h + 1) * HD],
                                       probs[:, k % 2, h, half * HALF:(half + 1) * HALF],
                                       start=(s == 0), stop=(s == SC - 1))
                mm.then_inc(pv_done, 1)

            pe.wait_ge(const_loaded, 16 * 3)
            tile(G1, -1, WHOLE)
            tile(G2, -1, WHOLE)
            pe.wait_ge(weights_split, 4)
            for t in NEXT_QKV:
                tile(t, -1, WHOLE)

            def body(b):
                for k in range(UNITS):
                    scores(b, k)
                    if k > 0:
                        values(b, k - 1)
                    elif not isinstance(b, int) or b > 0:
                        values(b - 1, UNITS - 1)
                    for t, parts in FILL.get(k, []):
                        if exists(t, b):
                            tile(t, b, parts)

            body_loop(pe, body)
            values(B - 1, UNITS - 1)
            for j in range(8):
                tile(H(j), B, WHOLE)

        @block.scalar
        def _(act):
            def evacuate(t, b):
                kind, rel, n = t
                bb = b + rel
                if kind != "QK":
                    return
                which, pair, half = QK_ORDER[n]
                act.wait_ge(ready["QK"], count(t, bb))
                cols = slice(half * HALF, (half + 1) * HALF)
                ps = fill_ps[bank_of(t)]
                if which == "K":
                    wait(act, scores_ready[1], UNITS * bb + SC * (pair - 1) + 4 * (half + 1))
                    dst = [kk[64 * h:64 * h + 64, h, HI, cols] for h in range(2)]
                    add = [bias[64 * h:64 * h + 64, BK, pair:pair + 1] for h in range(2)]
                else:
                    wait(act, scores_ready[1], UNITS * bb + SC * (pair - 1))
                    dst = [qq[64 * h:64 * h + 64, pair % 2, h, cols] for h in range(2)]
                    add = [bq_scaled[64 * h:64 * h + 64, pair:pair + 1] for h in range(2)]
                for h in range(2):
                    ins = nc.scalar.activation(dst[h], ps[64 * h:64 * h + 64, :], ACT.Identity, bias=add[h])
                ins.then_inc(qk_hi_done, 1)

            def exponentials(b, k):
                g = UNITS * b + k
                for h in range(2):
                    act.wait_ge(max_ready[h], g + 1)
                    wait(act, pv_done, g - 1 if not isinstance(g, int) or g > 1 else 0)
                    nc.scalar.activation(probs[:, k % 2, h, :], s_ps[h][:, :], ACT.Exp,
                                         bias=neg_max[:, k % 2, h:h + 1],
                                         accum_out=row_sum[:, k % 2, h:h + 1]).then_inc(exp_done[h], 1)

            def attention_hi(b, pair):
                act.wait_ge(pv_done, UNITS * b + SC * (pair + 1))
                wait(act, ready["H"], 8 * b)
                nc.scalar.activation(a_sb[:, HI, pair, :], pv_ps[:, :], ACT.Copy).then_inc(a_hi_done, 1)

            def normalised_hi(b, i):
                act.wait_ge(x_scaled, CH * b + i + 1)
                wait(act, ready["QK"], 16 * b)
                nc.scalar.activation(xn[:, HI, i, :], x_ring[:, i % 2, :], ACT.Copy).then_inc(xn_hi_done, 1)

            act.wait_ge(weights_loaded, 16)
            raw = stage[:, :].rearrange("p (c n) -> p c n", c=CH)
            nc.scalar.activation(wqk[:, HI, :, 0:C], raw[:, :, 0:C], ACT.Copy, scale=0.125).then_inc(weights_hi, 1)
            nc.scalar.activation(wqk[:, HI, :, C:], raw[:, :, C:], ACT.Copy).then_inc(weights_hi, 1)
            act.wait_ge(weights_loaded, 48)
            nc.scalar.activation(wv[:, HI, :, :].rearrange("p c n -> p (c n)"), stage[:, 0:CH * C],
                                 ACT.Copy).then_inc(weights_hi, 1)
            nc.scalar.activation(wp[:, HI, :, :].rearrange("p c n -> p (c n)"), stage[:, CH * C:],
                                 ACT.Copy).then_inc(weights_hi, 1)
            act.wait_ge(const_made, 2)
            for i in range(CH):
                normalised_hi(0, i)
            for t in NEXT_QKV:
                evacuate(t, -1)

            def body(b):
                last = isinstance(b, int) and b == B - 1
                for k in range(UNITS):
                    exponentials(b, k)
                    if k % SC == 0 and k > 0:
                        attention_hi(b, k // SC - 1)
                    elif k == 0 and (not isinstance(b, int) or b > 0):
                        attention_hi(b - 1, PAIRS - 1)
                    for t, parts in FILL.get(k, []):
                        if 1 in parts and exists(t, b):
                            evacuate(t, b)
                    if not last:
                        for i in GN_SCALE.get(k, ()):
                            normalised_hi(b + 1, i)

            body_loop(act, body)
            attention_hi(B - 1, PAIRS - 1)

        @block.vector
        def _(dve):
            def evacuate(t, b):
                kind, rel, n = t
                bb = b + rel
                ps = fill_ps[bank_of(t)]
                if kind == "QK":
                    which, pair, half = QK_ORDER[n]
                    dve.wait_ge(qk_hi_done, count(t, bb))
                    cols = slice(half * HALF, (half + 1) * HALF)
                    for h in range(2):
                        rows, other = slice(64 * h, 64 * h + 64), slice(64 - 64 * h, 128 - 64 * h)
                        if which == "K":
                            hi, dst, add = kk[rows, h, HI, cols], kk[rows, h, LO, cols], bias[rows, BK, pair:pair + 1]
                        else:
                            hi, dst = qq[rows, pair % 2, h, cols], qq[other, pair % 2, h, cols]
                            add = bq_scaled[rows, pair:pair + 1]
                        ins = nc.vector.scalar_tensor_tensor(out=dst, in0=ps[rows, :], scalar=add, in1=hi.bitcast(F32),
                                                             op0=ALU.add, op1=ALU.subtract)
                    ins.then_inc(evacuated["QK"], 1)
                elif kind == "V":
                    dve.wait_ge(ready["V"], count(t, bb))
                    wait(dve, vs_ready, UNITS * bb - SC + n + 1 if not isinstance(bb, int) or bb > 0 else 0)
                    nc.vector.tensor_tensor(v_sb[:, n, :], ps[:, :], bv_rows[:, :], ALU.add)\
                        .then_inc(evacuated["V"], 1)
                elif kind == "H":
                    o, half = n // 2, n % 2
                    dve.wait_ge(ready["H"], count(t, bb))
                    dve.wait_ge(res_loaded[o % 2], 32 * bb + 16 * (o // 2 + 1))
                    slot = x_ring[:, o % 2, half * HALF:(half + 1) * HALF]
                    nc.vector.scalar_tensor_tensor(out=slot, in0=ps[:, :], scalar=bias[:, BP, o:o + 1], in1=slot,
                                                   op0=ALU.add, op1=ALU.add).then_inc(evacuated["H"], 1)
                elif n == 0:
                    group_spread(bb)
                else:
                    dve.wait_ge(ready["G"], count(t, bb))
                    nc.vector.tensor_scalar(var_eps[:, :], ps[:, 0:CH], GN_EPS, None, ALU.add)\
                        .then_inc(evacuated["G"], 1)

            def statistics(b, i):
                dve.wait_ge(stats_loaded[i % 2], 32 * b + 16 * (i // 2 + 1))
                for half in range(2):
                    ins = nc.vector.bn_stats(st[:, i, half, :], x_ring[:, i % 2, half * HALF:(half + 1) * HALF])
                ins.then_inc(stats_done, 1)

            def aggregate(b):
                dve.wait_ge(stats_done, CH * (b + 1))
                nc.vector.memset(g_tmp[:, :], 0.0)
                for i in range(CH):
                    ins = nc.vector.bn_aggr(mv[:, i, :], st[:, i, :, :])
                ins.then_inc(gn_aggregated, 1)

            def group_spread(b):
                dve.wait_ge(ready["G"], count(G1, b))
                nc.vector.tensor_copy(g_mean[:, :], fill_ps[bank_of(G1)][:, 0:CH]).then_inc(evacuated["G"], 1)
                dve.wait_ge(evacuated["G"], count(G1, b))
                nc.vector.tensor_tensor(dev[:, :], mv[:, :, 0], g_mean[:, :], ALU.subtract).then_inc(gn_chain, 1)
                dve.wait_ge(gn_chain, 2 * b + 1)
                nc.vector.tensor_tensor(dev2[:, :], dev[:, :], dev[:, :], ALU.mult).then_inc(gn_chain, 1)
                dve.wait_ge(gn_chain, 2 * b + 2)
                nc.vector.tensor_tensor(spread[:, :], dev2[:, :], mv[:, :, 1], ALU.add).then_inc(gn_aggregated, 1)

            def affine(b):
                dve.wait_ge(gn_power_out, b + 1)
                nc.vector.tensor_tensor(g_scale[:, :], rstd[:, :], bias[:, GW, :], ALU.mult).then_inc(gn_affine, 1)
                dve.wait_ge(gn_affine, 3 * b + 1)
                nc.vector.tensor_tensor(g_tmp[:, :], g_mean[:, :], g_scale[:, :], ALU.mult).then_inc(gn_affine, 1)
                dve.wait_ge(gn_affine, 3 * b + 2)
                nc.vector.tensor_tensor(g_shift[:, :], bias[:, GB, :], g_tmp[:, :], ALU.subtract).then_inc(gn_affine, 1)

            def scale_x(b, i):
                dve.wait_ge(norm_loaded[i % 2], 32 * b + 16 * (i // 2 + 1))
                if i == 0:
                    dve.wait_ge(gn_affine, 3 * (b + 1))
                slot = x_ring[:, i % 2, :]
                nc.vector.tensor_scalar(slot, slot, g_scale[:, i:i + 1], g_shift[:, i:i + 1], ALU.mult, ALU.add)\
                    .then_inc(x_scaled, 1)

            def normalised_lo(b, i):
                dve.wait_ge(xn_hi_done, CH * b + i + 1)
                nc.vector.tensor_tensor(xn[:, LO, i, :], x_ring[:, i % 2, :], xn[:, HI, i, :].bitcast(F32),
                                        ALU.subtract).then_inc(xn_done, 1)

            def attention_lo(b, pair):
                dve.wait_ge(a_hi_done, PAIRS * b + pair + 1)
                nc.vector.tensor_tensor(a_sb[:, LO, pair, :], pv_ps[:, :], a_sb[:, HI, pair, :].bitcast(F32),
                                        ALU.subtract).then_inc(a_done, 1)

            def maxima(b, k):
                g = UNITS * b + k
                for h in range(2):
                    dve.wait_ge(scores_ready[h], g + 1)
                    nc.vector.tensor_reduce(neg_max[:, k % 2, h:h + 1], s_ps[h][:, :], AX_X, ALU.max,
                                            negate=True).then_inc(max_ready[h], 1)
                for h in range(2):
                    dve.wait_ge(exp_done[h], g + 1)
                wait(dve, vs_ready, g - 1 if not isinstance(g, int) or g > 1 else 0)
                nc.vector.reciprocal(inv_sum[:, k % 2, :], row_sum[:, k % 2, :]).then_inc(inv_ready, 1)

            nc.vector.memset(neg_half[:, :], -0.5).then_inc(const_made, 1)
            dve.wait_ge(const_loaded, 16 * 3)
            nc.vector.tensor_scalar(bq_scaled[:, :], bias[:, BQ, :], 0.125, None, ALU.mult).then_inc(const_made, 1)
            for i in range(CH):
                statistics(0, i)
            aggregate(0)
            evacuate(G1, -1)
            evacuate(G2, -1)
            raw = stage[:, :].rearrange("p (c n) -> p c n", c=CH)
            dve.wait_ge(weights_hi, 1)
            nc.vector.scalar_tensor_tensor(out=wqk[:, LO, :, 0:C], in0=raw[:, :, 0:C], scalar=0.125,
                                           in1=wqk[:, HI, :, 0:C].bitcast(F32), op0=ALU.mult, op1=ALU.subtract)\
                .then_inc(weights_split, 1)
            dve.wait_ge(weights_hi, 2)
            nc.vector.tensor_tensor(wqk[:, LO, :, C:], raw[:, :, C:], wqk[:, HI, :, C:].bitcast(F32), ALU.subtract)\
                .then_inc(weights_split, 1)
            affine(0)
            scale_x(0, 0)
            scale_x(0, 1)
            normalised_lo(0, 0)
            normalised_lo(0, 1)
            for n, w in ((0, wv), (1, wp)):
                dve.wait_ge(weights_hi, 3 + n)
                nc.vector.tensor_tensor(w[:, LO, :, :].rearrange("p c n -> p (c n)"),
                                        stage[:, n * CH * C:(n + 1) * CH * C],
                                        w[:, HI, :, :].rearrange("p c n -> p (c n)").bitcast(F32), ALU.subtract)\
                    .then_inc(weights_split, 1)
            scale_x(0, 2)
            scale_x(0, 3)
            normalised_lo(0, 2)
            normalised_lo(0, 3)
            for t in NEXT_QKV:
                evacuate(t, -1)

            def body(b):
                last = isinstance(b, int) and b == B - 1
                for k in range(UNITS):
                    maxima(b, k)
                    if k % SC == 0 and k > 0:
                        attention_lo(b, k // SC - 1)
                    elif k == 0 and (not isinstance(b, int) or b > 0):
                        attention_lo(b - 1, PAIRS - 1)
                    for t, parts in FILL.get(k, []):
                        if 1 in parts and exists(t, b):
                            evacuate(t, b)
                    if not last:
                        if k in GN_STATS:
                            statistics(b + 1, GN_STATS[k])
                        if k == GN_AGGREGATE:
                            aggregate(b + 1)
                        if k == GN_AFFINE:
                            affine(b + 1)
                        for i in GN_SCALE.get(k, ()):
                            scale_x(b + 1, i)
                        for i in GN_LO.get(k, ()):
                            normalised_lo(b + 1, i)

            body_loop(dve, body)
            attention_lo(B - 1, PAIRS - 1)
            for j in range(8):
                evacuate(H(j), B)

        @block.gpsimd
        def _(pool):
            def power(b):
                pool.wait_ge(evacuated["G"], 2 * (b + 1))
                nc.gpsimd.tensor_tensor(rstd[:, :], var_eps[:, :], neg_half[:, :], ALU.pow).then_inc(gn_power_out, 1)

            pool.wait_ge(const_made, 1)
            power(0)

            def body(b):
                last = isinstance(b, int) and b == B - 1
                for k in range(UNITS):
                    g = UNITS * b + k
                    pair, s = k // SC, k % SC
                    pool.wait_ge(inv_ready, g + 1)
                    if pair == 0:
                        pool.wait_ge(evacuated["V"], 8 * b + s + 1)
                    wait(pool, pv_done, g - 1 if not isinstance(g, int) or g > 1 else 0)
                    nc.gpsimd.tensor_tensor(
                        vs[:, k % 2, :].rearrange("p (h d) -> p h d", h=2),
                        v_sb[:, s, pair * P:(pair + 1) * P].rearrange("p (h d) -> p h d", h=2),
                        inv_sum[:, k % 2, :].unsqueeze(2).to_broadcast([P, 2, HD]), ALU.mult).then_inc(vs_ready, 1)
                    if k == GN_POWER and not last:
                        power(b + 1)

            body_loop(pool, body)


FFN0, FFN1, NEXT0, NEXT1 = range(4)
STEPS = (
    [("K", 0, 0), ("K", 1, 0), ("MEAN", FFN0), ("K", 2, 0), ("K", 3, 0), ("K", 0, 1), ("K", 1, 1), ("E", 0), ("VAR", FFN0),
     ("K", 2, 1), ("E", 1), ("CAST", FFN0), ("K", 3, 1), ("E", 2), ("SPLIT", FFN0), ("V", 0), ("E", 3), ("T", 0), ("V", 1),
     ("MEAN", FFN1), ("T", 1), ("X", 0), ("Y", 0, 0), ("Y", 1, 0), ("VAR", FFN1), ("Y", 2, 0), ("Y", 3, 0), ("CAST", FFN1),
     ("N", 0), ("V", 2), ("T", 2), ("X", 1), ("SPLIT", FFN1), ("MEAN", NEXT0), ("V", 3), ("T", 3), ("X", 2),
     ("N", 1), ("V", 4), ("T", 4), ("X", 3), ("V", 5), ("T", 5), ("X", 4), ("VAR", NEXT0), ("N", 2), ("V", 6), ("T", 6), ("X", 5),
     ("CAST", NEXT0), ("V", 7), ("T", 7), ("X", 6), ("MEAN", NEXT1), ("N", 3), ("Y", 0, 1), ("X", 7), ("Y", 1, 1), ("Y", 2, 1),
     ("Y", 3, 1), ("VAR", NEXT1), ("WF", 0), ("WF", 1), ("WF", 2), ("WF", 3), ("G", 0), ("G", 1), ("G", 2), ("G", 3),
     ("CAST", NEXT1), ("OB",), ("A", 0), ("A", 1), ("A", 2), ("A", 3)]
    + [("O", o, 0) for o in range(CH)] + [("SPLIT", NEXT0)] + [("O", o, 1) for o in range(CH)] + [("SPLIT", NEXT1)])
SHARED = ("K", "V", "Y", "WF", "G", "OB", "A", "O")
TILES1 = [s for s in STEPS if s[0] in SHARED]
LATER = {"MEAN", "VAR", "CAST", "SPLIT"}


def step_exists(step, b):
    kind = step[0]
    if kind in ("N", "WF"):
        return isinstance(b, int) and b == 0
    if not isinstance(b, int):
        return True
    ffn = kind == "Y" or (kind in LATER and step[1] in (FFN0, FFN1))
    following = kind in LATER and not ffn
    return {-1: following, 0: not ffn, B - 1: not following, B: ffn}.get(b, True)


def bank1_user_before(step, b):
    n = TILES1.index(step)
    for m in range(n - 3, n - 3 * len(TILES1), -1):
        if (m % len(TILES1)) % 3 != n % 3:
            continue
        prev, prev_b = TILES1[m % len(TILES1)], b + m // len(TILES1)
        if isinstance(prev_b, int) and prev_b < 0:
            return None
        if step_exists(prev, prev_b):
            return prev, prev_b
    return None


def layer1(nc, sem, t_dram, w_kv_t, w_q, w_out_t, w_ffn_t, qidx, scales, b_v, vectors, consts, out):
    ctx = ExitStack()

    def sb(name, shape, dt=F32):
        return ctx.enter_context(nc.sbuf_tensor(name, shape, dt))

    with ctx:
        wkv = sb("wkv", [P, 2, CH, 2 * C], F32R)
        wq = sb("wq", [P, CH, C])
        wo = sb("wo", [P, CH, C])
        wf = sb("wf", [P, 2, CH, C], F32R)
        xc = sb("xc", [P, CH, L])
        t2 = sb("t2", [P, CH, L])
        tn1 = sb("tn1", [P, 2, CH, L], F32R)
        tn2 = sb("tn2", [P, 2, CH, HALF], F32R)
        ke = sb("ke", [P, CH, L])
        g_sb = ke[:, 0:2, :].rearrange("p a (b n) -> p (a b) n", b=2)
        kt_sb = sb("kt_sb", [P, 2, C])
        v_sb = sb("v1_sb", [P, 2, C])
        a_mat = sb("a_mat", [P, 2, CH, C], F32R)
        sq = sb("sq", [P, CH, HALF])
        resid = sb("resid", [P, 2, HALF])
        total = sb("total", [P, HALF])
        diag = sb("diag", [P, 4, P])
        ctx_sb = sb("ctx_sb", [P, PAIRS, P])
        bv_rows = sb("bv1_rows", [P, C])
        bias = sb("bias1", [P, 3, CH])
        BQ, BK, BO = range(3)
        cst = sb("cst", [P, 3, P])
        MEAN_OF, ONES, IDENT = range(3)
        sc = sb("sc", [P, CH, 8])
        neg_half = sb("neg_half1", [P, 4])
        var_eps = sb("var_eps1", [P, 4])
        rstd = sb("rstd1", [P, 4])
        k_neg_max = sb("k_neg_max", [P, CH])
        k_sum = sb("k_sum", [P, CH])
        k_inv = sb("k_inv", [P, CH])
        ob = sb("ob", [P, CH])

        tile_ps = [ctx.enter_context(nc.psum_tensor(f"tile{i}", [P, HALF], F32)) for i in range(3)]
        kt_ps = [ctx.enter_context(nc.psum_tensor(f"kt_ps{i}", [P, HALF], F32)) for i in range(2)]
        ctx_ps = ctx.enter_context(nc.psum_tensor("ctx_ps", [P, PAIRS, P], F32))
        cast_ps = ctx.enter_context(nc.psum_tensor("cast_ps", [P, HALF], F32))
        var_ps = ctx.enter_context(nc.psum_tensor("var_ps", [P, HALF], F32))

        names = SHARED + ("T", "X")
        ready = {k: sem(f"l1_{k}_ready") for k in names}
        evacuated = {k: sem(f"l1_{k}_evacuated") for k in names}
        per = {"K": 8, "V": 8, "Y": 8, "WF": 4, "G": 4, "OB": 1, "A": 4, "O": 8, "T": 8, "X": 8}
        const_loaded, kv_loaded, kv_hi, kv_split = sem("l1_const_loaded"), sem("kv_loaded"), sem("kv_hi"), sem("kv_split")
        const_made = sem("l1_const_made")
        q_loaded, wft_loaded, nf4_chain, dequantised = sem("q_loaded"), sem("wft_loaded"), sem("nf4_chain"), sem("dequantised")
        xc_loaded = [sem(f"xc_loaded{h}") for h in range(2)]
        resid_loaded = [sem(f"resid_loaded{h}") for h in range(2)]
        stored = [sem(f"out_stored{h}") for h in range(2)]
        pool_chain, total_ready = sem("pool_chain"), sem("total_ready")
        mean_ready, centred, squared, sq_total_ready = sem("mean_ready"), sem("centred"), sem("squared"), sem("sq_total_ready")
        var_ready, eps_added, rstd_ready = sem("var_ready"), sem("eps_added"), sem("rstd_ready")
        diag_ready, cast_ready, normalised = sem("diag_ready"), sem("cast_ready"), sem("normalised")
        hi_done = {n: sem(f"norm{n}_hi_done") for n in (1, 2)}
        lo_done = {n: sem(f"norm{n}_lo_done") for n in (1, 2)}
        a_hi_done = sem("l1_a_hi_done")
        k_max_ready, k_exp_done, k_inv_ready, ctx_done = sem("k_max_ready"), sem("k_exp_done"), sem("k_inv_ready"), sem("ctx_done")

        def number(step):
            kind = step[0]
            if kind in ("K", "Y", "O"):
                return CH * step[2] + step[1]
            return 0 if kind == "OB" else step[1]

        def count(step, b):
            return per[step[0]] * (b - 1 if step[0] == "Y" else b) + number(step) + 1

        def job_index(b, job):
            return 4 * b + job - {-1: -2, B: 2}.get(b, 0) if isinstance(b, int) else 4 * b + job

        def norm_of(b, job):
            return (2, b - 1, job) if job in (FFN0, FFN1) else (1, b + 1, job - 2)

        def halves(t, half):
            return t[:, :, half * HALF:(half + 1) * HALF]

        def wait(eng, s, value):
            if not isinstance(value, int) or value > 0:
                eng.wait_ge(s, value)

        def iterations(eng, step):
            def iteration(b):
                for s in STEPS:
                    if step_exists(s, b):
                        step(s, b)
            iteration(0)
            with eng.Fori(1, B - 1) as b:
                iteration(b)
            iteration(B - 1)
            iteration(B)

        block = ctx.enter_context(nc.Block())

        @block.sync
        def _(sp):
            def load_t(b, half):
                if not isinstance(b, int) or b > 1:
                    sp.wait_ge(lo_done[2], 2 * (b - 2) + half + 1)
                elif b == 1:
                    sp.wait_ge(lo_done[1], half + 1)
                sp.dma_start(halves(xc, half), t_dram[b].rearrange("(c p) l -> p c l", p=P)[:, :, half * HALF:(half + 1) * HALF])\
                    .then_inc(xc_loaded[half], 16)

            def step(s, b):
                kind = s[0]
                if kind == "SPLIT" and s[1] == FFN0 and not (isinstance(b, int) and b >= B - 1):
                    load_t(b + 1, 0)
                if kind == "SPLIT" and s[1] == FFN1 and not (isinstance(b, int) and b >= B - 1):
                    load_t(b + 1, 1)
                if kind == "O":
                    n = number(s)
                    wait(sp, evacuated["O"], 8 * b + n - 1)
                    if isinstance(b, int) and b == 0 and n == 0:
                        sp.wait_ge(dequantised, 4)
                    sp.dma_start(resid[:, n % 2, :], t_dram[b, s[1] * P:(s[1] + 1) * P, s[2] * HALF:(s[2] + 1) * HALF])\
                        .then_inc(resid_loaded[n % 2], 16)
                if kind == "Y" and s[1] == CH - 1:
                    sp.wait_ge(evacuated["Y"], count(s, b))
                    sp.dma_start(out[b - 1].rearrange("(c p) l -> p c l", p=P)[:, :, s[2] * HALF:(s[2] + 1) * HALF],
                                 halves(t2, s[2])).then_inc(stored[s[2]], 16)

            sp.dma_start(ke[:, :, :], w_kv_t.rearrange("(c p) n -> p c n", p=P)).then_inc(kv_loaded, 16)
            load_t(0, 0)
            sp.dma_start(cst[:, :, :], consts).then_inc(const_loaded, 16)
            sp.dma_start(bias[:, :, :], vectors).then_inc(const_loaded, 16)
            sp.dma_start(bv_rows[:, :], b_v.partition_broadcast(P)).then_inc(const_loaded, 16)
            load_t(0, 1)
            sp.dma_start(wq[:, :, :], w_q.rearrange("(c p) n -> p c n", p=P)).then_inc(const_loaded, 16)
            sp.dma_start(wo[:, :, :], w_out_t.rearrange("(c p) n -> p c n", p=P)).then_inc(const_loaded, 16)
            sp.dma_start(sc[:, :, :], scales.rearrange("(c p) n -> p c n", p=P)).then_inc(q_loaded, 16)
            sp.dma_start(t2[:, 0:2, :].rearrange("p a (b n) -> p (a b) n", b=2).bitcast(I32),
                         qidx.rearrange("(c p) n -> p c n", p=P)).then_inc(q_loaded, 16)
            load_t(1, 0)
            load_t(1, 1)
            sp.wait_ge(dequantised, 4)
            sp.dma_start(t2[:, 0:2, :].rearrange("p a (b n) -> p (a b) n", b=2),
                         w_ffn_t.rearrange("(c p) n -> p c n", p=P)).then_inc(wft_loaded, 16)
            iterations(sp, step)
            for h in range(2):
                sp.wait_ge(stored[h], 16 * B)

        w_raw = t2[:, 0:2, :].rearrange("p a (b n) -> p (a b) n", b=2)
        w_lora = t2[:, 2:4, :].rearrange("p a (b n) -> p (a b) n", b=2)

        @block.tensor
        def _(pe):
            def split_product(out_ap, stationary, moving):
                for c in range(CH):
                    for n, (a, m) in enumerate(SPLITS):
                        mm = pe.matmul(out_ap, stationary(a, c), moving(m, c), start=(c == 0 and n == 0),
                                       stop=(c == CH - 1 and n == len(SPLITS) - 1))
                return mm

            def shared_tile(s, b):
                kind = s[0]
                ps = tile_ps[TILES1.index(s) % 3]
                before = bank1_user_before(s, b)
                if before:
                    wait(pe, evacuated[before[0][0]], count(*before))
                if kind == "K":
                    d, half = s[1], s[2]
                    pe.wait_ge(lo_done[1], 2 * b + half + 1)
                    mm = split_product(ps[:, :], lambda a, c: wkv[:, a, c, d * P:(d + 1) * P],
                                       lambda m, c: tn1[:, m, c, half * HALF:(half + 1) * HALF])
                elif kind == "V":
                    mm = split_product(ps[:, :], lambda a, c: tn1[:, a, c, s[1] * P:(s[1] + 1) * P],
                                       lambda m, c: wkv[:, m, c, C:])
                elif kind == "Y":
                    pe.wait_ge(lo_done[2], 2 * (b - 1) + s[2] + 1)
                    mm = split_product(ps[:, :], lambda a, c: wf[:, a, c, s[1] * P:(s[1] + 1) * P],
                                       lambda m, c: tn2[:, m, c, :])
                elif kind == "WF":
                    pe.wait_ge(wft_loaded, 16)
                    for m in range(CH):
                        mm = pe.matmul(ps[:, :], w_lora[:, m, s[1] * P:(s[1] + 1) * P], w_raw[:, m, :],
                                       start=(m == 0), stop=(m == CH - 1))
                elif kind == "G":
                    pe.wait_ge(ctx_done, b + 1)
                    mm = pe.matmul(ps[:, :], ctx_sb[:, s[1], :], wo[:, s[1], :], start=True, stop=True)
                elif kind == "OB":
                    pe.wait_ge(evacuated["G"], 4 * b + 4)
                    for o in range(CH):
                        for d in range(CH):
                            mm = pe.matmul(ps[:, o:o + 1], g_sb[:, d, o * P:(o + 1) * P], bias[:, BQ, d:d + 1],
                                           start=(d == 0), stop=(d == CH - 1))
                elif kind == "A":
                    pe.wait_ge(evacuated["G"], 4 * b + 4)
                    for d in range(CH):
                        mm = pe.matmul(ps[:, :], wq[:, d, s[1] * P:(s[1] + 1) * P], g_sb[:, d, :],
                                       start=(d == 0), stop=(d == CH - 1))
                else:
                    pe.wait_ge(evacuated["A"], 4 * b + 4)
                    mm = split_product(ps[:, :], lambda a, c: a_mat[:, a, c, s[1] * P:(s[1] + 1) * P],
                                       lambda m, c: tn1[:, m, c, s[2] * HALF:(s[2] + 1) * HALF])
                mm.then_inc(ready[kind], 1)

            def step(s, b):
                kind = s[0]
                if kind in SHARED:
                    shared_tile(s, b)
                elif kind == "T":
                    n = s[1]
                    if n == 0:
                        pe.wait_ge(k_exp_done, CH * b + CH)
                    wait(pe, evacuated["T"], 8 * b + n - 1)
                    for d in range(CH):
                        mm = pe.transpose(kt_ps[n % 2][:, d * P:(d + 1) * P], ke[:, d, n * P:(n + 1) * P], cst[:, IDENT, :])
                    mm.then_inc(ready["T"], 1)
                elif kind == "X":
                    n = s[1]
                    pe.wait_ge(evacuated["V"], 8 * b + n + 1)
                    pe.wait_ge(evacuated["T"], 8 * b + n + 1)
                    if n == 0:
                        wait(pe, ctx_done, b)
                    for p in range(PAIRS):
                        mm = pe.matmul(ctx_ps[:, p, :], v_sb[:, n % 2, p * P:(p + 1) * P], kt_sb[:, n % 2, p * P:(p + 1) * P],
                                       start=(n == 0 and p == 0), stop=(n == 7), skip_group_check=True)
                    mm.then_inc(ready["X"], 1)
                elif kind == "MEAN":
                    j = job_index(b, s[1])
                    pe.wait_ge(total_ready, j + 1)
                    wait(pe, normalised, j)
                    pe.matmul(cast_ps[:, :], cst[:, MEAN_OF, :], total[:, :], start=True, stop=True).then_inc(mean_ready, 1)
                elif kind == "VAR":
                    j = job_index(b, s[1])
                    pe.wait_ge(sq_total_ready, j + 1)
                    wait(pe, eps_added, j)
                    for n in range(4):
                        mm = pe.matmul(var_ps[:, n:n + 1], total[:, n * P:(n + 1) * P], cst[:, MEAN_OF, 0:1],
                                       start=True, stop=True)
                    mm.then_inc(var_ready, 1)
                elif kind == "CAST":
                    j = job_index(b, s[1])
                    pe.wait_ge(diag_ready, j + 1)
                    pe.matmul(cast_ps[:, :], cst[:, ONES, :], diag[:, :, :].rearrange("p a n -> p (a n)"),
                              start=True, stop=True).then_inc(cast_ready, 1)

            pe.wait_ge(const_loaded, 16 * 5)
            for job in (NEXT0, NEXT1):
                for kind in ("MEAN", "VAR", "CAST"):
                    step((kind, job), -1)
            pe.wait_ge(kv_split, 1)
            iterations(pe, step)

        @block.scalar
        def _(act):
            def step(s, b):
                kind = s[0]
                ps = tile_ps[TILES1.index(s) % 3] if kind in SHARED else None
                if kind == "K":
                    d, half = s[1], s[2]
                    act.wait_ge(ready["K"], count(s, b))
                    wait(act, ready["A"], 4 * b)
                    nc.scalar.activation(ke[:, d, half * HALF:(half + 1) * HALF], ps[:, :], ACT.Identity,
                                         bias=bias[:, BK, d:d + 1]).then_inc(evacuated["K"], 1)
                elif kind == "E":
                    d = s[1]
                    act.wait_ge(k_max_ready, CH * b + d + 1)
                    nc.scalar.activation(ke[:, d, :], ke[:, d, :], ACT.Exp, bias=k_neg_max[:, d:d + 1],
                                         accum_out=k_sum[:, d:d + 1]).then_inc(k_exp_done, 1)
                elif kind == "T":
                    act.wait_ge(ready["T"], count(s, b))
                    wait(act, ready["X"], 8 * b + s[1] - 1)
                    nc.scalar.activation(kt_sb[:, s[1] % 2, :], kt_ps[s[1] % 2][:, :], ACT.Copy).then_inc(evacuated["T"], 1)
                elif kind == "G":
                    act.wait_ge(ready["G"], count(s, b))
                    act.wait_ge(k_inv_ready, b + 1)
                    nc.scalar.activation(g_sb[:, s[1], :], ps[:, :], ACT.Copy, scale=k_inv[:, s[1]:s[1] + 1])\
                        .then_inc(evacuated["G"], 1)
                elif kind in ("A", "WF"):
                    act.wait_ge(ready[kind], count(s, b))
                    if kind == "A":
                        wait(act, ready["O"], 8 * b)
                    dst = a_mat if kind == "A" else wf
                    nc.scalar.activation(dst[:, HI, s[1], :], ps[:, :], ACT.Copy).then_inc(a_hi_done, 1)
                elif kind == "MEAN":
                    j = job_index(b, s[1])
                    n, bb, half = norm_of(b, s[1])
                    act.wait_ge(centred, j + 1)
                    wait(act, sq_total_ready, j)
                    nc.scalar.activation(sq[:, :, :], halves(xc, half), ACT.Square).then_inc(squared, 1)
                elif kind == "SPLIT":
                    n, bb, half = norm_of(b, s[1])
                    act.wait_ge(normalised, job_index(b, s[1]) + 1)
                    if n == 1:
                        wait(act, ready["O"], 8 * (bb - 1) + 4 * (half + 1) if not isinstance(bb, int) or bb > 0 else 0)
                        dst = halves(tn1[:, HI, :, :], half)
                    else:
                        if half == 1:
                            act.wait_ge(ready["Y"], 8 * bb + 4)
                        dst = tn2[:, HI, :, :]
                    nc.scalar.activation(dst, halves(xc, half), ACT.Copy).then_inc(hi_done[n], 1)

            act.wait_ge(kv_loaded, 16)
            nc.scalar.activation(wkv[:, HI, :, :], ke[:, :, :], ACT.Copy).then_inc(kv_hi, 1)
            for job in (NEXT0, NEXT1):
                step(("MEAN", job), -1)
                step(("SPLIT", job), -1)
            act.wait_ge(kv_split, 1)
            iterations(act, step)

        @block.vector
        def _(dve):
            def dequantise(m):
                base = m * (2 * len(NF4) - 1)
                if m == 0:
                    dve.wait_ge(q_loaded, 32)
                for n, value in enumerate(NF4):
                    if n == 0:
                        nc.vector.tensor_scalar(w_lora[:, m, :], w_raw[:, m, :].bitcast(I32), 0.0, value,
                                                ALU.is_equal, ALU.mult).then_inc(nf4_chain, 1)
                    else:
                        nc.vector.tensor_scalar(resid[:, n % 2, :], w_raw[:, m, :].bitcast(I32), float(n), value,
                                                ALU.is_equal, ALU.mult).then_inc(nf4_chain, 1)
                        dve.wait_ge(nf4_chain, base + 2 * n)
                        nc.vector.tensor_tensor(w_lora[:, m, :], w_lora[:, m, :], resid[:, n % 2, :], ALU.add)\
                            .then_inc(nf4_chain, 1)
                dve.wait_ge(nf4_chain, base + 2 * len(NF4) - 1)
                blocks = w_lora[:, m, :].rearrange("p (k n) -> p k n", k=8)
                nc.vector.tensor_tensor(blocks, blocks, sc[:, m, :].unsqueeze(2).to_broadcast([P, 8, C // 8]), ALU.mult)\
                    .then_inc(dequantised, 1)

            def step(s, b):
                kind = s[0]
                ps = tile_ps[TILES1.index(s) % 3] if kind in SHARED else None
                if kind == "E":
                    d = s[1]
                    dve.wait_ge(evacuated["K"], 8 * b + 4 + d + 1)
                    nc.vector.tensor_reduce(k_neg_max[:, d:d + 1], ke[:, d, :], AX_X, ALU.max, negate=True)\
                        .then_inc(k_max_ready, 1)
                elif kind == "N":
                    dequantise(s[1])
                elif kind == "V":
                    n = s[1]
                    dve.wait_ge(ready["V"], count(s, b))
                    wait(dve, ready["X"], 8 * b + n - 1)
                    nc.vector.tensor_tensor(v_sb[:, n % 2, :], ps[:, :], bv_rows[:, :], ALU.add).then_inc(evacuated["V"], 1)
                elif kind == "X" and s[1] == 7:
                    dve.wait_ge(k_exp_done, CH * (b + 1))
                    nc.vector.reciprocal(k_inv[:, :], k_sum[:, :]).then_inc(k_inv_ready, 1)
                    dve.wait_ge(ready["X"], 8 * (b + 1))
                    for h in range(2):
                        rows = slice(64 * h, 64 * h + 64)
                        ins = nc.vector.tensor_copy(ctx_sb[rows, :, rows], ctx_ps[rows, :, rows])
                    ins.then_inc(ctx_done, 1)
                elif kind == "OB":
                    dve.wait_ge(ready["OB"], count(s, b))
                    nc.vector.tensor_tensor(ob[:, :], ps[:, 0:CH], bias[:, BO, :], ALU.add).then_inc(evacuated["OB"], 1)
                elif kind in ("A", "WF"):
                    dve.wait_ge(a_hi_done, 4 * (b + 1) + s[1] + 1 if kind == "A" else s[1] + 1)
                    dst = a_mat if kind == "A" else wf
                    nc.vector.tensor_tensor(dst[:, LO, s[1], :], ps[:, :], dst[:, HI, s[1], :].bitcast(F32), ALU.subtract)\
                        .then_inc(evacuated[kind], 1)
                elif kind == "O":
                    o, half, n = s[1], s[2], number(s)
                    dve.wait_ge(ready["O"], count(s, b))
                    dve.wait_ge(evacuated["OB"], b + 1)
                    dve.wait_ge(resid_loaded[n % 2], 16 * (4 * b + n // 2 + 1))
                    if o == 0:
                        wait(dve, stored[half], 16 * b)
                    nc.vector.scalar_tensor_tensor(out=t2[:, o, half * HALF:(half + 1) * HALF], in0=ps[:, :],
                                                   scalar=ob[:, o:o + 1], in1=resid[:, n % 2, :],
                                                   op0=ALU.add, op1=ALU.add).then_inc(evacuated["O"], 1)
                elif kind == "Y":
                    o, half = s[1], s[2]
                    dve.wait_ge(ready["Y"], count(s, b))
                    dst = t2[:, o, half * HALF:(half + 1) * HALF]
                    nc.vector.tensor_tensor(dst, ps[:, :], dst, ALU.add).then_inc(evacuated["Y"], 1)
                elif kind == "MEAN":
                    j = job_index(b, s[1])
                    n, bb, half = norm_of(b, s[1])
                    dve.wait_ge(mean_ready, j + 1)
                    src = halves(t2 if n == 2 else xc, half)
                    nc.vector.tensor_tensor(halves(xc, half), src, cast_ps[:, :].unsqueeze(1).to_broadcast([P, CH, HALF]),
                                            ALU.subtract).then_inc(centred, 1)
                elif kind == "VAR":
                    j = job_index(b, s[1])
                    dve.wait_ge(var_ready, j + 1)
                    nc.vector.tensor_scalar(var_eps[:, :], var_ps[:, 0:4], LN_EPS, None, ALU.add).then_inc(eps_added, 1)
                    dve.wait_ge(rstd_ready, j + 1)
                    wait(dve, cast_ready, j)
                    nc.vector.tensor_tensor(diag[:, :, :], cst[:, IDENT, :].unsqueeze(1).to_broadcast([P, 4, P]),
                                            rstd[:, :].unsqueeze(2).to_broadcast([P, 4, P]), ALU.mult).then_inc(diag_ready, 1)
                elif kind == "CAST":
                    j = job_index(b, s[1])
                    half = norm_of(b, s[1])[2]
                    dve.wait_ge(cast_ready, j + 1)
                    nc.vector.tensor_tensor(halves(xc, half), halves(xc, half),
                                            cast_ps[:, :].unsqueeze(1).to_broadcast([P, CH, HALF]), ALU.mult)\
                        .then_inc(normalised, 1)
                elif kind == "SPLIT":
                    n, bb, half = norm_of(b, s[1])
                    dve.wait_ge(hi_done[n], 2 * bb + half + 1)
                    if n == 1:
                        hi, dst = halves(tn1[:, HI, :, :], half), halves(tn1[:, LO, :, :], half)
                    else:
                        hi, dst = tn2[:, HI, :, :], tn2[:, LO, :, :]
                    nc.vector.tensor_tensor(dst, halves(xc, half), hi.bitcast(F32), ALU.subtract).then_inc(lo_done[n], 1)

            nc.vector.memset(ctx_sb[:, :, :], 0.0).then_inc(const_made, 1)
            nc.vector.memset(neg_half[:, :], -0.5).then_inc(const_made, 1)
            dve.wait_ge(const_loaded, 16 * 5)
            for job in (NEXT0, NEXT1):
                for kind in ("MEAN", "VAR", "CAST", "SPLIT"):
                    step((kind, job), -1)
                if job == NEXT0:
                    dve.wait_ge(kv_hi, 1)
                    nc.vector.tensor_tensor(wkv[:, LO, :, :], ke[:, :, :], wkv[:, HI, :, :].bitcast(F32), ALU.subtract)\
                        .then_inc(kv_split, 1)
            iterations(dve, step)

        @block.gpsimd
        def _(pool):
            def sum_chunks(src, chained, last_sem):
                nc.gpsimd.tensor_tensor(total[:, :], src[:, 0, :], src[:, 1, :], ALU.add).then_inc(pool_chain, 1)
                pool.wait_ge(pool_chain, chained + 1)
                nc.gpsimd.tensor_tensor(total[:, :], total[:, :], src[:, 2, :], ALU.add).then_inc(pool_chain, 1)
                pool.wait_ge(pool_chain, chained + 2)
                nc.gpsimd.tensor_tensor(total[:, :], total[:, :], src[:, 3, :], ALU.add).then_inc(last_sem, 1)

            def norm_sums(b, job):
                j = job_index(b, job)
                n, bb, half = norm_of(b, job)
                if n == 2:
                    pool.wait_ge(evacuated["O"], 8 * bb + 4 * (half + 1))
                else:
                    pool.wait_ge(xc_loaded[half], 16 * (bb + 1))
                wait(pool, var_ready, j)
                sum_chunks(halves(t2 if n == 2 else xc, half), 4 * j, total_ready)
                pool.wait_ge(squared, j + 1)
                pool.wait_ge(mean_ready, j + 1)
                sum_chunks(sq, 4 * j + 2, sq_total_ready)
                pool.wait_ge(eps_added, j + 1)
                nc.gpsimd.tensor_tensor(rstd[:, :], var_eps[:, :], neg_half[:, :], ALU.pow).then_inc(rstd_ready, 1)

            def step(s, b):
                if s[0] == "MEAN":
                    norm_sums(b, s[1])

            pool.wait_ge(const_made, 2)
            norm_sums(-1, NEXT0)
            norm_sums(-1, NEXT1)
            iterations(pool, step)


def program(nc, x, w_qk_t, w_v_t, w_proj_t, b_v0, vectors0, group_mean,
            w_kv_t, w_q, w_out_t, w_ffn_t, qidx, scales, b_v1, vectors1, consts, t_dram, out):
    with ExitStack() as ctx:
        def sem(name):
            return ctx.enter_context(nc.semaphore(name))

        layer0(nc, sem, x, w_qk_t, w_v_t, w_proj_t, b_v0, vectors0, group_mean, t_dram)
        layer1(nc, sem, t_dram, w_kv_t, w_q, w_out_t, w_ffn_t, qidx, scales, b_v1, vectors1, consts, out)


def kernel(**inputs):
    import numpy as np
    import concourse.bacc as bacc
    from concourse.bass_utils import run_bass_kernel_spmd

    def columns(*vs):
        return np.ascontiguousarray(np.stack([v.reshape(CH, P).T for v in vs], axis=1))

    a = {k: np.asarray(v) for k, v in inputs.items()}
    w0 = a["L0_conv_w_qkv"].reshape(HEADS, 3, HD, C)
    b0 = a["L0_conv_b_qkv"].reshape(HEADS, 3, HD)
    wq0, wk0, wv0 = (w0[:, i].reshape(C, C) for i in range(3))
    bq0, bk0, bv0 = (b0[:, i].reshape(C) for i in range(3))
    w1, b1 = a["L1_attn_W_qkv"], a["L1_attn_b_qkv"]
    same_group = np.arange(P)[:, None] // (C // GROUPS) == np.arange(P)[None, :] // (C // GROUPS)
    arrays = {
        "x": a["x"].reshape(B, C, L),
        "w_qk_t": np.concatenate([wq0.T, wk0.T], axis=1),
        "w_v_t": wv0.T,
        "w_proj_t": a["L0_conv_w_proj"].T,
        "b_v0": bv0,
        "vectors0": columns(bq0, bk0, a["L0_conv_b_proj"], a["L0_conv_gn_w"], a["L0_conv_gn_b"]),
        "group_mean": np.where(same_group, np.float32(GROUPS / C), np.float32(0)),
        "w_kv_t": w1[C:].T,
        "w_q": w1[:C],
        "w_out_t": a["L1_attn_W_out"].T,
        "w_ffn_t": a["L1_ffn_W"].T,
        "qidx": a["L1_ffn_qidx"],
        "scales": a["L1_ffn_scales"].reshape(C, C // 64),
        "b_v1": b1[2 * C:],
        "vectors1": columns(b1[:C], b1[C:2 * C], a["L1_attn_b_out"]),
        "consts": np.ascontiguousarray(np.stack(
            [np.full((P, P), 1 / C, np.float32), np.ones((P, P), np.float32), np.eye(P, dtype=np.float32)], axis=1)),
    }
    arrays = {f"in_{k}": np.ascontiguousarray(v) for k, v in arrays.items()}

    nc = bacc.Bacc("TRN2", target_bir_lowering=False, num_devices=1)
    args = [nc.dram_tensor(k, v.shape, mybir.dt.from_np(v.dtype), kind="ExternalInput").ap() for k, v in arrays.items()]
    args.append(nc.dram_tensor("t_between", (B, C, L), F32).ap())
    args.append(nc.dram_tensor("out_0", (B, C, L), F32, kind="ExternalOutput").ap())
    program(nc, *args)
    r = run_bass_kernel_spmd(nc, [arrays], core_ids=[0])
    return r.results[0]["out_0"].reshape(B, C, 32, 32)
```

```python
from contextlib import ExitStack

import concourse.bass as bass
import numpy as np
from concourse import mybir

F32 = mybir.dt.float32
F32R = mybir.dt.float32r
I32 = mybir.dt.int32
ALU = mybir.AluOpType
ACT = mybir.ActivationFunctionType
AX_X = mybir.AxisListType.X

P = 128
B, C, L = 8, 512, 1024
CH = C // P
HEADS = 8
HD = C // HEADS
PAIRS = HEADS // 2
HALF = 512
SC = L // P
UNITS = PAIRS * SC
NF4_W = C * C // B // P
GROUPS = 32
GN_EPS = 1e-5
LN_EPS = 1e-5
HI, LO = 0, 1
SPLITS = ((HI, HI), (HI, LO), (LO, HI))
NF4 = (-1.0, -0.6961928009986877, -0.5250730514526367, -0.39491748809814453, -0.28444138169288635,
       -0.18477343022833334, -0.09105003625154495, 0.0, 0.07958029955625534, 0.16093020141124725,
       0.24611230194568634, 0.33791524171829224, 0.44070982933044434, 0.5626170039176941,
       0.7229568362236023, 1.0)

QK_ORDER = [("Q", 0, 0), ("K", 0, 0), ("Q", 0, 1), ("K", 0, 1), ("K", 1, 0), ("Q", 1, 0), ("Q", 1, 1), ("K", 1, 1),
            ("Q", 2, 0), ("K", 2, 0), ("Q", 2, 1), ("K", 2, 1), ("Q", 3, 0), ("K", 3, 0), ("Q", 3, 1), ("K", 3, 1)]


def QK(kind, pair, half, rel=0):
    return ("QK", rel, QK_ORDER.index((kind, pair, half)))


def V(s, rel=0):
    return ("V", rel, s)


def H(j):
    return ("H", -1, j)


WHOLE = (0, 1)
FILL = {
    0: [(QK("K", 0, 1), WHOLE), (V(3), WHOLE)],
    1: [(V(4), WHOLE), (V(5), WHOLE)],
    2: [(V(6), WHOLE), (H(0), WHOLE)],
    3: [(V(7), WHOLE), (H(1), WHOLE)],
    4: [(QK("K", 1, 0), WHOLE), (H(2), WHOLE)],
    5: [(QK("Q", 1, 0), WHOLE), (H(3), WHOLE)],
    6: [(QK("Q", 1, 1), WHOLE), (H(4), WHOLE), (H(5), WHOLE)],
    7: [(H(6), WHOLE), (H(7), WHOLE)],
    8 * 3: [(QK("K", 3, 1), WHOLE)],
    8 * 3 + 5: [(QK("Q", 0, 0, 1), WHOLE), (QK("K", 0, 0, 1), WHOLE)],
    8 * 3 + 6: [(QK("Q", 0, 1, 1), WHOLE), (V(0, 1), WHOLE)],
    8 * 3 + 7: [(V(1, 1), WHOLE), (V(2, 1), WHOLE)],
}
for _p in (1, 2):
    FILL[8 * _p] = [(QK("K", _p, 1), (0,))]
    FILL[8 * _p + 1] = [(QK("K", _p, 1), (1,))]
    FILL[8 * _p + 2] = [(QK("Q", _p + 1, 0), (0,))]
    FILL[8 * _p + 3] = [(QK("Q", _p + 1, 0), (1,))]
    FILL[8 * _p + 4] = [(QK("K", _p + 1, 0), WHOLE)]
    FILL[8 * _p + 5] = [(QK("Q", _p + 1, 1), (0,))]
    FILL[8 * _p + 6] = [(QK("Q", _p + 1, 1), (1,))]
G1, G2 = ("G", 1, 0), ("G", 1, 1)
FILL[8 * 2 + 3].append((G1, WHOLE))
FILL[8 * 2 + 6].append((G2, WHOLE))
TILES = [t for k in range(UNITS) for t, parts in FILL.get(k, []) if 1 in parts]
NEXT_QKV = [t for k in range(24, UNITS) for t, _ in FILL.get(k, []) if t[1] == 1]


def deferred(k):
    return k % SC < SC - 1 and len(FILL.get(k, [])) == 1 and 1 in FILL[k][0][1]


GN_STATS = {9: 0, 11: 1, 13: 2, 15: 3}
GN_AGGREGATE, GN_POWER, GN_AFFINE = 16, 22, 24
GN_SCALE = {24: (0, 1), 26: (2,), 27: (3,)}
GN_LO = {25: (0,), 26: (1,), 27: (2,), 28: (3,)}


def exists(tile, b):
    if not isinstance(b, int):
        return True
    return {-1: tile[1] == 1, 0: tile[1] != -1, B - 1: tile[1] != 1, B: tile[1] == -1}.get(b, True)


def bank_of(tile):
    return TILES.index(tile) % 2


def bank_user_before(tile, b):
    n = TILES.index(tile)
    for m in range(n - 2, n - 2 * len(TILES), -2):
        prev, prev_b = TILES[m % len(TILES)], b + m // len(TILES)
        if isinstance(prev_b, int) and prev_b < -1:
            return None
        if exists(prev, prev_b):
            return prev, prev_b + prev[1]
    return None


assert len(TILES) % 2 == 0

FFN0, FFN1, NEXT0, NEXT1 = range(4)
BESIDE_LAST_BATCH = {
    25: [("INIT",), ("KV", 0), ("KV", 1), ("SUM", NEXT0, 0)],
    26: [("KV", 2), ("KV", 3), ("SUM", NEXT0, 1)],
    27: [("SUM", NEXT0, 2)],
    28: [("MEAN", NEXT0)],
    29: [("SUM", NEXT0, 3), ("SUM", NEXT0, 4)],
    30: [("SUM", NEXT0, 5)],
}
BESIDE_LAST_PROJECTION = {
    0: [("VAR", NEXT0), ("SUM", NEXT0, 6)] + [("SUM", NEXT1, i) for i in range(3)],
    1: [("CAST", NEXT0)],
    2: [("MEAN", NEXT1), ("SPLIT", NEXT0)],
    3: [("SUM", NEXT1, i) for i in range(3, 7)],
    5: [("VAR", NEXT1)],
    6: [("CAST", NEXT1), ("SPLIT", NEXT1)],
}


def layer0(nc, sem, x, w_qk_t, w_v_t, w_proj_t, b_v, vectors, group_mean, qidx, scales, t_dram, w_lora_dram):
    ctx = ExitStack()

    def sb(name, shape, dt=F32):
        return ctx.enter_context(nc.sbuf_tensor(name, shape, dt))

    with ctx:
        wv = sb("wv", [P, 2, CH, C], F32R)
        wqk = sb("wqk", [P, 2, CH, 2 * C], F32R)
        xn = sb("xn", [P, 2, CH, L], F32R)
        kk = sb("kk", [P, 2, 2, L], F32R)
        v_sb = sb("v_sb", [P, SC, C])
        probs = sb("probs", [P, 2, 2, L])
        qq = sb("qq", [P, 2, 2, L], F32R)
        wp = sb("wp", [P, 2, CH, C], F32R)
        a_sb = sb("a_sb", [P, 2, CH, L], F32R)
        x_ring = sb("x_ring", [P, 2, L])
        vs = sb("vs", [P, 2, 2 * HD])
        nf4_q = sb("nf4_q", [P, NF4_W], I32)
        nf4_w = sb("nf4_w", [P, NF4_W])
        nf4_pick = sb("nf4_pick", [P, NF4_W])
        nf4_scale = sb("nf4_scale", [P, NF4_W // 64])
        bv_rows = sb("bv_rows", [P, C])
        bias = sb("bias", [P, 5, CH])
        BQ, BK, BP, GW, GB = range(5)
        bq_scaled = sb("bq_scaled", [P, CH])
        gmat = sb("gmat", [P, P])
        neg_half = sb("neg_half", [P, CH])
        neg_max = sb("neg_max", [P, 2, 2])
        row_sum = sb("row_sum", [P, 2, 2])
        inv_sum = sb("inv_sum", [P, 2, 2])
        st = sb("st", [P, CH, 2, 6])
        mv = sb("mv", [P, CH, 2])
        g_mean = sb("g_mean", [P, CH])
        dev = sb("dev", [P, CH])
        dev2 = sb("dev2", [P, CH])
        spread = sb("spread", [P, CH])
        var_eps = sb("var_eps", [P, CH])
        rstd = sb("rstd", [P, CH])
        g_scale = sb("g_scale", [P, CH])
        g_tmp = sb("g_tmp", [P, CH])
        g_shift = sb("g_shift", [P, CH])
        stage = probs[:, :, :, :].rearrange("p a b l -> p (a b l)")

        s_ps = [ctx.enter_context(nc.psum_tensor(f"scores{h}", [P, L], F32)) for h in range(2)]
        pv_ps = ctx.enter_context(nc.psum_tensor("pv_ps", [P, L], F32))
        fill_ps = [ctx.enter_context(nc.psum_tensor(f"fill{i}", [P, HALF], F32)) for i in range(2)]

        const_loaded, weights_loaded, weights_split = sem("const_loaded"), sem("weights_loaded"), sem("weights_split")
        weights_hi = sem("weights_hi")
        const_made = sem("const_made")
        stats_loaded = [sem(f"stats_loaded{i}") for i in range(2)]
        norm_loaded = [sem(f"norm_loaded{i}") for i in range(2)]
        res_loaded = [sem(f"res_loaded{i}") for i in range(2)]
        late_loaded = [sem(f"late_res_loaded{i}") for i in range(CH)]
        stats_done, gn_aggregated, gn_chain = sem("stats_done"), sem("gn_aggregated"), sem("gn_chain")
        gn_power_in, gn_power_out, gn_affine = sem("gn_power_in"), sem("gn_power_out"), sem("gn_affine")
        x_scaled, xn_hi_done, xn_done = sem("x_scaled"), sem("xn_hi_done"), sem("xn_done")
        ready = {k: sem(f"{k}_tile_ready") for k in ("QK", "V", "H", "G")}
        evacuated = {k: sem(f"{k}_tile_evacuated") for k in ("QK", "V", "H", "G")}
        qk_hi_done = sem("qk_hi_done")
        k_copied = [sem(f"k_copied{h}") for h in range(2)]
        scores_ready = [sem(f"scores_ready{h}") for h in range(2)]
        max_ready = [sem(f"max_ready{h}") for h in range(2)]
        exp_done = [sem(f"exp_done{h}") for h in range(2)]
        inv_ready, vs_ready, pv_done = sem("inv_ready"), sem("vs_ready"), sem("pv_done")
        a_hi_done, a_done = sem("a_hi_done"), sem("a_done")
        t_stored = [sem(f"t_stored{i}") for i in range(2)]
        nf4_q_loaded, nf4_scale_loaded, nf4_done, nf4_stored = (sem("nf4_q_loaded"), sem("nf4_scale_loaded"), sem("nf4_done"),
                                                                sem("nf4_stored"))

        per_batch = {"QK": 16, "V": 8, "H": 8, "G": 2}

        def count(tile, b):
            return per_batch[tile[0]] * b + tile[2] + 1

        def wait(eng, s, value):
            if not isinstance(value, int) or value > 0:
                eng.wait_ge(s, value)

        def body_loop(eng, body):
            body(0)
            with eng.Fori(1, B - 1) as b:
                body(b)
            body(B - 1)

        def sync(sp, loads, late_res):
            def load_stats(b, i):
                if i >= 2:
                    sp.wait_ge(stats_done, CH * b + i - 1)
                elif isinstance(b, int) and b == 1:
                    sp.wait_ge(xn_done, i + 3)
                elif not isinstance(b, int) or b > 1:
                    sp.wait_ge(t_stored[i], 32 * (b - 1))
                sp.dma_start(x_ring[:, i % 2, :], x[b, i * P:(i + 1) * P, :]).then_inc(stats_loaded[i % 2], 16)

            def load_norm(b, i):
                if i >= 2:
                    sp.wait_ge(xn_done, CH * b + i - 1)
                else:
                    sp.wait_ge(stats_done, CH * b + i + 3)
                sp.dma_start(x_ring[:, i % 2, :], x[b, i * P:(i + 1) * P, :]).then_inc(norm_loaded[i % 2], 16)

            def load_residual(b, i):
                if i >= 2:
                    sp.wait_ge(t_stored[i % 2], 32 * b + 16)
                else:
                    sp.wait_ge(xn_done, CH * (b + 1) + i + 3)
                sp.dma_start(x_ring[:, i % 2, :], x[b, i * P:(i + 1) * P, :]).then_inc(res_loaded[i % 2], 16)

            def store_t(b, o):
                sp.wait_ge(evacuated["H"], 8 * b + 2 * o + 2)
                src = late_res[o] if isinstance(b, int) and b == B - 1 else x_ring[:, o % 2, :]
                sp.dma_start(t_dram[b, o * P:(o + 1) * P, :], src).then_inc(t_stored[o % 2], 16)

            def load_nf4_indices(b):
                if not isinstance(b, int) or b > 0:
                    sp.wait_ge(nf4_done, 32 * b - 2)
                sp.dma_start(nf4_q[:, :], qidx[b]).then_inc(nf4_q_loaded, 16)

            def load_nf4_scales(b):
                sp.dma_start(nf4_scale[:, :], scales[b]).then_inc(nf4_scale_loaded, 16)

            def store_nf4(b):
                sp.wait_ge(nf4_done, 32 * b + 32)
                sp.dma_start(w_lora_dram[b], nf4_w[:, :]).then_inc(nf4_stored, 16)

            def copy_k(b, pair, half):
                sp.wait_ge(evacuated["QK"], count(QK("K", pair, half), b))
                cols = slice(half * HALF, (half + 1) * HALF)
                sp.dma_start(kk[64:128, 0, :, cols].bitcast(F32), kk[0:64, 0, :, cols].bitcast(F32)).then_inc(k_copied[half], 16)
                sp.dma_start(kk[0:64, 1, :, cols].bitcast(F32), kk[64:128, 1, :, cols].bitcast(F32)).then_inc(k_copied[half], 16)

            sp.dma_start(stage[:, :].rearrange("p (c n) -> p c n", c=CH),
                         w_qk_t.rearrange("(c p) n -> p c n", p=P)).then_inc(weights_loaded, 16)
            sp.dma_start(gmat[:, :], group_mean).then_inc(const_loaded, 16)
            sp.dma_start(bv_rows[:, :], b_v.partition_broadcast(P)).then_inc(const_loaded, 16)
            sp.dma_start(bias[:, :, :], vectors).then_inc(const_loaded, 16)
            for i in range(CH):
                load_stats(0, i)
            sp.wait_ge(weights_split, 2)
            sp.dma_start(stage[:, 0:CH * C].rearrange("p (c n) -> p c n", c=CH),
                         w_v_t.rearrange("(c p) n -> p c n", p=P)).then_inc(weights_loaded, 16)
            sp.dma_start(stage[:, CH * C:].rearrange("p (c n) -> p c n", c=CH),
                         w_proj_t.rearrange("(c p) n -> p c n", p=P)).then_inc(weights_loaded, 16)
            for i in range(CH):
                load_norm(0, i)
            load_nf4_indices(0)
            load_nf4_scales(0)
            copy_k(0, 0, 0)

            def body(b):
                first, last = isinstance(b, int) and b == 0, isinstance(b, int) and b == B - 1
                copy_k(b, 0, 1)
                if not first:
                    load_residual(b - 1, 0)
                    load_residual(b - 1, 1)
                    store_t(b - 1, 0)
                copy_k(b, 1, 0)
                if not first:
                    load_residual(b - 1, 2)
                    store_t(b - 1, 1)
                    load_residual(b - 1, 3)
                    store_t(b - 1, 2)
                    store_t(b - 1, 3)
                if not last:
                    load_stats(b + 1, 0)
                    load_stats(b + 1, 1)
                copy_k(b, 1, 1)
                if not last:
                    load_stats(b + 1, 2)
                    load_stats(b + 1, 3)
                else:
                    sp.wait_ge(ready["V"], 8 * B)
                    loads("wv spent")
                copy_k(b, 2, 0)
                copy_k(b, 2, 1)
                if not last:
                    load_norm(b + 1, 0)
                    load_norm(b + 1, 1)
                copy_k(b, 3, 0)
                copy_k(b, 3, 1)
                if not last:
                    load_norm(b + 1, 2)
                    load_norm(b + 1, 3)
                    copy_k(b + 1, 0, 0)
                    load_nf4_indices(b + 1)
                    store_nf4(b)
                    load_nf4_scales(b + 1)
                else:
                    for i in range(2):
                        sp.wait_ge(t_stored[i], 32 * b)
                    loads("wqk, xn and x_ring spent")
                    for o in range(CH):
                        if o == 2:
                            sp.wait_ge(scores_ready[1], UNITS * b + 3 * SC)
                        sp.dma_start(late_res[o], x[b, o * P:(o + 1) * P, :]).then_inc(late_loaded[o], 16)
                    store_nf4(b)

            body_loop(sp, body)
            for o in range(CH):
                store_t(B - 1, o)
            for i in range(2):
                sp.wait_ge(t_stored[i], 32 * B)
            sp.wait_ge(nf4_stored, 16 * B)

        def tensor(pe, step1):
            def split_product(out, stationary, moving, parts, before_last_chunk=None):
                steps = [(c, a, m) for c in range(CH) for a, m in SPLITS]
                cut = len(steps) // 2
                for part in parts:
                    for k in range(part * cut, (part + 1) * cut):
                        c, a, m = steps[k]
                        if k == len(steps) - len(SPLITS) and before_last_chunk:
                            before_last_chunk()
                        mm = pe.matmul(out, stationary(a, c), moving(m, c), start=(k == 0), stop=(k == len(steps) - 1))
                return mm

            def tile(t, b, parts):
                kind, rel, n = t
                if isinstance(b, int) and b == B:
                    out = s_ps[n // 2 % 2][:, n % 2 * HALF:(n % 2 + 1) * HALF]
                    if n >= 4:
                        pe.wait_ge(evacuated["H"], 8 * (B - 1) + n - 3)
                    elif n % 2 == 0:
                        pe.wait_ge(exp_done[n // 2], UNITS * B)
                else:
                    out = fill_ps[bank_of(t)]
                if 0 in parts:
                    before = bank_user_before(t, b) if not isinstance(b, int) or b < B else None
                    if before:
                        wait(pe, evacuated[before[0][0]], count(*before))
                    if kind in ("QK", "V") and rel == 1:
                        pe.wait_ge(xn_done, CH * (b + 2))
                    if kind == "H" and n == 0:
                        pe.wait_ge(a_done, 2 * (PAIRS * b - 1))
                if kind == "QK":
                    which, pair, half = QK_ORDER[n]
                    col = (pair if which == "Q" else PAIRS + pair) * P
                    mm = split_product(out[:, :], lambda a, c: wqk[:, a, c, col:col + P],
                                       lambda m, c: xn[:, m, c, half * HALF:(half + 1) * HALF], parts)
                elif kind == "V":
                    mm = split_product(out[:, :], lambda a, c: xn[:, a, c, n * P:(n + 1) * P],
                                       lambda m, c: wv[:, m, c, :], parts)
                elif kind == "H":
                    o, half = n // 2, n % 2
                    mm = split_product(out[:, :], lambda a, c: wp[:, a, c, o * P:(o + 1) * P],
                                       lambda m, c: a_sb[:, m, c, half * HALF:(half + 1) * HALF], parts,
                                       (lambda: pe.wait_ge(a_done, 2 * PAIRS * b)) if n == 0 else None)
                else:
                    pe.wait_ge(gn_aggregated, 2 * (b + 1) + n + 1)
                    mm = pe.matmul(out[:, 0:CH], gmat[:, :], mv[:, :, 0] if n == 0 else spread[:, :],
                                   start=True, stop=True)
                if 1 in parts:
                    mm.then_inc(ready[kind], 1)

            def scores(b, k, h):
                pair, s = k // SC, k % SC
                g = UNITS * b + k
                if s == 0 and h == 0:
                    pe.wait_ge(evacuated["QK"], count(QK("Q", pair, 1), b))
                if s % 4 == 0 and h == 0:
                    pe.wait_ge(k_copied[s // 4], 32 * (PAIRS * b + pair + 1))
                wait(pe, exp_done[h], g)
                for half in range(2):
                    for part in (HI, LO):
                        mm = pe.matmul(s_ps[h][:, half * HALF:(half + 1) * HALF],
                                       kk[:, h, part, s * P:(s + 1) * P],
                                       qq[:, pair % 2, h, half * HALF:(half + 1) * HALF],
                                       start=(part == HI), stop=(part == LO))
                mm.then_inc(scores_ready[h], 1)

            def values(b, k):
                s = k % SC
                pe.wait_ge(vs_ready, UNITS * b + k + 1)
                for half in range(2):
                    if s == 0:
                        wait(pe, a_done, 2 * (PAIRS * b + k // SC) - 1 + half)
                    for h in range(2):
                        mm = pe.matmul(pv_ps[64 * h:64 * h + 64, half * HALF:(half + 1) * HALF],
                                       vs[:, k % 2, h * HD:(h + 1) * HD],
                                       probs[:, k % 2, h, half * HALF:(half + 1) * HALF],
                                       start=(s == 0), stop=(s == SC - 1))
                mm.then_inc(pv_done, 1)

            pe.wait_ge(const_loaded, 16 * 3)
            tile(G1, -1, WHOLE)
            tile(G2, -1, WHOLE)
            pe.wait_ge(weights_split, 4)
            for t in NEXT_QKV:
                tile(t, -1, WHOLE)

            def body(b):
                for k in range(UNITS):
                    fill = [(t, parts) for t, parts in FILL.get(k, []) if exists(t, b)]
                    scores(b, k, 0)
                    between = len(fill) == 1
                    for t, parts in fill[:between]:
                        tile(t, b, parts)
                    scores(b, k, 1)
                    if k > 0:
                        values(b, k - 1)
                    elif not isinstance(b, int) or b > 0:
                        values(b - 1, UNITS - 1)
                    for t, parts in fill[between:]:
                        tile(t, b, parts)
                    if isinstance(b, int) and b == B - 1:
                        for s in BESIDE_LAST_BATCH.get(k, ()):
                            step1(s, -1)

            body_loop(pe, body)
            values(B - 1, UNITS - 1)
            for j in range(8):
                tile(H(j), B, WHOLE)
                for s in BESIDE_LAST_PROJECTION.get(j, ()):
                    step1(s, -1)

        def scalar(act, step1):
            def evacuate(t, b):
                kind, rel, n = t
                bb = b + rel
                if kind != "QK":
                    return
                which, pair, half = QK_ORDER[n]
                act.wait_ge(ready["QK"], count(t, bb))
                cols = slice(half * HALF, (half + 1) * HALF)
                ps = fill_ps[bank_of(t)]
                if which == "K":
                    wait(act, scores_ready[1], UNITS * bb + SC * (pair - 1) + 4 * (half + 1))
                    dst = [kk[64 * h:64 * h + 64, h, HI, cols] for h in range(2)]
                    add = [bias[64 * h:64 * h + 64, BK, pair:pair + 1] for h in range(2)]
                else:
                    wait(act, scores_ready[1], UNITS * bb + SC * (pair - 1))
                    dst = [qq[64 * h:64 * h + 64, pair % 2, h, cols] for h in range(2)]
                    add = [bq_scaled[64 * h:64 * h + 64, pair:pair + 1] for h in range(2)]
                for h in range(2):
                    ins = nc.scalar.activation(dst[h], ps[64 * h:64 * h + 64, :], ACT.Identity, bias=add[h])
                ins.then_inc(qk_hi_done, 1)

            def exponentials(b, k):
                g = UNITS * b + k
                for h in range(2):
                    act.wait_ge(max_ready[h], g + 1)
                    wait(act, pv_done, g - 1 if not isinstance(g, int) or g > 1 else 0)
                    nc.scalar.activation(probs[:, k % 2, h, :], s_ps[h][:, :], ACT.Exp,
                                         bias=neg_max[:, k % 2, h:h + 1],
                                         accum_out=row_sum[:, k % 2, h:h + 1]).then_inc(exp_done[h], 1)

            def attention_hi(b, pair):
                act.wait_ge(pv_done, UNITS * b + SC * (pair + 1))
                wait(act, ready["H"], 8 * b)
                for half in range(2):
                    cols = slice(half * HALF, (half + 1) * HALF)
                    nc.scalar.activation(a_sb[:, HI, pair, cols], pv_ps[:, cols], ACT.Copy).then_inc(a_hi_done, 1)

            def normalised_hi(b, i):
                act.wait_ge(x_scaled, CH * b + i + 1)
                wait(act, ready["QK"], 16 * b)
                nc.scalar.activation(xn[:, HI, i, :], x_ring[:, i % 2, :], ACT.Copy).then_inc(xn_hi_done, 1)

            act.wait_ge(weights_loaded, 16)
            raw = stage[:, :].rearrange("p (c n) -> p c n", c=CH)
            nc.scalar.activation(wqk[:, HI, :, 0:C], raw[:, :, 0:C], ACT.Copy, scale=0.125).then_inc(weights_hi, 1)
            nc.scalar.activation(wqk[:, HI, :, C:], raw[:, :, C:], ACT.Copy).then_inc(weights_hi, 1)
            act.wait_ge(weights_loaded, 48)
            nc.scalar.activation(wv[:, HI, :, :].rearrange("p c n -> p (c n)"), stage[:, 0:CH * C],
                                 ACT.Copy).then_inc(weights_hi, 1)
            nc.scalar.activation(wp[:, HI, :, :].rearrange("p c n -> p (c n)"), stage[:, CH * C:],
                                 ACT.Copy).then_inc(weights_hi, 1)
            act.wait_ge(const_made, 2)
            for i in range(CH):
                normalised_hi(0, i)
            for t in NEXT_QKV:
                evacuate(t, -1)

            def body(b):
                last = isinstance(b, int) and b == B - 1
                for k in range(UNITS):
                    exponentials(b, k)
                    if k % SC == 0 and k > 0:
                        attention_hi(b, k // SC - 1)
                    elif k == 0 and (not isinstance(b, int) or b > 0):
                        attention_hi(b - 1, PAIRS - 1)
                    for t, parts in FILL.get(k, []):
                        if 1 in parts and exists(t, b):
                            evacuate(t, b)
                    if not last:
                        for i in GN_SCALE.get(k, ()):
                            normalised_hi(b + 1, i)
                    else:
                        for s in BESIDE_LAST_BATCH.get(k, ()):
                            step1(s, -1)

            body_loop(act, body)
            attention_hi(B - 1, PAIRS - 1)
            for j in range(8):
                for s in BESIDE_LAST_PROJECTION.get(j, ()):
                    step1(s, -1)

        def vector(dve, step1, late_res):
            def evacuate(t, b):
                kind, rel, n = t
                bb = b + rel
                late = isinstance(b, int) and b == B
                ps = s_ps[n // 2 % 2][:, n % 2 * HALF:(n % 2 + 1) * HALF] if late else fill_ps[bank_of(t)]
                if kind == "QK":
                    which, pair, half = QK_ORDER[n]
                    dve.wait_ge(qk_hi_done, count(t, bb))
                    cols = slice(half * HALF, (half + 1) * HALF)
                    for h in range(2):
                        rows, other = slice(64 * h, 64 * h + 64), slice(64 - 64 * h, 128 - 64 * h)
                        if which == "K":
                            hi, dst, add = kk[rows, h, HI, cols], kk[rows, h, LO, cols], bias[rows, BK, pair:pair + 1]
                        else:
                            hi, dst = qq[rows, pair % 2, h, cols], qq[other, pair % 2, h, cols]
                            add = bq_scaled[rows, pair:pair + 1]
                        ins = nc.vector.scalar_tensor_tensor(out=dst, in0=ps[rows, :], scalar=add, in1=hi.bitcast(F32),
                                                             op0=ALU.add, op1=ALU.subtract)
                    ins.then_inc(evacuated["QK"], 1)
                elif kind == "V":
                    dve.wait_ge(ready["V"], count(t, bb))
                    wait(dve, vs_ready, UNITS * bb - SC + n + 1 if not isinstance(bb, int) or bb > 0 else 0)
                    nc.vector.tensor_tensor(v_sb[:, n, :], ps[:, :], bv_rows[:, :], ALU.add)\
                        .then_inc(evacuated["V"], 1)
                elif kind == "H":
                    o, half = n // 2, n % 2
                    dve.wait_ge(ready["H"], count(t, bb))
                    if late:
                        dve.wait_ge(late_loaded[o], 16)
                    else:
                        dve.wait_ge(res_loaded[o % 2], 32 * bb + 16 * (o // 2 + 1))
                    slot = (late_res[o] if late else x_ring[:, o % 2, :])[:, half * HALF:(half + 1) * HALF]
                    nc.vector.scalar_tensor_tensor(out=slot, in0=ps[:, :], scalar=bias[:, BP, o:o + 1], in1=slot,
                                                   op0=ALU.add, op1=ALU.add).then_inc(evacuated["H"], 1)
                elif n == 0:
                    group_spread(bb)
                else:
                    dve.wait_ge(ready["G"], count(t, bb))
                    nc.vector.tensor_scalar(var_eps[:, :], ps[:, 0:CH], GN_EPS, None, ALU.add)\
                        .then_inc(evacuated["G"], 1)

            def statistics(b, i):
                dve.wait_ge(stats_loaded[i % 2], 32 * b + 16 * (i // 2 + 1))
                for half in range(2):
                    ins = nc.vector.bn_stats(st[:, i, half, :], x_ring[:, i % 2, half * HALF:(half + 1) * HALF])
                ins.then_inc(stats_done, 1)

            def aggregate(b):
                dve.wait_ge(stats_done, CH * (b + 1))
                nc.vector.memset(g_tmp[:, :], 0.0)
                for i in range(CH):
                    ins = nc.vector.bn_aggr(mv[:, i, :], st[:, i, :, :])
                ins.then_inc(gn_aggregated, 1)

            def group_spread(b):
                dve.wait_ge(ready["G"], count(G1, b))
                nc.vector.tensor_copy(g_mean[:, :], fill_ps[bank_of(G1)][:, 0:CH]).then_inc(evacuated["G"], 1)
                dve.wait_ge(evacuated["G"], count(G1, b))
                nc.vector.tensor_tensor(dev[:, :], mv[:, :, 0], g_mean[:, :], ALU.subtract).then_inc(gn_chain, 1)
                dve.wait_ge(gn_chain, 2 * b + 1)
                nc.vector.tensor_tensor(dev2[:, :], dev[:, :], dev[:, :], ALU.mult).then_inc(gn_chain, 1)
                dve.wait_ge(gn_chain, 2 * b + 2)
                nc.vector.tensor_tensor(spread[:, :], dev2[:, :], mv[:, :, 1], ALU.add).then_inc(gn_aggregated, 1)

            def affine(b):
                dve.wait_ge(gn_power_out, b + 1)
                nc.vector.tensor_tensor(g_scale[:, :], rstd[:, :], bias[:, GW, :], ALU.mult).then_inc(gn_affine, 1)
                dve.wait_ge(gn_affine, 3 * b + 1)
                nc.vector.tensor_tensor(g_tmp[:, :], g_mean[:, :], g_scale[:, :], ALU.mult).then_inc(gn_affine, 1)
                dve.wait_ge(gn_affine, 3 * b + 2)
                nc.vector.tensor_tensor(g_shift[:, :], bias[:, GB, :], g_tmp[:, :], ALU.subtract).then_inc(gn_affine, 1)

            def scale_x(b, i):
                dve.wait_ge(norm_loaded[i % 2], 32 * b + 16 * (i // 2 + 1))
                if i == 0:
                    dve.wait_ge(gn_affine, 3 * (b + 1))
                slot = x_ring[:, i % 2, :]
                nc.vector.tensor_scalar(slot, slot, g_scale[:, i:i + 1], g_shift[:, i:i + 1], ALU.mult, ALU.add)\
                    .then_inc(x_scaled, 1)

            def normalised_lo(b, i):
                dve.wait_ge(xn_hi_done, CH * b + i + 1)
                nc.vector.tensor_tensor(xn[:, LO, i, :], x_ring[:, i % 2, :], xn[:, HI, i, :].bitcast(F32),
                                        ALU.subtract).then_inc(xn_done, 1)

            def attention_lo(b, pair):
                for half in range(2):
                    dve.wait_ge(a_hi_done, 2 * (PAIRS * b + pair) + half + 1)
                    cols = slice(half * HALF, (half + 1) * HALF)
                    nc.vector.tensor_tensor(a_sb[:, LO, pair, cols], pv_ps[:, cols], a_sb[:, HI, pair, cols].bitcast(F32),
                                            ALU.subtract).then_inc(a_done, 1)

            def maxima(b, k):
                for h in range(2):
                    dve.wait_ge(scores_ready[h], UNITS * b + k + 1)
                    nc.vector.tensor_reduce(neg_max[:, k % 2, h:h + 1], s_ps[h][:, :], AX_X, ALU.max,
                                            negate=True).then_inc(max_ready[h], 1)

            def inverse_sums(b, k):
                g = UNITS * b + k
                for h in range(2):
                    dve.wait_ge(exp_done[h], g + 1)
                wait(dve, vs_ready, g - 1 if not isinstance(g, int) or g > 1 else 0)
                nc.vector.reciprocal(inv_sum[:, k % 2, :], row_sum[:, k % 2, :]).then_inc(inv_ready, 1)

            nc.vector.memset(neg_half[:, :], -0.5).then_inc(const_made, 1)
            dve.wait_ge(const_loaded, 16 * 3)
            nc.vector.tensor_scalar(bq_scaled[:, :], bias[:, BQ, :], 0.125, None, ALU.mult).then_inc(const_made, 1)
            for i in range(CH):
                statistics(0, i)
            aggregate(0)
            evacuate(G1, -1)
            evacuate(G2, -1)
            raw = stage[:, :].rearrange("p (c n) -> p c n", c=CH)
            dve.wait_ge(weights_hi, 1)
            nc.vector.scalar_tensor_tensor(out=wqk[:, LO, :, 0:C], in0=raw[:, :, 0:C], scalar=0.125,
                                           in1=wqk[:, HI, :, 0:C].bitcast(F32), op0=ALU.mult, op1=ALU.subtract)\
                .then_inc(weights_split, 1)
            dve.wait_ge(weights_hi, 2)
            nc.vector.tensor_tensor(wqk[:, LO, :, C:], raw[:, :, C:], wqk[:, HI, :, C:].bitcast(F32), ALU.subtract)\
                .then_inc(weights_split, 1)
            affine(0)
            scale_x(0, 0)
            scale_x(0, 1)
            normalised_lo(0, 0)
            normalised_lo(0, 1)
            for n, w in ((0, wv), (1, wp)):
                dve.wait_ge(weights_hi, 3 + n)
                nc.vector.tensor_tensor(w[:, LO, :, :].rearrange("p c n -> p (c n)"),
                                        stage[:, n * CH * C:(n + 1) * CH * C],
                                        w[:, HI, :, :].rearrange("p c n -> p (c n)").bitcast(F32), ALU.subtract)\
                    .then_inc(weights_split, 1)
            scale_x(0, 2)
            scale_x(0, 3)
            normalised_lo(0, 2)
            normalised_lo(0, 3)
            for t in NEXT_QKV:
                evacuate(t, -1)

            def body(b):
                last = isinstance(b, int) and b == B - 1
                for k in range(UNITS):
                    maxima(b, k)
                    if k % SC and deferred(k - 1):
                        evacuate(FILL[k - 1][0][0], b)
                    if not last and k in GN_STATS:
                        statistics(b + 1, GN_STATS[k])
                    if not last:
                        if k == GN_AFFINE:
                            affine(b + 1)
                        for i in GN_LO.get(k, ()):
                            normalised_lo(b + 1, i)
                        for i in GN_SCALE.get(k, ()):
                            scale_x(b + 1, i)
                    inverse_sums(b, k)
                    if k % SC == 0 and k > 0:
                        attention_lo(b, k // SC - 1)
                    elif k == 0 and (not isinstance(b, int) or b > 0):
                        attention_lo(b - 1, PAIRS - 1)
                    for t, parts in FILL.get(k, []):
                        if 1 in parts and exists(t, b) and not deferred(k):
                            evacuate(t, b)
                    if not last:
                        if k == GN_AGGREGATE:
                            aggregate(b + 1)
                    else:
                        for s in BESIDE_LAST_BATCH.get(k, ()):
                            step1(s, -1)

            body_loop(dve, body)
            attention_lo(B - 1, PAIRS - 1)
            for j in range(8):
                evacuate(H(j), B)
                for s in BESIDE_LAST_PROJECTION.get(j, ()):
                    step1(s, -1)

        def gpsimd(pool, step1):
            def power(b):
                pool.wait_ge(evacuated["G"], 2 * (b + 1))
                nc.gpsimd.tensor_tensor(rstd[:, :], var_eps[:, :], neg_half[:, :], ALU.pow).then_inc(gn_power_out, 1)

            def dequantise(b, k):
                if k == 1:
                    nc.gpsimd.tensor_scalar(nf4_w[:, :], nf4_q[:, :], 0.0, NF4[0], ALU.is_equal, ALU.mult).then_inc(nf4_done, 1)
                if k % 2 == 1 and k < UNITS - 1:
                    n = k // 2 + 1
                    nc.gpsimd.tensor_scalar(nf4_pick[:, :], nf4_q[:, :], float(n), NF4[n], ALU.is_equal, ALU.mult)\
                        .then_inc(nf4_done, 1)
                elif k == UNITS - 1:
                    blocks = nf4_w[:, :].rearrange("p (k n) -> p k n", n=64)
                    nc.gpsimd.tensor_tensor(blocks, blocks, nf4_scale[:, :].unsqueeze(2).to_broadcast([P, NF4_W // 64, 64]),
                                            ALU.mult).then_inc(nf4_done, 1)
                elif k > 0:
                    nc.gpsimd.tensor_tensor(nf4_w[:, :], nf4_w[:, :], nf4_pick[:, :], ALU.add).then_inc(nf4_done, 1)

            pool.wait_ge(const_made, 1)
            power(0)

            def body(b):
                last = isinstance(b, int) and b == B - 1
                for k in range(UNITS):
                    g = UNITS * b + k
                    pair, s = k // SC, k % SC
                    pool.wait_ge(inv_ready, g + 1)
                    if pair == 0:
                        pool.wait_ge(evacuated["V"], 8 * b + s + 1)
                    wait(pool, pv_done, g - 1 if not isinstance(g, int) or g > 1 else 0)
                    if k == 1:
                        pool.wait_ge(nf4_q_loaded, 16 * b + 16)
                        wait(pool, nf4_stored, 16 * b)
                    elif k > 1:
                        pool.wait_ge(nf4_done, 32 * b + k)
                    if k == UNITS - 1:
                        pool.wait_ge(nf4_scale_loaded, 16 * b + 16)
                    nc.gpsimd.tensor_tensor(
                        vs[:, k % 2, :].rearrange("p (h d) -> p h d", h=2),
                        v_sb[:, s, pair * P:(pair + 1) * P].rearrange("p (h d) -> p h d", h=2),
                        inv_sum[:, k % 2, :].unsqueeze(2).to_broadcast([P, 2, HD]), ALU.mult).then_inc(vs_ready, 1)
                    if k == GN_POWER and not last:
                        power(b + 1)
                    dequantise(b, k)
                    if last:
                        for step in BESIDE_LAST_BATCH.get(k, ()):
                            step1(step, -1)

            body_loop(pool, body)
            for j in range(8):
                for step in BESIDE_LAST_PROJECTION.get(j, ()):
                    step1(step, -1)

        engines = {"sync": sync, "tensor": tensor, "scalar": scalar, "vector": vector, "gpsimd": gpsimd}
        spent = {"QK": (ready["QK"], 16 * B), "QK read": (evacuated["QK"], 16 * B), "scores": (scores_ready[1], UNITS * B),
                 "v": (vs_ready, UNITS * B), "H": evacuated["H"], "nf4": (nf4_stored, 16 * B)}
    return engines, spent


STEPS = (
    [("K", 0, 0), ("K", 1, 0), ("MEAN", FFN0), ("K", 2, 0), ("K", 3, 0), ("K", 0, 1),
     ("K", 1, 1), ("E", 0), ("VAR", FFN0), ("K", 2, 1), ("E", 1), ("CAST", FFN0), ("K", 3, 1), ("E", 2), ("E", 3),
     ("V", 0), ("SPLIT", FFN0), ("V", 1), ("T", 0), ("T", 1), ("X", 0), ("MEAN", FFN1),
     ("Y", 0, 0), ("Y", 1, 0), ("Y", 2, 0), ("X", 1), ("V", 2), ("T", 2), ("VAR", FFN1), ("Y", 3, 0),
     ("CAST", FFN1), ("V", 3), ("T", 3), ("X", 2), ("SPLIT", FFN1), ("MEAN", NEXT0),
     ("V", 4), ("T", 4), ("X", 3), ("V", 5), ("T", 5), ("X", 4), ("V", 6), ("T", 6),
     ("X", 5), ("VAR", NEXT0), ("V", 7), ("CAST", NEXT0), ("T", 7), ("X", 6), ("MEAN", NEXT1),
     ("Y", 0, 1), ("X", 7), ("Y", 1, 1), ("Y", 2, 1),
     ("G", 0), ("G", 1), ("G", 2), ("G", 3), ("Y", 3, 1), ("VAR", NEXT1), ("OB",), ("CAST", NEXT1),
     ("A", 0), ("A", 1), ("A", 2), ("A", 3), ("WF", 0), ("WF", 1), ("WF", 2), ("WF", 3)]
    + [("O", o, 0) for o in range(CH)] + [("SPLIT", NEXT0)] + [("O", o, 1) for o in range(CH)] + [("SPLIT", NEXT1)])
SHARED = ("K", "V", "Y", "WF", "G", "OB", "A", "O")
TILES1 = [s for s in STEPS if s[0] in SHARED]
LATER = {"MEAN", "VAR", "CAST", "SPLIT"}


def step_exists(step, b):
    kind = step[0]
    if kind == "WF":
        return isinstance(b, int) and b == 0
    if not isinstance(b, int):
        return True
    ffn = kind == "Y" or (kind in LATER and step[1] in (FFN0, FFN1))
    following = kind in LATER and not ffn
    return {-1: following, 0: not ffn, B - 1: not following, B: ffn}.get(b, True)


def bank1_user_before(step, b):
    n = TILES1.index(step)
    for m in range(n - 3, n - 3 * len(TILES1), -1):
        if (m % len(TILES1)) % 3 != n % 3:
            continue
        prev, prev_b = TILES1[m % len(TILES1)], b + m // len(TILES1)
        if isinstance(prev_b, int) and prev_b < 0:
            return None
        if step_exists(prev, prev_b):
            return prev, prev_b
    return None


def layer1(nc, sem, spent, t_dram, w_kv_t, w_q, w_out_t, w_ffn_t, w_lora_dram, b_v, vectors, consts, out):
    ctx = ExitStack()

    def sb(name, shape, dt=F32):
        return ctx.enter_context(nc.sbuf_tensor(name, shape, dt))

    with ctx:
        used = [0]

        def part(name, shape, dt=F32):
            used[0] += -(-int(np.prod(shape[1:])) * 4 // 32) * 32
            return sb(name, shape, dt)

        ke = part("ke", [P, CH, L])
        g_sb = ke[:, 0:2, :].rearrange("p a (b n) -> p (a b) n", b=2)
        xc = part("xc", [P, CH, L])
        wkv = part("wkv", [P, 2, CH, 2 * C], F32R)
        total = part("total", [P, HALF])
        diag = part("diag", [P, 4, P])
        bv_rows = part("bv1_rows", [P, C])
        cst = part("cst", [P, 3, P])
        MEAN_OF, ONES, IDENT = range(3)
        bias = part("bias1", [P, 3, CH])
        BQ, BK, BO = range(3)
        neg_half = part("neg_half1", [P, 4])
        var_eps = part("var_eps1", [P, 4])
        rstd = part("rstd1", [P, 4])
        k_neg_max = part("k_neg_max", [P, CH])
        k_sum = part("k_sum", [P, CH])
        k_inv = part("k_inv", [P, CH])
        ob = part("ob", [P, CH])
        part("gap", [P, 72 * 256 - used[0] // 4])
        wo = part("wo", [P, CH, C])
        tn1 = part("tn1", [P, 2, CH, L], F32R)
        kt_sb = part("kt_sb", [P, 2, C])
        v_sb = part("v1_sb", [P, 2, C])
        a_lo = part("a_lo", [P, CH, C], F32R)
        wq = part("wq", [P, CH, C])
        tn2 = part("tn2", [P, 2, CH, HALF], F32R)
        t2 = part("t2", [P, CH, L])
        wf = part("wf", [P, 2, CH, C], F32R)
        a_hi = part("a_hi", [P, CH, C], F32R)
        sq = part("sq", [P, CH, HALF])
        resid = part("resid", [P, 2, HALF])
        ctx_sb = part("ctx_sb", [P, PAIRS, P])
        late_res = [w[:, 2 * i:2 * i + 2, :].rearrange("p a n -> p (a n)") for w in (wo, wq) for i in range(2)]
        matrix = {"A": {HI: a_hi, LO: a_lo}, "WF": {HI: wf[:, HI, :, :], LO: wf[:, LO, :, :]}}

        tile_ps = [ctx.enter_context(nc.psum_tensor(f"tile{i}", [P, HALF], F32)) for i in range(3)]
        kt_ps = [ctx.enter_context(nc.psum_tensor(f"kt_ps{i}", [P, HALF], F32)) for i in range(2)]
        ctx_ps = ctx.enter_context(nc.psum_tensor("ctx_ps", [P, PAIRS, P], F32))
        cast_ps = ctx.enter_context(nc.psum_tensor("cast_ps", [P, HALF], F32))
        var_ps = ctx.enter_context(nc.psum_tensor("var_ps", [P, HALF], F32))

        names = SHARED + ("T", "X")
        ready = {k: sem(f"l1_{k}_ready") for k in names}
        evacuated = {k: sem(f"l1_{k}_evacuated") for k in names}
        per = {"K": 8, "V": 8, "Y": 8, "WF": 4, "G": 4, "OB": 1, "A": 4, "O": 8, "T": 8, "X": 8}
        const_loaded, kv_loaded, kv_hi, kv_split = sem("l1_const_loaded"), sem("kv_loaded"), sem("kv_hi"), sem("kv_split")
        const_made, ctx_cleared = sem("l1_const_made"), sem("ctx_cleared")
        projections_loaded, ffn_loaded = sem("projections_loaded"), sem("ffn_loaded")
        xc_loaded = [sem(f"xc_loaded{h}") for h in range(2)]
        resid_loaded = [sem(f"resid_loaded{h}") for h in range(2)]
        stored = [sem(f"out_stored{h}") for h in range(2)]
        pool_chain, total_ready = sem("pool_chain"), sem("total_ready")
        mean_ready, centred, squared, sq_total_ready = sem("mean_ready"), sem("centred"), sem("squared"), sem("sq_total_ready")
        var_ready, eps_added, rstd_ready = sem("var_ready"), sem("eps_added"), sem("rstd_ready")
        diag_ready, cast_ready, normalised = sem("diag_ready"), sem("cast_ready"), sem("normalised")
        hi_done = {n: sem(f"norm{n}_hi_done") for n in (1, 2)}
        lo_done = {n: sem(f"norm{n}_lo_done") for n in (1, 2)}
        matrix_hi_done = {"A": sem("a_mat_hi_done"), "WF": sem("wf_hi_done")}
        k_max_ready, k_exp_done, k_inv_ready, ctx_done = sem("k_max_ready"), sem("k_exp_done"), sem("k_inv_ready"), sem("ctx_done")

        def number(step):
            kind = step[0]
            if kind in ("K", "Y", "O"):
                return CH * step[2] + step[1]
            return 0 if kind == "OB" else step[1]

        def count(step, b):
            return per[step[0]] * (b - 1 if step[0] == "Y" else b) + number(step) + 1

        def job_index(b, job):
            return 4 * b + job - {-1: -2, B: 2}.get(b, 0) if isinstance(b, int) else 4 * b + job

        def norm_of(b, job):
            return (2, b - 1, job) if job in (FFN0, FFN1) else (1, b + 1, job - 2)

        def halves(t, half):
            return t[:, :, half * HALF:(half + 1) * HALF]

        def wait(eng, s, value):
            if not isinstance(value, int) or value > 0:
                eng.wait_ge(s, value)

        def iterations(eng, step):
            def iteration(b):
                for s in STEPS:
                    if step_exists(s, b):
                        step(s, b)
            iteration(0)
            with eng.Fori(1, B - 1) as b:
                iteration(b)
            iteration(B - 1)
            iteration(B)

        def sync(sp):
            def load_t(b, half):
                if not isinstance(b, int) or b > 1:
                    sp.wait_ge(lo_done[2], 2 * (b - 2) + half + 1)
                elif b == 1:
                    sp.wait_ge(lo_done[1], half + 1)
                sp.dma_start(halves(xc, half), t_dram[b].rearrange("(c p) l -> p c l", p=P)[:, :, half * HALF:(half + 1) * HALF])\
                    .then_inc(xc_loaded[half], 16)

            def step(s, b):
                kind = s[0]
                if kind == "SPLIT" and s[1] == FFN0 and not (isinstance(b, int) and b >= B - 1):
                    load_t(b + 1, 0)
                if kind == "SPLIT" and s[1] == FFN1 and not (isinstance(b, int) and b >= B - 1):
                    load_t(b + 1, 1)
                if kind == "O":
                    n = number(s)
                    wait(sp, evacuated["O"], 8 * b + n - 1)
                    sp.dma_start(resid[:, n % 2, :], t_dram[b, s[1] * P:(s[1] + 1) * P, s[2] * HALF:(s[2] + 1) * HALF])\
                        .then_inc(resid_loaded[n % 2], 16)
                if kind == "Y" and s[1] == CH - 1:
                    sp.wait_ge(evacuated["Y"], count(s, b))
                    sp.dma_start(out[b - 1].rearrange("(c p) l -> p c l", p=P)[:, :, s[2] * HALF:(s[2] + 1) * HALF],
                                 halves(t2, s[2])).then_inc(stored[s[2]], 16)

            def loads(what):
                if what == "wv spent":
                    sp.dma_start(ke[:, :, :], w_kv_t.rearrange("(c p) n -> p c n", p=P)).then_inc(kv_loaded, 16)
                else:
                    load_t(0, 0)
                    sp.dma_start(cst[:, :, :], consts).then_inc(const_loaded, 16)
                    sp.dma_start(bias[:, :, :], vectors).then_inc(const_loaded, 16)
                    sp.dma_start(bv_rows[:, :], b_v.partition_broadcast(P)).then_inc(const_loaded, 16)
                    load_t(0, 1)

            def rest():
                sp.dma_start(wo[:, :, :], w_out_t.rearrange("(c p) n -> p c n", p=P)).then_inc(projections_loaded, 16)
                sp.dma_start(wq[:, :, :], w_q.rearrange("(c p) n -> p c n", p=P)).then_inc(projections_loaded, 16)
                load_t(1, 0)
                load_t(1, 1)
                sp.dma_start(w_lora, w_lora_dram.rearrange("(c d) (r h) n -> (d r) c (h n)", d=2, h=2)).then_inc(ffn_loaded, 16)
                sp.dma_start(w_raw, w_ffn_t.rearrange("(c p) n -> p c n", p=P)).then_inc(ffn_loaded, 16)
                iterations(sp, step)
                for h in range(2):
                    sp.wait_ge(stored[h], 16 * B)

            return loads, rest

        w_raw = t2[:, 0:2, :].rearrange("p a (b n) -> p (a b) n", b=2)
        w_lora = t2[:, 2:4, :].rearrange("p a (b n) -> p (a b) n", b=2)

        def tensor(pe):
            def split_product(out_ap, stationary, moving):
                for c in range(CH):
                    for n, (a, m) in enumerate(SPLITS):
                        mm = pe.matmul(out_ap, stationary(a, c), moving(m, c), start=(c == 0 and n == 0),
                                       stop=(c == CH - 1 and n == len(SPLITS) - 1))
                return mm

            def shared_tile(s, b):
                kind = s[0]
                bank = TILES1.index(s) % 3
                ps = tile_ps[bank]
                before = bank1_user_before(s, b)
                if not before:
                    pe.wait_ge(spent["H"], 8 * (B - 1) + 5 + bank)
                else:
                    wait(pe, evacuated[before[0][0]], count(*before))
                if kind == "K":
                    d, half = s[1], s[2]
                    pe.wait_ge(lo_done[1], 2 * b + half + 1)
                    mm = split_product(ps[:, :], lambda a, c: wkv[:, a, c, d * P:(d + 1) * P],
                                       lambda m, c: tn1[:, m, c, half * HALF:(half + 1) * HALF])
                elif kind == "V":
                    mm = split_product(ps[:, :], lambda a, c: tn1[:, a, c, s[1] * P:(s[1] + 1) * P],
                                       lambda m, c: wkv[:, m, c, C:])
                elif kind == "Y":
                    pe.wait_ge(lo_done[2], 2 * (b - 1) + s[2] + 1)
                    mm = split_product(ps[:, :], lambda a, c: wf[:, a, c, s[1] * P:(s[1] + 1) * P],
                                       lambda m, c: tn2[:, m, c, :])
                elif kind == "WF":
                    pe.wait_ge(ffn_loaded, 32)
                    for m in range(CH):
                        mm = pe.matmul(ps[:, :], w_lora[:, m, s[1] * P:(s[1] + 1) * P], w_raw[:, m, :],
                                       start=(m == 0), stop=(m == CH - 1))
                elif kind == "G":
                    pe.wait_ge(ctx_done, b + 1)
                    if isinstance(b, int) and b == 0 and s[1] == 0:
                        pe.wait_ge(projections_loaded, 32)
                    mm = pe.matmul(ps[:, :], ctx_sb[:, s[1], :], wo[:, s[1], :], start=True, stop=True)
                elif kind == "OB":
                    pe.wait_ge(evacuated["G"], 4 * b + 4)
                    for o in range(CH):
                        for d in range(CH):
                            mm = pe.matmul(ps[:, o:o + 1], g_sb[:, d, o * P:(o + 1) * P], bias[:, BQ, d:d + 1],
                                           start=(d == 0), stop=(d == CH - 1))
                elif kind == "A":
                    pe.wait_ge(evacuated["G"], 4 * b + 4)
                    for d in range(CH):
                        mm = pe.matmul(ps[:, :], wq[:, d, s[1] * P:(s[1] + 1) * P], g_sb[:, d, :],
                                       start=(d == 0), stop=(d == CH - 1))
                else:
                    pe.wait_ge(evacuated["A"], 4 * b + 4)
                    mm = split_product(ps[:, :], lambda a, c: matrix["A"][a][:, c, s[1] * P:(s[1] + 1) * P],
                                       lambda m, c: tn1[:, m, c, s[2] * HALF:(s[2] + 1) * HALF])
                mm.then_inc(ready[kind], 1)

            def step(s, b):
                kind = s[0]
                if kind in SHARED:
                    shared_tile(s, b)
                elif kind == "T":
                    n = s[1]
                    if n == 0:
                        pe.wait_ge(k_exp_done, CH * b + CH)
                        if isinstance(b, int) and b == 0:
                            pe.wait_ge(spent["H"], 8 * B)
                    wait(pe, evacuated["T"], 8 * b + n - 1)
                    for d in range(CH):
                        mm = pe.transpose(kt_ps[n % 2][:, d * P:(d + 1) * P], ke[:, d, n * P:(n + 1) * P], cst[:, IDENT, :])
                    mm.then_inc(ready["T"], 1)
                elif kind == "X":
                    n = s[1]
                    pe.wait_ge(evacuated["V"], 8 * b + n + 1)
                    pe.wait_ge(evacuated["T"], 8 * b + n + 1)
                    if n == 0:
                        wait(pe, ctx_done, b)
                    for p in range(PAIRS):
                        mm = pe.matmul(ctx_ps[:, p, :], v_sb[:, n % 2, p * P:(p + 1) * P], kt_sb[:, n % 2, p * P:(p + 1) * P],
                                       start=(n == 0 and p == 0), stop=(n == 7), skip_group_check=True)
                    mm.then_inc(ready["X"], 1)
                elif kind == "MEAN":
                    j = job_index(b, s[1])
                    pe.wait_ge(total_ready, j + 1)
                    if isinstance(j, int) and j == 0:
                        pe.wait_ge(const_loaded, 16 * 3)
                        pe.wait_ge(*spent["QK read"])
                    wait(pe, normalised, j)
                    pe.matmul(cast_ps[:, :], cst[:, MEAN_OF, :], total[:, :], start=True, stop=True).then_inc(mean_ready, 1)
                elif kind == "VAR":
                    j = job_index(b, s[1])
                    pe.wait_ge(sq_total_ready, j + 1)
                    wait(pe, eps_added, j)
                    for n in range(4):
                        mm = pe.matmul(var_ps[:, n:n + 1], total[:, n * P:(n + 1) * P], cst[:, MEAN_OF, 0:1],
                                       start=True, stop=True)
                    mm.then_inc(var_ready, 1)
                elif kind == "CAST":
                    j = job_index(b, s[1])
                    pe.wait_ge(diag_ready, j + 1)
                    pe.matmul(cast_ps[:, :], cst[:, ONES, :], diag[:, :, :].rearrange("p a n -> p (a n)"),
                              start=True, stop=True).then_inc(cast_ready, 1)

            def rest():
                pe.wait_ge(kv_split, CH)
                iterations(pe, step)

            return step, rest

        def scalar(act):
            def step(s, b):
                kind = s[0]
                ps = tile_ps[TILES1.index(s) % 3] if kind in SHARED else None
                if kind == "KV":
                    if s[1] == 0:
                        act.wait_ge(kv_loaded, 16)
                        act.wait_ge(*spent["QK"])
                    nc.scalar.activation(wkv[:, HI, s[1], :], ke[:, s[1], :], ACT.Copy).then_inc(kv_hi, 1)
                elif kind == "K":
                    d, half = s[1], s[2]
                    act.wait_ge(ready["K"], count(s, b))
                    wait(act, ready["A"], 4 * b)
                    nc.scalar.activation(ke[:, d, half * HALF:(half + 1) * HALF], ps[:, :], ACT.Identity,
                                         bias=bias[:, BK, d:d + 1]).then_inc(evacuated["K"], 1)
                elif kind == "E":
                    d = s[1]
                    act.wait_ge(k_max_ready, CH * b + d + 1)
                    nc.scalar.activation(ke[:, d, :], ke[:, d, :], ACT.Exp, bias=k_neg_max[:, d:d + 1],
                                         accum_out=k_sum[:, d:d + 1]).then_inc(k_exp_done, 1)
                elif kind == "T":
                    act.wait_ge(ready["T"], count(s, b))
                    wait(act, ready["X"], 8 * b + s[1] - 1)
                    nc.scalar.activation(kt_sb[:, s[1] % 2, :], kt_ps[s[1] % 2][:, :], ACT.Copy).then_inc(evacuated["T"], 1)
                elif kind == "G":
                    act.wait_ge(ready["G"], count(s, b))
                    act.wait_ge(k_inv_ready, b + 1)
                    nc.scalar.activation(g_sb[:, s[1], :], ps[:, :], ACT.Copy, scale=k_inv[:, s[1]:s[1] + 1])\
                        .then_inc(evacuated["G"], 1)
                elif kind in ("A", "WF"):
                    act.wait_ge(ready[kind], count(s, b))
                    if kind == "A":
                        wait(act, ready["O"], 8 * b)
                    nc.scalar.activation(matrix[kind][HI][:, s[1], :], ps[:, :], ACT.Copy).then_inc(matrix_hi_done[kind], 1)
                elif kind == "MEAN":
                    j = job_index(b, s[1])
                    n, bb, half = norm_of(b, s[1])
                    act.wait_ge(centred, j + 1)
                    wait(act, sq_total_ready, j)
                    nc.scalar.activation(sq[:, :, :], halves(xc, half), ACT.Square).then_inc(squared, 1)
                elif kind == "SPLIT":
                    n, bb, half = norm_of(b, s[1])
                    act.wait_ge(normalised, job_index(b, s[1]) + 1)
                    if n == 1:
                        if isinstance(bb, int) and bb == 0 and half == 0:
                            act.wait_ge(*spent["scores"])
                        wait(act, ready["O"], 8 * (bb - 1) + 4 * (half + 1) if not isinstance(bb, int) or bb > 0 else 0)
                        dst = halves(tn1[:, HI, :, :], half)
                    else:
                        if half == 1:
                            act.wait_ge(ready["Y"], 8 * bb + 4)
                        dst = tn2[:, HI, :, :]
                    nc.scalar.activation(dst, halves(xc, half), ACT.Copy).then_inc(hi_done[n], 1)

            def rest():
                iterations(act, step)

            return step, rest

        def vector(dve):
            def step(s, b):
                kind = s[0]
                ps = tile_ps[TILES1.index(s) % 3] if kind in SHARED else None
                if kind == "INIT":
                    dve.wait_ge(*spent["QK"])
                    nc.vector.memset(neg_half[:, :], -0.5).then_inc(const_made, 1)
                elif kind == "KV":
                    dve.wait_ge(kv_hi, s[1] + 1)
                    nc.vector.tensor_tensor(wkv[:, LO, s[1], :], ke[:, s[1], :], wkv[:, HI, s[1], :].bitcast(F32),
                                            ALU.subtract).then_inc(kv_split, 1)
                elif kind == "E":
                    d = s[1]
                    dve.wait_ge(evacuated["K"], 8 * b + 4 + d + 1)
                    nc.vector.tensor_reduce(k_neg_max[:, d:d + 1], ke[:, d, :], AX_X, ALU.max, negate=True)\
                        .then_inc(k_max_ready, 1)
                elif kind == "V":
                    n = s[1]
                    dve.wait_ge(ready["V"], count(s, b))
                    wait(dve, ready["X"], 8 * b + n - 1)
                    nc.vector.tensor_tensor(v_sb[:, n % 2, :], ps[:, :], bv_rows[:, :], ALU.add).then_inc(evacuated["V"], 1)
                elif kind == "X" and s[1] == 7:
                    dve.wait_ge(k_exp_done, CH * (b + 1))
                    nc.vector.reciprocal(k_inv[:, :], k_sum[:, :]).then_inc(k_inv_ready, 1)
                    dve.wait_ge(ready["X"], 8 * (b + 1))
                    for h in range(2):
                        rows = slice(64 * h, 64 * h + 64)
                        ins = nc.vector.tensor_copy(ctx_sb[rows, :, rows], ctx_ps[rows, :, rows])
                    ins.then_inc(ctx_done, 1)
                elif kind == "OB":
                    dve.wait_ge(ready["OB"], count(s, b))
                    nc.vector.tensor_tensor(ob[:, :], ps[:, 0:CH], bias[:, BO, :], ALU.add).then_inc(evacuated["OB"], 1)
                elif kind in ("A", "WF"):
                    dve.wait_ge(matrix_hi_done[kind], count(s, b))
                    hi, lo = matrix[kind][HI], matrix[kind][LO]
                    nc.vector.tensor_tensor(lo[:, s[1], :], ps[:, :], hi[:, s[1], :].bitcast(F32), ALU.subtract)\
                        .then_inc(evacuated[kind], 1)
                elif kind == "O":
                    o, half, n = s[1], s[2], number(s)
                    dve.wait_ge(ready["O"], count(s, b))
                    dve.wait_ge(evacuated["OB"], b + 1)
                    dve.wait_ge(resid_loaded[n % 2], 16 * (4 * b + n // 2 + 1))
                    if o == 0:
                        wait(dve, stored[half], 16 * b)
                    nc.vector.scalar_tensor_tensor(out=t2[:, o, half * HALF:(half + 1) * HALF], in0=ps[:, :],
                                                   scalar=ob[:, o:o + 1], in1=resid[:, n % 2, :],
                                                   op0=ALU.add, op1=ALU.add).then_inc(evacuated["O"], 1)
                elif kind == "Y":
                    o, half = s[1], s[2]
                    dve.wait_ge(ready["Y"], count(s, b))
                    dst = t2[:, o, half * HALF:(half + 1) * HALF]
                    nc.vector.tensor_tensor(dst, ps[:, :], dst, ALU.add).then_inc(evacuated["Y"], 1)
                elif kind == "MEAN":
                    j = job_index(b, s[1])
                    n, bb, half = norm_of(b, s[1])
                    dve.wait_ge(mean_ready, j + 1)
                    src = halves(t2 if n == 2 else xc, half)
                    nc.vector.tensor_tensor(halves(xc, half), src, cast_ps[:, :].unsqueeze(1).to_broadcast([P, CH, HALF]),
                                            ALU.subtract).then_inc(centred, 1)
                elif kind == "VAR":
                    j = job_index(b, s[1])
                    dve.wait_ge(var_ready, j + 1)
                    nc.vector.tensor_scalar(var_eps[:, :], var_ps[:, 0:4], LN_EPS, None, ALU.add).then_inc(eps_added, 1)
                    dve.wait_ge(rstd_ready, j + 1)
                    wait(dve, cast_ready, j)
                    nc.vector.tensor_tensor(diag[:, :, :], cst[:, IDENT, :].unsqueeze(1).to_broadcast([P, 4, P]),
                                            rstd[:, :].unsqueeze(2).to_broadcast([P, 4, P]), ALU.mult).then_inc(diag_ready, 1)
                elif kind == "CAST":
                    j = job_index(b, s[1])
                    half = norm_of(b, s[1])[2]
                    dve.wait_ge(cast_ready, j + 1)
                    nc.vector.tensor_tensor(halves(xc, half), halves(xc, half),
                                            cast_ps[:, :].unsqueeze(1).to_broadcast([P, CH, HALF]), ALU.mult)\
                        .then_inc(normalised, 1)
                elif kind == "SPLIT":
                    n, bb, half = norm_of(b, s[1])
                    dve.wait_ge(hi_done[n], 2 * bb + half + 1)
                    if isinstance(bb, int) and n == 1 and bb == 0 and half == 0:
                        dve.wait_ge(*spent["v"])
                    if n == 1:
                        hi, dst = halves(tn1[:, HI, :, :], half), halves(tn1[:, LO, :, :], half)
                    else:
                        hi, dst = tn2[:, HI, :, :], tn2[:, LO, :, :]
                    nc.vector.tensor_tensor(dst, halves(xc, half), hi.bitcast(F32), ALU.subtract).then_inc(lo_done[n], 1)

            def rest():
                dve.wait_ge(*spent["nf4"])
                nc.vector.memset(ctx_sb[:, :, :], 0.0).then_inc(ctx_cleared, 1)
                iterations(dve, step)

            return step, rest

        def gpsimd(pool):
            def norm_sum(b, job, part):
                j = job_index(b, job)
                n, bb, half = norm_of(b, job)
                if part == 6:
                    pool.wait_ge(eps_added, j + 1)
                    nc.gpsimd.tensor_tensor(rstd[:, :], var_eps[:, :], neg_half[:, :], ALU.pow).then_inc(rstd_ready, 1)
                    return
                src = sq[:, :, :] if part >= 3 else halves(t2 if n == 2 else xc, half)
                if part == 0:
                    if n == 2:
                        pool.wait_ge(evacuated["O"], 8 * bb + 4 * (half + 1))
                    else:
                        pool.wait_ge(xc_loaded[half], 16 * (bb + 1))
                    wait(pool, var_ready, j)
                elif part == 3:
                    pool.wait_ge(squared, j + 1)
                    pool.wait_ge(mean_ready, j + 1)
                else:
                    pool.wait_ge(pool_chain, 4 * j + part - part // 3)
                if part % 3 == 0:
                    ins = nc.gpsimd.tensor_tensor(total[:, :], src[:, 0, :], src[:, 1, :], ALU.add)
                else:
                    ins = nc.gpsimd.tensor_tensor(total[:, :], total[:, :], src[:, part % 3 + 1, :], ALU.add)
                ins.then_inc({2: total_ready, 5: sq_total_ready}.get(part, pool_chain), 1)

            def step(s, b):
                if s[0] == "INIT":
                    pool.wait_ge(const_made, 1)
                elif s[0] == "SUM":
                    norm_sum(b, s[1], s[2])
                elif s[0] == "MEAN" and not (isinstance(b, int) and b < 0):
                    for part in range(7):
                        norm_sum(b, s[1], part)

            def rest():
                iterations(pool, step)

            return step, rest

    return {"sync": sync, "tensor": tensor, "scalar": scalar, "vector": vector, "gpsimd": gpsimd}, late_res


def program(nc, x, w_qk_t, w_v_t, w_proj_t, b_v0, vectors0, group_mean,
            w_kv_t, w_q, w_out_t, w_ffn_t, qidx, scales, b_v1, vectors1, consts, t_dram, w_lora_dram, out):
    with ExitStack() as ctx:
        def sem(name):
            return ctx.enter_context(nc.semaphore(name))

        first, spent = layer0(nc, sem, x, w_qk_t, w_v_t, w_proj_t, b_v0, vectors0, group_mean, qidx, scales, t_dram, w_lora_dram)
        second, late_res = layer1(nc, sem, spent, t_dram, w_kv_t, w_q, w_out_t, w_ffn_t, w_lora_dram, b_v1, vectors1, consts, out)
        block = ctx.enter_context(nc.Block())

        @block.sync
        def _(sp):
            loads1, rest1 = second["sync"](sp)
            first["sync"](sp, loads1, late_res)
            rest1()

        @block.tensor
        def _(pe):
            step1, rest1 = second["tensor"](pe)
            first["tensor"](pe, step1)
            rest1()

        @block.scalar
        def _(act):
            step1, rest1 = second["scalar"](act)
            first["scalar"](act, step1)
            rest1()

        @block.vector
        def _(dve):
            step1, rest1 = second["vector"](dve)
            first["vector"](dve, step1, late_res)
            rest1()

        @block.gpsimd
        def _(pool):
            step1, rest1 = second["gpsimd"](pool)
            first["gpsimd"](pool, step1)
            rest1()


def kernel(**inputs):
    import concourse.bacc as bacc
    from concourse.bass_utils import run_bass_kernel_spmd

    def columns(*vs):
        return np.ascontiguousarray(np.stack([v.reshape(CH, P).T for v in vs], axis=1))

    a = {k: np.asarray(v) for k, v in inputs.items()}
    w0 = a["L0_conv_w_qkv"].reshape(HEADS, 3, HD, C)
    b0 = a["L0_conv_b_qkv"].reshape(HEADS, 3, HD)
    wq0, wk0, wv0 = (w0[:, i].reshape(C, C) for i in range(3))
    bq0, bk0, bv0 = (b0[:, i].reshape(C) for i in range(3))
    w1, b1 = a["L1_attn_W_qkv"], a["L1_attn_b_qkv"]
    same_group = np.arange(P)[:, None] // (C // GROUPS) == np.arange(P)[None, :] // (C // GROUPS)
    arrays = {
        "x": a["x"].reshape(B, C, L),
        "w_qk_t": np.concatenate([wq0.T, wk0.T], axis=1),
        "w_v_t": wv0.T,
        "w_proj_t": a["L0_conv_w_proj"].T,
        "b_v0": bv0,
        "vectors0": columns(bq0, bk0, a["L0_conv_b_proj"], a["L0_conv_gn_w"], a["L0_conv_gn_b"]),
        "group_mean": np.where(same_group, np.float32(GROUPS / C), np.float32(0)),
        "w_kv_t": w1[C:].T,
        "w_q": w1[:C],
        "w_out_t": a["L1_attn_W_out"].T,
        "w_ffn_t": a["L1_ffn_W"].T,
        "qidx": a["L1_ffn_qidx"].reshape(B, P, NF4_W),
        "scales": a["L1_ffn_scales"].reshape(B, P, NF4_W // 64),
        "b_v1": b1[2 * C:],
        "vectors1": columns(b1[:C], b1[C:2 * C], a["L1_attn_b_out"]),
        "consts": np.ascontiguousarray(np.stack(
            [np.full((P, P), 1 / C, np.float32), np.ones((P, P), np.float32), np.eye(P, dtype=np.float32)], axis=1)),
    }
    arrays = {f"in_{k}": np.ascontiguousarray(v) for k, v in arrays.items()}

    nc = bacc.Bacc("TRN2", target_bir_lowering=False, num_devices=1)
    args = [nc.dram_tensor(k, v.shape, mybir.dt.from_np(v.dtype), kind="ExternalInput").ap() for k, v in arrays.items()]
    args.append(nc.dram_tensor("t_between", (B, C, L), F32).ap())
    args.append(nc.dram_tensor("w_lora", (B, P, NF4_W), F32).ap())
    args.append(nc.dram_tensor("out_0", (B, C, L), F32, kind="ExternalOutput").ap())
    program(nc, *args)
    r = run_bass_kernel_spmd(nc, [arrays], core_ids=[0])
    return r.results[0]["out_0"].reshape(B, C, 32, 32)
```

```python
from contextlib import ExitStack

import concourse.bass as bass
import numpy as np
from concourse import mybir

F32 = mybir.dt.float32
F32R = mybir.dt.float32r
I32 = mybir.dt.int32
ALU = mybir.AluOpType
ACT = mybir.ActivationFunctionType
AX_X = mybir.AxisListType.X

P = 128
B, C, L = 8, 512, 1024
CH = C // P
HEADS = 8
HD = C // HEADS
PAIRS = HEADS // 2
HALF = 512
SC = L // P
UNITS = PAIRS * SC
NF4_W = C * C // B // P
GROUPS = 32
GN_EPS = 1e-5
LN_EPS = 1e-5
HI, LO = 0, 1
SPLITS = ((HI, HI), (HI, LO), (LO, HI))
NF4 = (-1.0, -0.6961928009986877, -0.5250730514526367, -0.39491748809814453, -0.28444138169288635,
       -0.18477343022833334, -0.09105003625154495, 0.0, 0.07958029955625534, 0.16093020141124725,
       0.24611230194568634, 0.33791524171829224, 0.44070982933044434, 0.5626170039176941,
       0.7229568362236023, 1.0)

QK_ORDER = [("Q", 0, 0), ("K", 0, 0), ("Q", 0, 1), ("K", 0, 1), ("K", 1, 0), ("Q", 1, 0), ("Q", 1, 1), ("K", 1, 1),
            ("Q", 2, 0), ("K", 2, 0), ("Q", 2, 1), ("K", 2, 1), ("Q", 3, 0), ("K", 3, 0), ("Q", 3, 1), ("K", 3, 1)]


def QK(kind, pair, half, rel=0):
    return ("QK", rel, QK_ORDER.index((kind, pair, half)))


def V(s, rel=0):
    return ("V", rel, s)


def H(j):
    return ("H", -1, j)


WHOLE = (0, 1)
FILL = {
    0: [(QK("K", 0, 1), WHOLE), (V(3), WHOLE)],
    1: [(V(4), WHOLE), (V(5), WHOLE)],
    2: [(V(6), WHOLE), (H(0), WHOLE)],
    3: [(V(7), WHOLE), (H(1), WHOLE)],
    4: [(QK("K", 1, 0), WHOLE), (H(2), WHOLE)],
    5: [(QK("Q", 1, 0), WHOLE), (H(3), WHOLE)],
    6: [(QK("Q", 1, 1), WHOLE), (H(4), WHOLE), (H(5), WHOLE)],
    7: [(H(6), WHOLE), (H(7), WHOLE)],
    8: [(QK("K", 1, 1), WHOLE)],
    27: [(QK("Q", 0, 0, 1), (0,))],
    28: [(QK("K", 0, 0, 1), (0,))],
    29: [(QK("Q", 0, 0, 1), (1,)), (QK("K", 0, 0, 1), (1,))],
    30: [(QK("Q", 0, 1, 1), WHOLE), (V(0, 1), WHOLE)],
    31: [(V(1, 1), WHOLE), (V(2, 1), WHOLE)],
}
for _n, _tile in enumerate([QK("Q", 2, 0), QK("K", 2, 0), QK("Q", 2, 1), QK("K", 2, 1),
                            QK("Q", 3, 0), QK("K", 3, 0), QK("Q", 3, 1), QK("K", 3, 1)]):
    FILL[9 + 2 * _n] = [(_tile, (0,))]
    FILL[10 + 2 * _n] = [(_tile, (1,))]
G1, G2 = ("G", 1, 0), ("G", 1, 1)
FILL[18].append((G1, WHOLE))
FILL[20].append((G2, WHOLE))
TILES = [t for k in range(UNITS) for t, parts in FILL.get(k, []) if 1 in parts]
FULL_TILES = [t for t in TILES if t[0] != "G"]
NEXT_QKV = [t for t in FULL_TILES if t[1] == 1]


def deferred(k):
    return k % SC < SC - 1 and sum(t[0] != "G" for t, _ in FILL.get(k, [])) == 1 and 1 in FILL[k][0][1]


GN_STATS = {9: 0, 11: 1, 13: 2, 15: 3}
GN_AGGREGATE, GN_POWER, GN_AFFINE = 16, 21, 22
GN_SCALE = {22: (0,), 23: (1,), 26: (2,), 27: (3,)}
GN_HI = {24: (0,), 25: (1,), 26: (2,), 27: (3,)}
GN_LO = {25: (0,), 26: (1,), 27: (2,), 28: (3,)}


def exists(tile, b):
    if not isinstance(b, int):
        return True
    return {-1: tile[1] == 1, 0: tile[1] != -1, B - 1: tile[1] != 1, B: tile[1] == -1}.get(b, True)


def bank_of(tile, b):
    if isinstance(b, int) and b == 0 and tile in (V(7), QK("Q", 1, 0)):
        return 1 - FULL_TILES.index(tile) % 2
    if tile[0] != "G":
        return FULL_TILES.index(tile) % 2
    (k,) = [k for k in FILL if (tile, WHOLE) in FILL[k]]
    return 1 - bank_of(FILL[k][0][0], b)


def bank_user_before(tile, b):
    n = TILES.index(tile)
    for m in range(n - 1, n - 2 * len(TILES), -1):
        prev, prev_b = TILES[m % len(TILES)], b + m // len(TILES)
        if bank_of(prev, prev_b) != bank_of(tile, b):
            continue
        if isinstance(prev_b, int) and prev_b < -1:
            return None
        if exists(prev, prev_b):
            return prev, prev_b + prev[1]
    return None


assert len(FULL_TILES) % 2 == 0

FFN0, FFN1, NEXT0, NEXT1 = range(4)
BESIDE_LAST_BATCH = {
    25: [("INIT",), ("KV", 0), ("KV", 1)],
    26: [("KV", 2), ("SUM", NEXT0, 0)],
    27: [("KV", 3), ("SUM", NEXT0, 1), ("SUM", NEXT0, 2)],
    28: [("MEAN", NEXT0)],
    29: [("SUM", NEXT0, 3), ("SUM", NEXT0, 4)],
    30: [("SUM", NEXT0, 5)],
}
BESIDE_LAST_PROJECTION = {
    0: [("VAR", NEXT0), ("DIAG", NEXT0), ("SUM", NEXT0, 6)] + [("SUM", NEXT1, i) for i in range(3)],
    1: [("CAST", NEXT0)],
    2: [("MEAN", NEXT1), ("SPLIT", NEXT0)],
    3: [("SUM", NEXT1, i) for i in range(3, 7)],
    5: [("VAR", NEXT1), ("DIAG", NEXT1)],
    6: [("CAST", NEXT1), ("SPLIT", NEXT1)],
}


def layer0(nc, sem, x, w_qk_t, w_v_t, w_proj_t, b_v, vectors, group_mean, qidx, scales, t_dram, w_lora_dram):
    ctx = ExitStack()

    def sb(name, shape, dt=F32):
        return ctx.enter_context(nc.sbuf_tensor(name, shape, dt))

    with ctx:
        wv = sb("wv", [P, 2, CH, C], F32R)
        wqk = sb("wqk", [P, 2, CH, 2 * C], F32R)
        xn = sb("xn", [P, 2, CH, L], F32R)
        kk = sb("kk", [P, 2, 2, L], F32R)
        v_sb = sb("v_sb", [P, SC, C])
        probs = sb("probs", [P, 2, 2, L])
        qq = sb("qq", [P, 2, 2, L], F32R)
        wp = sb("wp", [P, 2, CH, C], F32R)
        a_sb = sb("a_sb", [P, 2, CH, L], F32R)
        x_ring = sb("x_ring", [P, 2, L])
        vs = sb("vs", [P, 2, 2 * HD])
        nf4_q = sb("nf4_q", [P, NF4_W], I32)
        nf4_w = sb("nf4_w", [P, NF4_W])
        nf4_pick = sb("nf4_pick", [P, NF4_W])
        nf4_scale = sb("nf4_scale", [P, NF4_W // 64])
        bv_rows = sb("bv_rows", [P, C])
        bias = sb("bias", [P, 5, CH])
        BQ, BK, BP, GW, GB = range(5)
        bq_scaled = sb("bq_scaled", [P, CH])
        gmat = sb("gmat", [P, P])
        neg_half = sb("neg_half", [P, CH])
        neg_max = sb("neg_max", [P, 2, 2])
        row_sum = sb("row_sum", [P, 2, 2])
        inv_sum = sb("inv_sum", [P, 2, 2])
        st = sb("st", [P, CH, 2, 6])
        mv = sb("mv", [P, CH, 2])
        g_mean = sb("g_mean", [P, CH])
        dev = sb("dev", [P, CH])
        dev2 = sb("dev2", [P, CH])
        spread = sb("spread", [P, CH])
        var_eps = sb("var_eps", [P, CH])
        rstd = sb("rstd", [P, CH])
        g_scale = sb("g_scale", [P, CH])
        g_tmp = sb("g_tmp", [P, CH])
        g_shift = sb("g_shift", [P, CH])
        x0 = v_sb[:, :, :].rearrange("p (i h) n -> p i (h n)", i=CH)
        raw_qk = probs[:, :, :, :].rearrange("p a b l -> p (a b l)").rearrange("p (c n) -> p c n", c=CH)
        raw_v = x_ring[:, :, :].rearrange("p a (b n) -> p (a b) n", b=2)
        raw_p = raw_v

        s_ps = [ctx.enter_context(nc.psum_tensor(f"scores{h}", [P, L], F32)) for h in range(2)]
        pv_ps = ctx.enter_context(nc.psum_tensor("pv_ps", [P, L], F32))
        fill_ps = [ctx.enter_context(nc.psum_tensor(f"fill{i}", [P, HALF], F32)) for i in range(2)]

        const_loaded, bv_loaded, weights_split = sem("const_loaded"), sem("bv_loaded"), sem("weights_split")
        qk_loaded, wv_loaded, wp_loaded = sem("w_qk_loaded"), sem("w_v_loaded"), sem("w_proj_loaded")
        x0_loaded = [sem(f"x0_loaded{i}") for i in range(CH)]
        weights_hi = sem("weights_hi")
        const_made = sem("const_made")
        stats_loaded = [sem(f"stats_loaded{i}") for i in range(2)]
        norm_loaded = [sem(f"norm_loaded{i}") for i in range(2)]
        res_loaded = [sem(f"res_loaded{i}") for i in range(2)]
        late_loaded = [sem(f"late_res_loaded{i}") for i in range(CH)]
        stats_done, gn_aggregated, gn_chain = sem("stats_done"), sem("gn_aggregated"), sem("gn_chain")
        gn_power_in, gn_power_out, gn_affine = sem("gn_power_in"), sem("gn_power_out"), sem("gn_affine")
        x_scaled, xn_hi_done, xn_done = sem("x_scaled"), sem("xn_hi_done"), sem("xn_done")
        ready = {k: sem(f"{k}_tile_ready") for k in ("QK", "V", "H", "G")}
        evacuated = {k: sem(f"{k}_tile_evacuated") for k in ("QK", "V", "H", "G")}
        qk_hi_done = sem("qk_hi_done")
        k_copied = [sem(f"k_copied{h}") for h in range(2)]
        scores_ready = [sem(f"scores_ready{h}") for h in range(2)]
        max_ready = [sem(f"max_ready{h}") for h in range(2)]
        exp_done = [sem(f"exp_done{h}") for h in range(2)]
        inv_ready, vs_ready, pv_done = sem("inv_ready"), sem("vs_ready"), sem("pv_done")
        a_hi_done, a_done = sem("a_hi_done"), sem("a_done")
        t_stored = [sem(f"t_stored{i}") for i in range(2)]
        nf4_q_loaded, nf4_scale_loaded, nf4_done, nf4_stored = (sem("nf4_q_loaded"), sem("nf4_scale_loaded"), sem("nf4_done"),
                                                                sem("nf4_stored"))

        per_batch = {"QK": 16, "V": 8, "H": 8, "G": 2}

        def count(tile, b):
            return per_batch[tile[0]] * b + tile[2] + 1

        def wait(eng, s, value):
            if not isinstance(value, int) or value > 0:
                eng.wait_ge(s, value)

        def chunk(b, i):
            return x0[:, i, :] if isinstance(b, int) and b == 0 else x_ring[:, i % 2, :]

        def body_loop(eng, body):
            body(0)
            with eng.Fori(1, B - 1) as b:
                body(b)
            body(B - 1)

        def sync(sp, loads, late_res):
            def load_stats(b, i):
                if i >= 2:
                    sp.wait_ge(stats_done, CH * b + i - 1)
                elif isinstance(b, int) and b == 1:
                    sp.wait_ge(weights_split, 4)
                elif not isinstance(b, int) or b > 1:
                    sp.wait_ge(t_stored[i], 32 * (b - 1))
                sp.dma_start(x_ring[:, i % 2, :], x[b, i * P:(i + 1) * P, :]).then_inc(stats_loaded[i % 2], 16)

            def load_norm(b, i):
                if i >= 2:
                    sp.wait_ge(xn_done, CH * b + i - 1)
                else:
                    sp.wait_ge(stats_done, CH * b + i + 3)
                sp.dma_start(x_ring[:, i % 2, :], x[b, i * P:(i + 1) * P, :]).then_inc(norm_loaded[i % 2], 16)

            def load_residual(b, i):
                if i >= 2:
                    sp.wait_ge(t_stored[i % 2], 32 * b + 16)
                else:
                    sp.wait_ge(xn_done, CH * (b + 1) + i + 3)
                sp.dma_start(x_ring[:, i % 2, :], x[b, i * P:(i + 1) * P, :]).then_inc(res_loaded[i % 2], 16)

            def store_t(b, o):
                sp.wait_ge(evacuated["H"], 8 * b + 2 * o + 2)
                src = late_res[o] if isinstance(b, int) and b == B - 1 else x_ring[:, o % 2, :]
                sp.dma_start(t_dram[b, o * P:(o + 1) * P, :], src).then_inc(t_stored[o % 2], 16)

            def load_nf4_indices(b):
                if not isinstance(b, int) or b > 0:
                    sp.wait_ge(nf4_done, 32 * b - 2)
                sp.dma_start(nf4_q[:, :], qidx[b]).then_inc(nf4_q_loaded, 16)

            def load_nf4_scales(b):
                sp.dma_start(nf4_scale[:, :], scales[b]).then_inc(nf4_scale_loaded, 16)

            def store_nf4(b):
                sp.wait_ge(nf4_done, 32 * b + 32)
                sp.dma_start(w_lora_dram[b], nf4_w[:, :]).then_inc(nf4_stored, 16)

            def copy_k(b, pair, half):
                sp.wait_ge(evacuated["QK"], count(QK("K", pair, half), b))
                cols = slice(half * HALF, (half + 1) * HALF)
                sp.dma_start(kk[64:128, 0, :, cols].bitcast(F32), kk[0:64, 0, :, cols].bitcast(F32)).then_inc(k_copied[half], 16)
                sp.dma_start(kk[0:64, 1, :, cols].bitcast(F32), kk[64:128, 1, :, cols].bitcast(F32)).then_inc(k_copied[half], 16)

            sp.dma_start(gmat[:, :], group_mean).then_inc(const_loaded, 16)
            sp.dma_start(bias[:, :, :], vectors).then_inc(const_loaded, 16)
            for i in range(CH):
                sp.dma_start(x0[:, i, :], x[0, i * P:(i + 1) * P, :]).then_inc(x0_loaded[i], 16)
            sp.dma_start(raw_qk, w_qk_t.rearrange("(c p) n -> p c n", p=P)).then_inc(qk_loaded, 16)
            sp.dma_start(raw_v, w_v_t.rearrange("(c p) n -> p c n", p=P)).then_inc(wv_loaded, 16)
            sp.dma_start(bv_rows[:, :], b_v.partition_broadcast(P)).then_inc(bv_loaded, 16)
            sp.wait_ge(weights_split, 3)
            sp.dma_start(raw_p, w_proj_t.rearrange("(c p) n -> p c n", p=P)).then_inc(wp_loaded, 16)
            load_nf4_indices(0)
            load_nf4_scales(0)
            copy_k(0, 0, 0)

            def body(b):
                first, last = isinstance(b, int) and b == 0, isinstance(b, int) and b == B - 1
                copy_k(b, 0, 1)
                if not first:
                    load_residual(b - 1, 0)
                    load_residual(b - 1, 1)
                    store_t(b - 1, 0)
                copy_k(b, 1, 0)
                if not first:
                    load_residual(b - 1, 2)
                    store_t(b - 1, 1)
                    load_residual(b - 1, 3)
                    store_t(b - 1, 2)
                    store_t(b - 1, 3)
                if not last:
                    load_stats(b + 1, 0)
                    load_stats(b + 1, 1)
                copy_k(b, 1, 1)
                if not last:
                    load_stats(b + 1, 2)
                    load_stats(b + 1, 3)
                else:
                    sp.wait_ge(ready["V"], 8 * B)
                    loads("wv spent")
                copy_k(b, 2, 0)
                copy_k(b, 2, 1)
                if not last:
                    load_norm(b + 1, 0)
                    load_norm(b + 1, 1)
                copy_k(b, 3, 0)
                copy_k(b, 3, 1)
                if not last:
                    load_norm(b + 1, 2)
                    load_norm(b + 1, 3)
                    copy_k(b + 1, 0, 0)
                    load_nf4_indices(b + 1)
                    store_nf4(b)
                    load_nf4_scales(b + 1)
                else:
                    for i in range(2):
                        sp.wait_ge(t_stored[i], 32 * b)
                    loads("wqk, xn and x_ring spent")
                    for o in range(CH):
                        if o == 2:
                            sp.wait_ge(scores_ready[1], UNITS * b + 3 * SC)
                        sp.dma_start(late_res[o], x[b, o * P:(o + 1) * P, :]).then_inc(late_loaded[o], 16)
                    store_nf4(b)

            body_loop(sp, body)
            for o in range(CH):
                store_t(B - 1, o)
            for i in range(2):
                sp.wait_ge(t_stored[i], 32 * B)
            sp.wait_ge(nf4_stored, 16 * B)

        def tensor(pe, step1):
            def split_product(out, stationary, moving, parts, before_last_chunk=None):
                steps = [(c, a, m) for c in range(CH) for a, m in SPLITS]
                cut = len(steps) // 2
                for part in parts:
                    for k in range(part * cut, (part + 1) * cut):
                        c, a, m = steps[k]
                        if k == len(steps) - len(SPLITS) and before_last_chunk:
                            before_last_chunk()
                        mm = pe.matmul(out, stationary(a, c), moving(m, c), start=(k == 0), stop=(k == len(steps) - 1))
                return mm

            def tile(t, b, parts):
                kind, rel, n = t
                if isinstance(b, int) and b == B:
                    out = s_ps[n // 2 % 2][:, n % 2 * HALF:(n % 2 + 1) * HALF]
                    if n >= 4:
                        pe.wait_ge(evacuated["H"], 8 * (B - 1) + n - 3)
                    elif n % 2 == 0:
                        pe.wait_ge(exp_done[n // 2], UNITS * B)
                else:
                    out = fill_ps[bank_of(t, b)]
                if 0 in parts:
                    before = bank_user_before(t, b) if not isinstance(b, int) or b < B else None
                    if before:
                        wait(pe, evacuated[before[0][0]], count(*before))
                if kind in ("QK", "V") and rel == 1:
                    for part in parts:
                        if part == 0:
                            pe.wait_ge(xn_done, CH * (b + 2) - (CH // 2 if parts == (0,) else 0))
                        elif parts == (1,):
                            pe.wait_ge(xn_done, CH * (b + 2))
                if 0 in parts:
                    if kind == "H" and n == 0:
                        pe.wait_ge(a_done, 2 * (PAIRS * b - 1))
                if kind == "QK":
                    which, pair, half = QK_ORDER[n]
                    col = (pair if which == "Q" else PAIRS + pair) * P
                    mm = split_product(out[:, :], lambda a, c: wqk[:, a, c, col:col + P],
                                       lambda m, c: xn[:, m, c, half * HALF:(half + 1) * HALF], parts)
                elif kind == "V":
                    mm = split_product(out[:, :], lambda a, c: xn[:, a, c, n * P:(n + 1) * P],
                                       lambda m, c: wv[:, m, c, :], parts)
                elif kind == "H":
                    o, half = n // 2, n % 2
                    mm = split_product(out[:, :], lambda a, c: wp[:, a, c, o * P:(o + 1) * P],
                                       lambda m, c: a_sb[:, m, c, half * HALF:(half + 1) * HALF], parts,
                                       (lambda: pe.wait_ge(a_done, 2 * PAIRS * b)) if n == 0 else None)
                else:
                    pe.wait_ge(gn_aggregated, 2 * (b + 1) + n + 1)
                    mm = pe.matmul(out[:, 0:CH], gmat[:, :], mv[:, :, 0] if n == 0 else spread[:, :],
                                   start=True, stop=True)
                if 1 in parts:
                    mm.then_inc(ready[kind], 1)

            def scores(b, k, h):
                pair, s = k // SC, k % SC
                g = UNITS * b + k
                if s == 0 and h == 0:
                    pe.wait_ge(evacuated["QK"], count(QK("Q", pair, 1), b))
                if s % 4 == 0 and h == 0:
                    pe.wait_ge(k_copied[s // 4], 32 * (PAIRS * b + pair + 1))
                wait(pe, exp_done[h], g)
                for half in range(2):
                    for part in (HI, LO):
                        mm = pe.matmul(s_ps[h][:, half * HALF:(half + 1) * HALF],
                                       kk[:, h, part, s * P:(s + 1) * P],
                                       qq[:, pair % 2, h, half * HALF:(half + 1) * HALF],
                                       start=(part == HI), stop=(part == LO))
                mm.then_inc(scores_ready[h], 1)

            def values(b, k):
                s = k % SC
                pe.wait_ge(vs_ready, UNITS * b + k + 1)
                for half in range(2):
                    if s == 0:
                        wait(pe, a_done, 2 * (PAIRS * b + k // SC) - 1 + half)
                    for h in range(2):
                        mm = pe.matmul(pv_ps[64 * h:64 * h + 64, half * HALF:(half + 1) * HALF],
                                       vs[:, k % 2, h * HD:(h + 1) * HD],
                                       probs[:, k % 2, h, half * HALF:(half + 1) * HALF],
                                       start=(s == 0), stop=(s == SC - 1))
                mm.then_inc(pv_done, 1)

            pe.wait_ge(const_loaded, 16 * 2)
            tile(G1, -1, WHOLE)
            tile(G2, -1, WHOLE)
            for t in NEXT_QKV:
                pe.wait_ge(weights_split, 3 if t[0] == "V" else 1 if QK_ORDER[t[2]][0] == "Q" else 2)
                tile(t, -1, WHOLE)

            def body(b):
                for k in range(UNITS):
                    fill = [(t, parts) for t, parts in FILL.get(k, []) if exists(t, b)]
                    scores(b, k, 0)
                    between = sum(t[0] != "G" for t, _ in fill) == 1
                    for t, parts in fill[:between]:
                        tile(t, b, parts)
                    scores(b, k, 1)
                    if k > 0:
                        values(b, k - 1)
                    elif not isinstance(b, int) or b > 0:
                        values(b - 1, UNITS - 1)
                    for t, parts in fill[between:]:
                        tile(t, b, parts)
                    if isinstance(b, int) and b == B - 1:
                        for s in BESIDE_LAST_BATCH.get(k, ()):
                            step1(s, -1)

            body_loop(pe, body)
            values(B - 1, UNITS - 1)
            for j in range(8):
                tile(H(j), B, WHOLE)
                for s in BESIDE_LAST_PROJECTION.get(j, ()):
                    step1(s, -1)

        def scalar(act, step1):
            def evacuate(t, b):
                kind, rel, n = t
                bb = b + rel
                if kind != "QK":
                    return
                which, pair, half = QK_ORDER[n]
                act.wait_ge(ready["QK"], count(t, bb))
                cols = slice(half * HALF, (half + 1) * HALF)
                ps = fill_ps[bank_of(t, b)]
                if which == "K":
                    wait(act, scores_ready[1], UNITS * bb + SC * (pair - 1) + 4 * (half + 1))
                    dst = [kk[64 * h:64 * h + 64, h, HI, cols] for h in range(2)]
                    add = [bias[64 * h:64 * h + 64, BK, pair:pair + 1] for h in range(2)]
                else:
                    wait(act, scores_ready[1], UNITS * bb + SC * (pair - 1))
                    dst = [qq[64 * h:64 * h + 64, pair % 2, h, cols] for h in range(2)]
                    add = [bq_scaled[64 * h:64 * h + 64, pair:pair + 1] for h in range(2)]
                for h in range(2):
                    ins = nc.scalar.activation(dst[h], ps[64 * h:64 * h + 64, :], ACT.Identity, bias=add[h])
                ins.then_inc(qk_hi_done, 1)

            def exponentials(b, k):
                g = UNITS * b + k
                for h in range(2):
                    act.wait_ge(max_ready[h], g + 1)
                    wait(act, pv_done, g - 1 if not isinstance(g, int) or g > 1 else 0)
                    nc.scalar.activation(probs[:, k % 2, h, :], s_ps[h][:, :], ACT.Exp,
                                         bias=neg_max[:, k % 2, h:h + 1],
                                         accum_out=row_sum[:, k % 2, h:h + 1]).then_inc(exp_done[h], 1)

            def attention_hi(b, pair):
                act.wait_ge(pv_done, UNITS * b + SC * (pair + 1))
                wait(act, ready["H"], 8 * b)
                for half in range(2):
                    cols = slice(half * HALF, (half + 1) * HALF)
                    nc.scalar.activation(a_sb[:, HI, pair, cols], pv_ps[:, cols], ACT.Copy).then_inc(a_hi_done, 1)

            def normalised_hi(b, i):
                act.wait_ge(x_scaled, CH * b + i + 1)
                wait(act, ready["QK"], 16 * b)
                nc.scalar.activation(xn[:, HI, i, :], chunk(b, i), ACT.Copy).then_inc(xn_hi_done, 1)

            act.wait_ge(qk_loaded, 16)
            nc.scalar.activation(wqk[:, HI, :, 0:C], raw_qk[:, :, 0:C], ACT.Copy, scale=0.125).then_inc(weights_hi, 1)
            act.wait_ge(const_made, 2)
            normalised_hi(0, 0)
            normalised_hi(0, 1)
            nc.scalar.activation(wqk[:, HI, :, C:], raw_qk[:, :, C:], ACT.Copy).then_inc(weights_hi, 1)
            normalised_hi(0, 2)
            normalised_hi(0, 3)
            act.wait_ge(wv_loaded, 16)
            nc.scalar.activation(wv[:, HI, :, :], raw_v, ACT.Copy).then_inc(weights_hi, 1)
            for n, t in enumerate(NEXT_QKV):
                evacuate(t, -1)
                if n == 2:
                    act.wait_ge(wp_loaded, 16)
                    nc.scalar.activation(wp[:, HI, :, :], raw_p, ACT.Copy).then_inc(weights_hi, 1)

            def body(b):
                last = isinstance(b, int) and b == B - 1
                for k in range(UNITS):
                    exponentials(b, k)
                    if k % SC == 0 and k > 0:
                        attention_hi(b, k // SC - 1)
                    elif k == 0 and (not isinstance(b, int) or b > 0):
                        attention_hi(b - 1, PAIRS - 1)
                    for t, parts in FILL.get(k, []):
                        if 1 in parts and exists(t, b):
                            evacuate(t, b)
                    if not last:
                        for i in GN_HI.get(k, ()):
                            normalised_hi(b + 1, i)
                    else:
                        for s in BESIDE_LAST_BATCH.get(k, ()):
                            step1(s, -1)

            body_loop(act, body)
            attention_hi(B - 1, PAIRS - 1)
            for j in range(8):
                for s in BESIDE_LAST_PROJECTION.get(j, ()):
                    step1(s, -1)

        def vector(dve, step1, late_res):
            def evacuate(t, b):
                kind, rel, n = t
                bb = b + rel
                late = isinstance(b, int) and b == B
                ps = s_ps[n // 2 % 2][:, n % 2 * HALF:(n % 2 + 1) * HALF] if late else fill_ps[bank_of(t, b)]
                if kind == "QK":
                    which, pair, half = QK_ORDER[n]
                    dve.wait_ge(qk_hi_done, count(t, bb))
                    cols = slice(half * HALF, (half + 1) * HALF)
                    for h in range(2):
                        rows, other = slice(64 * h, 64 * h + 64), slice(64 - 64 * h, 128 - 64 * h)
                        if which == "K":
                            hi, dst, add = kk[rows, h, HI, cols], kk[rows, h, LO, cols], bias[rows, BK, pair:pair + 1]
                        else:
                            hi, dst = qq[rows, pair % 2, h, cols], qq[other, pair % 2, h, cols]
                            add = bq_scaled[rows, pair:pair + 1]
                        ins = nc.vector.scalar_tensor_tensor(out=dst, in0=ps[rows, :], scalar=add, in1=hi.bitcast(F32),
                                                             op0=ALU.add, op1=ALU.subtract)
                    ins.then_inc(evacuated["QK"], 1)
                elif kind == "V":
                    dve.wait_ge(ready["V"], count(t, bb))
                    wait(dve, vs_ready, UNITS * bb - SC + n + 1 if not isinstance(bb, int) or bb > 0 else 0)
                    nc.vector.tensor_tensor(v_sb[:, n, :], ps[:, :], bv_rows[:, :], ALU.add)\
                        .then_inc(evacuated["V"], 1)
                elif kind == "H":
                    o, half = n // 2, n % 2
                    dve.wait_ge(ready["H"], count(t, bb))
                    if late:
                        dve.wait_ge(late_loaded[o], 16)
                    else:
                        dve.wait_ge(res_loaded[o % 2], 32 * bb + 16 * (o // 2 + 1))
                    slot = (late_res[o] if late else x_ring[:, o % 2, :])[:, half * HALF:(half + 1) * HALF]
                    nc.vector.scalar_tensor_tensor(out=slot, in0=ps[:, :], scalar=bias[:, BP, o:o + 1], in1=slot,
                                                   op0=ALU.add, op1=ALU.add).then_inc(evacuated["H"], 1)
                elif n == 0:
                    group_spread(bb)
                else:
                    dve.wait_ge(ready["G"], count(t, bb))
                    nc.vector.tensor_scalar(var_eps[:, :], ps[:, 0:CH], GN_EPS, None, ALU.add)\
                        .then_inc(evacuated["G"], 1)

            def statistics(b, i):
                if isinstance(b, int) and b == 0:
                    dve.wait_ge(x0_loaded[i], 16)
                else:
                    dve.wait_ge(stats_loaded[i % 2], 32 * (b - 1) + 16 * (i // 2 + 1))
                for half in range(2):
                    ins = nc.vector.bn_stats(st[:, i, half, :], chunk(b, i)[:, half * HALF:(half + 1) * HALF])
                ins.then_inc(stats_done, 1)

            def aggregate(b):
                dve.wait_ge(stats_done, CH * (b + 1))
                nc.vector.memset(g_tmp[:, :], 0.0)
                for i in range(CH):
                    ins = nc.vector.bn_aggr(mv[:, i, :], st[:, i, :, :])
                ins.then_inc(gn_aggregated, 1)

            def group_spread(b):
                dve.wait_ge(ready["G"], count(G1, b))
                nc.vector.tensor_copy(g_mean[:, :], fill_ps[bank_of(G1, b)][:, 0:CH]).then_inc(evacuated["G"], 1)
                dve.wait_ge(evacuated["G"], count(G1, b))
                nc.vector.tensor_tensor(dev[:, :], mv[:, :, 0], g_mean[:, :], ALU.subtract).then_inc(gn_chain, 1)
                dve.wait_ge(gn_chain, 2 * b + 1)
                nc.vector.tensor_tensor(dev2[:, :], dev[:, :], dev[:, :], ALU.mult).then_inc(gn_chain, 1)
                dve.wait_ge(gn_chain, 2 * b + 2)
                nc.vector.tensor_tensor(spread[:, :], dev2[:, :], mv[:, :, 1], ALU.add).then_inc(gn_aggregated, 1)

            def affine(b):
                dve.wait_ge(gn_power_out, b + 1)
                nc.vector.tensor_tensor(g_scale[:, :], rstd[:, :], bias[:, GW, :], ALU.mult).then_inc(gn_affine, 1)
                dve.wait_ge(gn_affine, 3 * b + 1)
                nc.vector.tensor_tensor(g_tmp[:, :], g_mean[:, :], g_scale[:, :], ALU.mult).then_inc(gn_affine, 1)
                dve.wait_ge(gn_affine, 3 * b + 2)
                nc.vector.tensor_tensor(g_shift[:, :], bias[:, GB, :], g_tmp[:, :], ALU.subtract).then_inc(gn_affine, 1)

            def scale_x(b, i):
                if not isinstance(b, int) or b > 0:
                    dve.wait_ge(norm_loaded[i % 2], 32 * (b - 1) + 16 * (i // 2 + 1))
                if i == 0:
                    dve.wait_ge(gn_affine, 3 * (b + 1))
                slot = chunk(b, i)
                nc.vector.tensor_scalar(slot, slot, g_scale[:, i:i + 1], g_shift[:, i:i + 1], ALU.mult, ALU.add)\
                    .then_inc(x_scaled, 1)

            def normalised_lo(b, i):
                dve.wait_ge(xn_hi_done, CH * b + i + 1)
                nc.vector.tensor_tensor(xn[:, LO, i, :], chunk(b, i), xn[:, HI, i, :].bitcast(F32),
                                        ALU.subtract).then_inc(xn_done, 1)

            def attention_lo(b, pair):
                for half in range(2):
                    dve.wait_ge(a_hi_done, 2 * (PAIRS * b + pair) + half + 1)
                    cols = slice(half * HALF, (half + 1) * HALF)
                    nc.vector.tensor_tensor(a_sb[:, LO, pair, cols], pv_ps[:, cols], a_sb[:, HI, pair, cols].bitcast(F32),
                                            ALU.subtract).then_inc(a_done, 1)

            def maxima(b, k, h):
                dve.wait_ge(scores_ready[h], UNITS * b + k + 1)
                nc.vector.tensor_reduce(neg_max[:, k % 2, h:h + 1], s_ps[h][:, :], AX_X, ALU.max,
                                        negate=True).then_inc(max_ready[h], 1)

            def inverse_sums(b, k):
                g = UNITS * b + k
                for h in range(2):
                    dve.wait_ge(exp_done[h], g + 1)
                wait(dve, vs_ready, g - 1 if not isinstance(g, int) or g > 1 else 0)
                nc.vector.reciprocal(inv_sum[:, k % 2, :], row_sum[:, k % 2, :]).then_inc(inv_ready, 1)

            nc.vector.memset(neg_half[:, :], -0.5).then_inc(const_made, 1)
            dve.wait_ge(const_loaded, 16 * 2)
            nc.vector.tensor_scalar(bq_scaled[:, :], bias[:, BQ, :], 0.125, None, ALU.mult).then_inc(const_made, 1)
            for i in range(CH):
                statistics(0, i)
            aggregate(0)
            evacuate(G1, -1)
            evacuate(G2, -1)
            affine(0)
            scale_x(0, 0)
            scale_x(0, 1)
            scale_x(0, 2)
            scale_x(0, 3)
            dve.wait_ge(weights_hi, 1)
            nc.vector.scalar_tensor_tensor(out=wqk[:, LO, :, 0:C], in0=raw_qk[:, :, 0:C], scalar=0.125,
                                           in1=wqk[:, HI, :, 0:C].bitcast(F32), op0=ALU.mult, op1=ALU.subtract)\
                .then_inc(weights_split, 1)
            for i in range(CH):
                normalised_lo(0, i)
            dve.wait_ge(weights_hi, 2)
            nc.vector.tensor_tensor(wqk[:, LO, :, C:], raw_qk[:, :, C:], wqk[:, HI, :, C:].bitcast(F32), ALU.subtract)\
                .then_inc(weights_split, 1)
            dve.wait_ge(weights_hi, 3)
            nc.vector.tensor_tensor(wv[:, LO, :, :], raw_v, wv[:, HI, :, :].bitcast(F32), ALU.subtract)\
                .then_inc(weights_split, 1)
            dve.wait_ge(bv_loaded, 16)
            for n, t in enumerate(NEXT_QKV):
                evacuate(t, -1)
                if n == 2:
                    dve.wait_ge(weights_hi, 4)
                    nc.vector.tensor_tensor(wp[:, LO, :, :], raw_p, wp[:, HI, :, :].bitcast(F32), ALU.subtract)\
                        .then_inc(weights_split, 1)

            def body(b):
                last = isinstance(b, int) and b == B - 1
                for k in range(UNITS):
                    maxima(b, k, 0)
                    left = k % SC and deferred(k - 1)
                    if left and k % SC > 1:
                        evacuate(FILL[k - 1][0][0], b)
                    maxima(b, k, 1)
                    if left and k % SC == 1:
                        evacuate(FILL[k - 1][0][0], b)
                    if not last and k in GN_STATS:
                        statistics(b + 1, GN_STATS[k])
                    if not last:
                        if k == GN_AFFINE:
                            affine(b + 1)
                        for i in GN_LO.get(k, ()):
                            normalised_lo(b + 1, i)
                        for i in GN_SCALE.get(k, ()):
                            scale_x(b + 1, i)
                    inverse_sums(b, k)
                    if k % SC == 0 and k > 0:
                        attention_lo(b, k // SC - 1)
                    elif k == 0 and (not isinstance(b, int) or b > 0):
                        attention_lo(b - 1, PAIRS - 1)
                    for t, parts in FILL.get(k, []):
                        if 1 in parts and exists(t, b) and not (deferred(k) and t[0] != "G"):
                            evacuate(t, b)
                    if not last:
                        if k == GN_AGGREGATE:
                            aggregate(b + 1)
                    else:
                        for s in BESIDE_LAST_BATCH.get(k, ()):
                            step1(s, -1)

            body_loop(dve, body)
            attention_lo(B - 1, PAIRS - 1)
            for j in range(8):
                evacuate(H(j), B)
                for s in BESIDE_LAST_PROJECTION.get(j, ()):
                    step1(s, -1)

        def gpsimd(pool, step1):
            def power(b):
                pool.wait_ge(evacuated["G"], 2 * (b + 1))
                nc.gpsimd.tensor_tensor(rstd[:, :], var_eps[:, :], neg_half[:, :], ALU.pow).then_inc(gn_power_out, 1)

            def dequantise(b, k):
                if k == 1:
                    nc.gpsimd.tensor_scalar(nf4_w[:, :], nf4_q[:, :], 0.0, NF4[0], ALU.is_equal, ALU.mult).then_inc(nf4_done, 1)
                if k % 2 == 1 and k < UNITS - 1:
                    n = k // 2 + 1
                    nc.gpsimd.tensor_scalar(nf4_pick[:, :], nf4_q[:, :], float(n), NF4[n], ALU.is_equal, ALU.mult)\
                        .then_inc(nf4_done, 1)
                elif k == UNITS - 1:
                    blocks = nf4_w[:, :].rearrange("p (k n) -> p k n", n=64)
                    nc.gpsimd.tensor_tensor(blocks, blocks, nf4_scale[:, :].unsqueeze(2).to_broadcast([P, NF4_W // 64, 64]),
                                            ALU.mult).then_inc(nf4_done, 1)
                elif k > 0:
                    nc.gpsimd.tensor_tensor(nf4_w[:, :], nf4_w[:, :], nf4_pick[:, :], ALU.add).then_inc(nf4_done, 1)

            pool.wait_ge(const_made, 1)
            power(0)

            def body(b):
                last = isinstance(b, int) and b == B - 1
                for k in range(UNITS):
                    g = UNITS * b + k
                    pair, s = k // SC, k % SC
                    pool.wait_ge(inv_ready, g + 1)
                    if pair == 0:
                        pool.wait_ge(evacuated["V"], 8 * b + s + 1)
                    wait(pool, pv_done, g - 1 if not isinstance(g, int) or g > 1 else 0)
                    if k == 1:
                        pool.wait_ge(nf4_q_loaded, 16 * b + 16)
                        wait(pool, nf4_stored, 16 * b)
                    elif k > 1:
                        pool.wait_ge(nf4_done, 32 * b + k)
                    if k == UNITS - 1:
                        pool.wait_ge(nf4_scale_loaded, 16 * b + 16)
                    nc.gpsimd.tensor_tensor(
                        vs[:, k % 2, :].rearrange("p (h d) -> p h d", h=2),
                        v_sb[:, s, pair * P:(pair + 1) * P].rearrange("p (h d) -> p h d", h=2),
                        inv_sum[:, k % 2, :].unsqueeze(2).to_broadcast([P, 2, HD]), ALU.mult).then_inc(vs_ready, 1)
                    if k == GN_POWER and not last:
                        power(b + 1)
                    dequantise(b, k)
                    if last:
                        for step in BESIDE_LAST_BATCH.get(k, ()):
                            step1(step, -1)

            body_loop(pool, body)
            for j in range(8):
                for step in BESIDE_LAST_PROJECTION.get(j, ()):
                    step1(step, -1)

        engines = {"sync": sync, "tensor": tensor, "scalar": scalar, "vector": vector, "gpsimd": gpsimd}
        spent = {"QK": (ready["QK"], 16 * B), "QK read": (evacuated["QK"], 16 * B), "scores": (scores_ready[1], UNITS * B),
                 "v": (vs_ready, UNITS * B), "H": evacuated["H"], "nf4": (nf4_stored, 16 * B)}
    return engines, spent


STEPS = (
    [("K", 0, 0), ("K", 1, 0), ("MEAN", FFN0), ("K", 2, 0), ("K", 3, 0), ("K", 0, 1), ("K", 1, 1), ("E", 0), ("VAR", FFN0),
     ("K", 2, 1), ("E", 1), ("DIAG", FFN0), ("K", 3, 1), ("E", 2), ("E", 3), ("CAST", FFN0), ("V", 0), ("V", 1),
     ("T", 0), ("SPLIT", FFN0), ("T", 1), ("X", 0), ("V", 2), ("T", 2), ("X", 1), ("MEAN", FFN1), ("Y", 0, 0), ("Y", 1, 0),
     ("V", 3), ("T", 3), ("X", 2), ("Y", 2, 0), ("VAR", FFN1), ("Y", 3, 0), ("DIAG", FFN1), ("V", 4), ("CAST", FFN1),
     ("T", 4), ("X", 3), ("SPLIT", FFN1), ("V", 5), ("T", 5), ("X", 4), ("MEAN", NEXT0),
     ("V", 6), ("T", 6), ("X", 5), ("V", 7), ("T", 7), ("X", 6), ("Y", 0, 1), ("VAR", NEXT0), ("X", 7), ("Y", 1, 1),
     ("DIAG", NEXT0), ("Y", 2, 1), ("CAST", NEXT0), ("G", 0), ("G", 1), ("G", 2), ("G", 3), ("MEAN", NEXT1), ("Y", 3, 1),
     ("OB", 0), ("A", 0), ("OB", 1), ("A", 1), ("VAR", NEXT1), ("A", 2), ("OB", 2), ("DIAG", NEXT1), ("A", 3),
     ("CAST", NEXT1), ("OB", 3),
     ("WF", 0), ("WF", 1), ("WF", 2), ("WF", 3)]
    + [("O", o, 0) for o in range(CH)] + [("SPLIT", NEXT0)] + [("O", o, 1) for o in range(CH)] + [("SPLIT", NEXT1)])
SHARED = ("K", "V", "Y", "WF", "G", "A", "O")
TILES1 = [s for s in STEPS if s[0] in SHARED]
LATER = {"MEAN", "VAR", "DIAG", "CAST", "SPLIT"}


def step_exists(step, b):
    kind = step[0]
    if kind == "WF":
        return isinstance(b, int) and b == 0
    if not isinstance(b, int):
        return True
    ffn = kind == "Y" or (kind in LATER and step[1] in (FFN0, FFN1))
    following = kind in LATER and not ffn
    return {-1: following, 0: not ffn, B - 1: not following, B: ffn}.get(b, True)


_END = STEPS.index(("O", 0, 1))
_FFN = [s for s in STEPS if s[0] == "Y" or s[0] in LATER and s[1] in (FFN0, FFN1)]
LAST_STEPS = ([(s, B - 1) for s in STEPS[:_END]] + [(("O", 0, 1), B - 1), (("O", 1, 1), B - 1), (("MEAN", FFN0), B)]
              + [(("O", 2, 1), B - 1), (("O", 3, 1), B - 1)]
              + [(s, B) for s in (("VAR", FFN0), ("DIAG", FFN0), ("CAST", FFN0), ("SPLIT", FFN0), ("MEAN", FFN1))]
              + [(s, B) for s in (("Y", 0, 0), ("Y", 1, 0), ("VAR", FFN1), ("DIAG", FFN1), ("Y", 2, 0), ("CAST", FFN1),
                                  ("SPLIT", FFN1), ("Y", 3, 0))]
              + [(("Y", o, 1), B) for o in range(CH)])
assert sorted(s for s, b in LAST_STEPS if b == B) == sorted(_FFN)


def bank1_user_before(step, b):
    n = TILES1.index(step)
    for m in range(n - 1, n - 3 * len(TILES1), -1):
        if (m % len(TILES1)) % 3 != n % 3:
            continue
        prev, prev_b = TILES1[m % len(TILES1)], b + m // len(TILES1)
        if isinstance(prev_b, int) and prev_b < 0:
            return None
        if step_exists(prev, prev_b):
            return prev, prev_b
    return None


def layer1(nc, sem, spent, t_dram, w_kv_t, w_q, w_out_t, w_ffn_t, w_lora_dram, b_v, vectors, consts, out):
    ctx = ExitStack()

    def sb(name, shape, dt=F32):
        return ctx.enter_context(nc.sbuf_tensor(name, shape, dt))

    with ctx:
        used = [0]

        def part(name, shape, dt=F32):
            used[0] += -(-int(np.prod(shape[1:])) * 4 // 32) * 32
            return sb(name, shape, dt)

        ke = part("ke", [P, CH, L])
        g_sb = ke[:, 0:2, :].rearrange("p a (b n) -> p (a b) n", b=2)
        xc = part("xc", [P, CH, L])
        wkv = part("wkv", [P, 2, CH, 2 * C], F32R)
        total = part("total", [P, HALF])
        diag = part("diag", [P, 4, P])
        bv_rows = part("bv1_rows", [P, C])
        cst = part("cst", [P, 3, P])
        MEAN_OF, ONES, IDENT = range(3)
        bias = part("bias1", [P, 3, CH])
        BQ, BK, BO = range(3)
        neg_half = part("neg_half1", [P, 4])
        var_eps = part("var_eps1", [P, 4])
        rstd = part("rstd1", [P, 4])
        k_neg_max = part("k_neg_max", [P, CH])
        k_sum = part("k_sum", [P, CH])
        k_inv = part("k_inv", [P, CH])
        ob = part("ob", [P, CH])
        part("gap", [P, 72 * 256 - used[0] // 4])
        wo = part("wo", [P, CH, C])
        tn1 = part("tn1", [P, 2, CH, L], F32R)
        kt_sb = part("kt_sb", [P, 2, C])
        v_sb = part("v1_sb", [P, 2, C])
        a_lo = part("a_lo", [P, CH, C], F32R)
        wq = part("wq", [P, CH, C])
        tn2 = part("tn2", [P, 2, CH, HALF], F32R)
        t2 = part("t2", [P, CH, L])
        wf = part("wf", [P, 2, CH, C], F32R)
        a_hi = part("a_hi", [P, CH, C], F32R)
        sq = part("sq", [P, CH, HALF])
        resid = part("resid", [P, 2, HALF])
        ctx_sb = part("ctx_sb", [P, PAIRS, P])
        late_res = [w[:, 2 * i:2 * i + 2, :].rearrange("p a n -> p (a n)") for w in (wo, wq) for i in range(2)]
        matrix = {"A": {HI: a_hi, LO: a_lo}, "WF": {HI: wf[:, HI, :, :], LO: wf[:, LO, :, :]}}

        tile_ps = [ctx.enter_context(nc.psum_tensor(f"tile{i}", [P, HALF], F32)) for i in range(3)]
        kt_ps = [ctx.enter_context(nc.psum_tensor(f"kt_ps{i}", [P, HALF], F32)) for i in range(2)]
        ctx_ps = ctx.enter_context(nc.psum_tensor("ctx_ps", [P, PAIRS, P], F32))
        cast_ps = ctx.enter_context(nc.psum_tensor("cast_ps", [P, HALF], F32))
        var_ps = ctx.enter_context(nc.psum_tensor("var_ps", [P, HALF], F32))

        names = SHARED + ("T", "X", "OB")
        ready = {k: sem(f"l1_{k}_ready") for k in names}
        evacuated = {k: sem(f"l1_{k}_evacuated") for k in names}
        per = {"K": 8, "V": 8, "Y": 8, "WF": 4, "G": 4, "OB": 4, "A": 4, "O": 8, "T": 8, "X": 8}
        const_loaded, kv_loaded, kv_hi, kv_split = sem("l1_const_loaded"), sem("kv_loaded"), sem("kv_hi"), sem("kv_split")
        const_made, ctx_cleared = sem("l1_const_made"), sem("ctx_cleared")
        projections_loaded, ffn_loaded = sem("projections_loaded"), sem("ffn_loaded")
        xc_loaded = [sem(f"xc_loaded{h}") for h in range(2)]
        resid_loaded = [sem(f"resid_loaded{h}") for h in range(2)]
        stored = [sem(f"out_stored{h}") for h in range(2)]
        pool_chain, late_chain, total_ready = sem("pool_chain"), sem("late_chain"), sem("total_ready")
        mean_ready, centred, squared, sq_total_ready = sem("mean_ready"), sem("centred"), sem("squared"), sem("sq_total_ready")
        var_ready, eps_added, rstd_ready = sem("var_ready"), sem("eps_added"), sem("rstd_ready")
        diag_ready, cast_ready, normalised = sem("diag_ready"), sem("cast_ready"), sem("normalised")
        hi_done = {n: sem(f"norm{n}_hi_done") for n in (1, 2)}
        lo_done = {n: sem(f"norm{n}_lo_done") for n in (1, 2)}
        late_normalised, late_hi, late_lo = sem("late_normalised"), sem("late_hi"), sem("late_lo")
        matrix_hi_done = {"A": sem("a_mat_hi_done"), "WF": sem("wf_hi_done")}
        k_max_ready, k_exp_done, k_inv_ready, ctx_done = sem("k_max_ready"), sem("k_exp_done"), sem("k_inv_ready"), sem("ctx_done")

        def number(step):
            kind = step[0]
            if kind in ("K", "Y", "O"):
                return CH * step[2] + step[1]
            return step[1]

        def count(step, b):
            return per[step[0]] * (b - 1 if step[0] == "Y" else b) + number(step) + 1

        def job_index(b, job):
            return 4 * b + job - {-1: -2, B: 2}.get(b, 0) if isinstance(b, int) else 4 * b + job

        def norm_of(b, job):
            return (2, b - 1, job) if job in (FFN0, FFN1) else (1, b + 1, job - 2)

        def halves(t, half):
            return t[:, :, half * HALF:(half + 1) * HALF]

        def late_tn(part, half):
            return tn2[:, part, :, :] if half == 0 else halves(tn1[:, part, :, :], half)

        def wait(eng, s, value):
            if not isinstance(value, int) or value > 0:
                eng.wait_ge(s, value)

        def iterations(eng, step):
            def iteration(b):
                for s in STEPS:
                    if step_exists(s, b):
                        step(s, b)
            iteration(0)
            with eng.Fori(1, B - 1) as b:
                iteration(b)
            for s, b in LAST_STEPS:
                if step_exists(s, b):
                    step(s, b)

        def sync(sp):
            def load_t(b, half):
                if not isinstance(b, int) or b > 1:
                    sp.wait_ge(lo_done[2], 2 * (b - 2) + half + 1)
                elif b == 1:
                    sp.wait_ge(lo_done[1], half + 1)
                sp.dma_start(halves(xc, half), t_dram[b].rearrange("(c p) l -> p c l", p=P)[:, :, half * HALF:(half + 1) * HALF])\
                    .then_inc(xc_loaded[half], 16)

            def step(s, b):
                kind = s[0]
                if kind == "SPLIT" and s[1] == FFN0 and not (isinstance(b, int) and b >= B - 1):
                    load_t(b + 1, 0)
                if kind == "SPLIT" and s[1] == FFN1 and not (isinstance(b, int) and b >= B - 1):
                    load_t(b + 1, 1)
                if kind == "O":
                    n = number(s)
                    wait(sp, evacuated["O"], 8 * b + n - 1)
                    sp.dma_start(resid[:, n % 2, :], t_dram[b, s[1] * P:(s[1] + 1) * P, s[2] * HALF:(s[2] + 1) * HALF])\
                        .then_inc(resid_loaded[n % 2], 16)
                if kind == "Y" and s[2] == 1 and isinstance(b, int) and b == B:
                    sp.wait_ge(evacuated["Y"], count(s, b))
                    sp.dma_start(out[b - 1, s[1] * P:(s[1] + 1) * P, HALF:], t2[:, s[1], HALF:]).then_inc(stored[1], 16)
                elif kind == "Y" and s[1] == CH - 1:
                    sp.wait_ge(evacuated["Y"], count(s, b))
                    sp.dma_start(out[b - 1].rearrange("(c p) l -> p c l", p=P)[:, :, s[2] * HALF:(s[2] + 1) * HALF],
                                 halves(t2, s[2])).then_inc(stored[s[2]], 16)

            def loads(what):
                if what == "wv spent":
                    sp.dma_start(ke[:, :, :], w_kv_t.rearrange("(c p) n -> p c n", p=P)).then_inc(kv_loaded, 16)
                else:
                    load_t(0, 0)
                    sp.dma_start(cst[:, :, :], consts).then_inc(const_loaded, 16)
                    sp.dma_start(bias[:, :, :], vectors).then_inc(const_loaded, 16)
                    sp.dma_start(bv_rows[:, :], b_v.partition_broadcast(P)).then_inc(const_loaded, 16)
                    load_t(0, 1)

            def rest():
                sp.dma_start(wo[:, :, :], w_out_t.rearrange("(c p) n -> p c n", p=P)).then_inc(projections_loaded, 16)
                sp.dma_start(wq[:, :, :], w_q.rearrange("(c p) n -> p c n", p=P)).then_inc(projections_loaded, 16)
                load_t(1, 0)
                load_t(1, 1)
                sp.dma_start(w_lora, w_lora_dram.rearrange("(c d) (r h) n -> (d r) c (h n)", d=2, h=2)).then_inc(ffn_loaded, 16)
                sp.dma_start(w_raw, w_ffn_t.rearrange("(c p) n -> p c n", p=P)).then_inc(ffn_loaded, 16)
                iterations(sp, step)
                sp.wait_ge(stored[0], 16 * B)
                sp.wait_ge(stored[1], 16 * (B - 1 + CH))

            return loads, rest

        w_raw = t2[:, 0:2, :].rearrange("p a (b n) -> p (a b) n", b=2)
        w_lora = t2[:, 2:4, :].rearrange("p a (b n) -> p (a b) n", b=2)

        def tensor(pe):
            def split_product(out_ap, stationary, moving, before_chunk=None):
                for c in range(CH):
                    if before_chunk:
                        before_chunk(c)
                    for n, (a, m) in enumerate(SPLITS):
                        mm = pe.matmul(out_ap, stationary(a, c), moving(m, c), start=(c == 0 and n == 0),
                                       stop=(c == CH - 1 and n == len(SPLITS) - 1))
                return mm

            def shared_tile(s, b):
                kind = s[0]
                bank = TILES1.index(s) % 3
                ps = tile_ps[bank]
                before = bank1_user_before(s, b)
                if not before:
                    pe.wait_ge(spent["H"], 8 * (B - 1) + 5 + bank)
                else:
                    wait(pe, evacuated[before[0][0]], count(*before))
                if kind == "K":
                    d, half = s[1], s[2]
                    pe.wait_ge(lo_done[1], 2 * b + half + 1)
                    mm = split_product(ps[:, :], lambda a, c: wkv[:, a, c, d * P:(d + 1) * P],
                                       lambda m, c: tn1[:, m, c, half * HALF:(half + 1) * HALF])
                elif kind == "V":
                    mm = split_product(ps[:, :], lambda a, c: tn1[:, a, c, s[1] * P:(s[1] + 1) * P],
                                       lambda m, c: wkv[:, m, c, C:])
                elif kind == "Y":
                    late = isinstance(b, int) and b == B
                    if not late:
                        pe.wait_ge(lo_done[2], 2 * (b - 1) + s[2] + 1)
                    mm = split_product(ps[:, :], lambda a, c: wf[:, a, c, s[1] * P:(s[1] + 1) * P],
                                       lambda m, c: late_tn(m, s[2])[:, c, :] if late else tn2[:, m, c, :],
                                       (lambda c: pe.wait_ge(late_lo, CH * s[2] + c + 1)) if late and s[1] == 0 else None)
                elif kind == "WF":
                    pe.wait_ge(ffn_loaded, 32)
                    for m in range(CH):
                        mm = pe.matmul(ps[:, :], w_lora[:, m, s[1] * P:(s[1] + 1) * P], w_raw[:, m, :],
                                       start=(m == 0), stop=(m == CH - 1))
                elif kind == "G":
                    pe.wait_ge(ctx_done, b + 1)
                    if isinstance(b, int) and b == 0 and s[1] == 0:
                        pe.wait_ge(projections_loaded, 32)
                    mm = pe.matmul(ps[:, :], ctx_sb[:, s[1], :], wo[:, s[1], :], start=True, stop=True)
                elif kind == "A":
                    pe.wait_ge(evacuated["G"], 4 * b + 4)
                    for d in range(CH):
                        mm = pe.matmul(ps[:, :], wq[:, d, s[1] * P:(s[1] + 1) * P], g_sb[:, d, :],
                                       start=(d == 0), stop=(d == CH - 1))
                else:
                    mm = split_product(ps[:, :], lambda a, c: matrix["A"][a][:, c, s[1] * P:(s[1] + 1) * P],
                                       lambda m, c: tn1[:, m, c, s[2] * HALF:(s[2] + 1) * HALF],
                                       (lambda c: pe.wait_ge(evacuated["A"], 4 * b + c + 1)) if number(s) == 0 else None)
                mm.then_inc(ready[kind], 1)

            def step(s, b):
                kind = s[0]
                if kind in SHARED:
                    shared_tile(s, b)
                elif kind == "T":
                    n = s[1]
                    if n == 0:
                        pe.wait_ge(k_exp_done, CH * b + CH)
                        if isinstance(b, int) and b == 0:
                            pe.wait_ge(spent["H"], 8 * B)
                    wait(pe, evacuated["T"], 8 * b + n - 1)
                    for d in range(CH):
                        mm = pe.transpose(kt_ps[n % 2][:, d * P:(d + 1) * P], ke[:, d, n * P:(n + 1) * P], cst[:, IDENT, :])
                    mm.then_inc(ready["T"], 1)
                elif kind == "OB":
                    o = s[1]
                    if o == 0:
                        pe.wait_ge(evacuated["G"], 4 * b + 4)
                    for d in range(CH):
                        mm = pe.matmul(ctx_ps[:, 0, o:o + 1], g_sb[:, d, o * P:(o + 1) * P], bias[:, BQ, d:d + 1],
                                       start=(d == 0), stop=(d == CH - 1))
                    mm.then_inc(ready["OB"], 1)
                elif kind == "X":
                    n = s[1]
                    pe.wait_ge(evacuated["V"], 8 * b + n + 1)
                    pe.wait_ge(evacuated["T"], 8 * b + n + 1)
                    if n == 0:
                        wait(pe, evacuated["OB"], b)
                    for p in range(PAIRS):
                        for h in range(2):
                            rows, cols = slice(64 * h, 64 * h + 64), slice(p * P + 64 * h, p * P + 64 * h + 64)
                            mm = pe.matmul(ctx_ps[rows, p, rows], v_sb[:, n % 2, cols], kt_sb[:, n % 2, cols],
                                           start=(n == 0 and p == 0), stop=(n == 7), skip_group_check=True)
                    mm.then_inc(ready["X"], 1)
                elif kind == "MEAN":
                    j = job_index(b, s[1])
                    pe.wait_ge(total_ready, j + 1)
                    if isinstance(j, int) and j == 0:
                        pe.wait_ge(const_loaded, 16 * 3)
                        pe.wait_ge(*spent["QK read"])
                    if isinstance(b, int) and b == B and s[1] == FFN1:
                        pe.wait_ge(late_normalised, CH)
                    else:
                        wait(pe, normalised, j)
                    pe.matmul(cast_ps[:, :], cst[:, MEAN_OF, :], total[:, :], start=True, stop=True).then_inc(mean_ready, 1)
                elif kind == "VAR":
                    j = job_index(b, s[1])
                    pe.wait_ge(sq_total_ready, j + 1)
                    wait(pe, eps_added, j)
                    for n in range(4):
                        mm = pe.matmul(var_ps[:, n:n + 1], total[:, n * P:(n + 1) * P], cst[:, MEAN_OF, 0:1],
                                       start=True, stop=True)
                    mm.then_inc(var_ready, 1)
                elif kind == "CAST":
                    j = job_index(b, s[1])
                    pe.wait_ge(diag_ready, j + 1)
                    pe.matmul(cast_ps[:, :], cst[:, ONES, :], diag[:, :, :].rearrange("p a n -> p (a n)"),
                              start=True, stop=True).then_inc(cast_ready, 1)

            def rest():
                pe.wait_ge(kv_split, CH)
                iterations(pe, step)

            return step, rest

        def scalar(act):
            def step(s, b):
                kind = s[0]
                ps = tile_ps[TILES1.index(s) % 3] if kind in SHARED else None
                if kind == "KV":
                    if s[1] == 0:
                        act.wait_ge(kv_loaded, 16)
                        act.wait_ge(*spent["QK"])
                    nc.scalar.activation(wkv[:, HI, s[1], :], ke[:, s[1], :], ACT.Copy).then_inc(kv_hi, 1)
                elif kind == "K":
                    d, half = s[1], s[2]
                    act.wait_ge(ready["K"], count(s, b))
                    wait(act, ready["A"], 4 * b)
                    nc.scalar.activation(ke[:, d, half * HALF:(half + 1) * HALF], ps[:, :], ACT.Identity,
                                         bias=bias[:, BK, d:d + 1]).then_inc(evacuated["K"], 1)
                elif kind == "E":
                    d = s[1]
                    act.wait_ge(k_max_ready, CH * b + d + 1)
                    nc.scalar.activation(ke[:, d, :], ke[:, d, :], ACT.Exp, bias=k_neg_max[:, d:d + 1],
                                         accum_out=k_sum[:, d:d + 1]).then_inc(k_exp_done, 1)
                elif kind == "T":
                    act.wait_ge(ready["T"], count(s, b))
                    wait(act, ready["X"], 8 * b + s[1] - 1)
                    nc.scalar.activation(kt_sb[:, s[1] % 2, :], kt_ps[s[1] % 2][:, :], ACT.Copy).then_inc(evacuated["T"], 1)
                elif kind == "G":
                    act.wait_ge(ready["G"], count(s, b))
                    act.wait_ge(k_inv_ready, b + 1)
                    nc.scalar.activation(g_sb[:, s[1], :], ps[:, :], ACT.Copy, scale=k_inv[:, s[1]:s[1] + 1])\
                        .then_inc(evacuated["G"], 1)
                elif kind in ("A", "WF"):
                    act.wait_ge(ready[kind], count(s, b))
                    if kind == "A":
                        wait(act, ready["O"], 8 * b)
                    nc.scalar.activation(matrix[kind][HI][:, s[1], :], ps[:, :], ACT.Copy).then_inc(matrix_hi_done[kind], 1)
                elif kind == "MEAN":
                    j = job_index(b, s[1])
                    n, bb, half = norm_of(b, s[1])
                    act.wait_ge(centred, j + 1)
                    wait(act, sq_total_ready, j)
                    nc.scalar.activation(sq[:, :, :], halves(xc, half), ACT.Square).then_inc(squared, 1)
                elif kind == "SPLIT":
                    n, bb, half = norm_of(b, s[1])
                    if isinstance(b, int) and b == B:
                        for c in range(CH):
                            act.wait_ge(late_normalised, CH * half + c + 1)
                            nc.scalar.activation(late_tn(HI, half)[:, c, :], halves(xc, half)[:, c, :], ACT.Copy).then_inc(late_hi, 1)
                        return
                    act.wait_ge(normalised, job_index(b, s[1]) + 1)
                    if n == 1:
                        if isinstance(bb, int) and bb == 0 and half == 0:
                            act.wait_ge(*spent["scores"])
                        wait(act, ready["O"], 8 * (bb - 1) + 4 * (half + 1) if not isinstance(bb, int) or bb > 0 else 0)
                        dst = halves(tn1[:, HI, :, :], half)
                    else:
                        if half == 1:
                            act.wait_ge(ready["Y"], 8 * bb + 4)
                        dst = tn2[:, HI, :, :]
                    nc.scalar.activation(dst, halves(xc, half), ACT.Copy).then_inc(hi_done[n], 1)

            def rest():
                iterations(act, step)

            return step, rest

        def vector(dve):
            def late_sum(src, chained, last_sem):
                for c in range(1, CH):
                    if c > 1:
                        dve.wait_ge(late_chain, chained + c - 1)
                    ins = nc.vector.tensor_tensor(total[:, :], src[:, 0, :] if c == 1 else total[:, :], src[:, c, :], ALU.add)
                    ins.then_inc(late_chain if c < CH - 1 else last_sem, 1)

            def step(s, b):
                kind = s[0]
                ps = tile_ps[TILES1.index(s) % 3] if kind in SHARED else None
                if kind == "INIT":
                    dve.wait_ge(*spent["QK"])
                    nc.vector.memset(neg_half[:, :], -0.5).then_inc(const_made, 1)
                elif kind == "KV":
                    dve.wait_ge(kv_hi, s[1] + 1)
                    nc.vector.tensor_tensor(wkv[:, LO, s[1], :], ke[:, s[1], :], wkv[:, HI, s[1], :].bitcast(F32),
                                            ALU.subtract).then_inc(kv_split, 1)
                elif kind == "E":
                    d = s[1]
                    dve.wait_ge(evacuated["K"], 8 * b + 4 + d + 1)
                    nc.vector.tensor_reduce(k_neg_max[:, d:d + 1], ke[:, d, :], AX_X, ALU.max, negate=True)\
                        .then_inc(k_max_ready, 1)
                elif kind == "V":
                    n = s[1]
                    dve.wait_ge(ready["V"], count(s, b))
                    wait(dve, ready["X"], 8 * b + n - 1)
                    nc.vector.tensor_tensor(v_sb[:, n % 2, :], ps[:, :], bv_rows[:, :], ALU.add).then_inc(evacuated["V"], 1)
                elif kind == "X" and s[1] == 7:
                    dve.wait_ge(k_exp_done, CH * (b + 1))
                    nc.vector.reciprocal(k_inv[:, :], k_sum[:, :]).then_inc(k_inv_ready, 1)
                    dve.wait_ge(ready["X"], 8 * (b + 1))
                    for h in range(2):
                        rows = slice(64 * h, 64 * h + 64)
                        ins = nc.vector.tensor_copy(ctx_sb[rows, :, rows], ctx_ps[rows, :, rows])
                    ins.then_inc(ctx_done, 1)
                elif kind == "OB" and s[1] == CH - 1:
                    dve.wait_ge(ready["OB"], count(s, b))
                    nc.vector.tensor_tensor(ob[:, :], ctx_ps[:, 0, 0:CH], bias[:, BO, :], ALU.add).then_inc(evacuated["OB"], 1)
                elif kind in ("A", "WF"):
                    dve.wait_ge(matrix_hi_done[kind], count(s, b))
                    hi, lo = matrix[kind][HI], matrix[kind][LO]
                    nc.vector.tensor_tensor(lo[:, s[1], :], ps[:, :], hi[:, s[1], :].bitcast(F32), ALU.subtract)\
                        .then_inc(evacuated[kind], 1)
                elif kind == "O":
                    o, half, n = s[1], s[2], number(s)
                    dve.wait_ge(ready["O"], count(s, b))
                    dve.wait_ge(evacuated["OB"], b + 1)
                    dve.wait_ge(resid_loaded[n % 2], 16 * (4 * b + n // 2 + 1))
                    if o == 0:
                        wait(dve, stored[half], 16 * b)
                    nc.vector.scalar_tensor_tensor(out=t2[:, o, half * HALF:(half + 1) * HALF], in0=ps[:, :],
                                                   scalar=ob[:, o:o + 1], in1=resid[:, n % 2, :],
                                                   op0=ALU.add, op1=ALU.add).then_inc(evacuated["O"], 1)
                elif kind == "Y":
                    o, half = s[1], s[2]
                    dve.wait_ge(ready["Y"], count(s, b))
                    dst = t2[:, o, half * HALF:(half + 1) * HALF]
                    nc.vector.tensor_tensor(dst, ps[:, :], dst, ALU.add).then_inc(evacuated["Y"], 1)
                elif kind == "MEAN":
                    j = job_index(b, s[1])
                    n, bb, half = norm_of(b, s[1])
                    src = halves(t2 if n == 2 else xc, half)
                    dve.wait_ge(mean_ready, j + 1)
                    nc.vector.tensor_tensor(halves(xc, half), src, cast_ps[:, :].unsqueeze(1).to_broadcast([P, CH, HALF]),
                                            ALU.subtract).then_inc(centred, 1)
                    if isinstance(b, int) and b == B:
                        dve.wait_ge(squared, j + 1)
                        late_sum(sq, 2 * half, sq_total_ready)
                elif kind == "VAR":
                    j = job_index(b, s[1])
                    dve.wait_ge(var_ready, j + 1)
                    nc.vector.tensor_scalar(var_eps[:, :], var_ps[:, 0:4], LN_EPS, None, ALU.add).then_inc(eps_added, 1)
                elif kind == "DIAG":
                    j = job_index(b, s[1])
                    dve.wait_ge(rstd_ready, j + 1)
                    wait(dve, cast_ready, j)
                    nc.vector.tensor_tensor(diag[:, :, :], cst[:, IDENT, :].unsqueeze(1).to_broadcast([P, 4, P]),
                                            rstd[:, :].unsqueeze(2).to_broadcast([P, 4, P]), ALU.mult).then_inc(diag_ready, 1)
                elif kind == "CAST":
                    j = job_index(b, s[1])
                    half = norm_of(b, s[1])[2]
                    dve.wait_ge(cast_ready, j + 1)
                    if isinstance(b, int) and b == B:
                        for c in range(CH):
                            part = halves(xc, half)[:, c, :]
                            nc.vector.tensor_tensor(part, part, cast_ps[:, :], ALU.mult).then_inc(late_normalised, 1)
                        return
                    nc.vector.tensor_tensor(halves(xc, half), halves(xc, half),
                                            cast_ps[:, :].unsqueeze(1).to_broadcast([P, CH, HALF]), ALU.mult)\
                        .then_inc(normalised, 1)
                elif kind == "SPLIT":
                    n, bb, half = norm_of(b, s[1])
                    if isinstance(b, int) and b == B:
                        for c in range(CH):
                            dve.wait_ge(late_hi, CH * half + c + 1)
                            nc.vector.tensor_tensor(late_tn(LO, half)[:, c, :], halves(xc, half)[:, c, :],
                                                    late_tn(HI, half)[:, c, :].bitcast(F32), ALU.subtract).then_inc(late_lo, 1)
                        return
                    dve.wait_ge(hi_done[n], 2 * bb + half + 1)
                    if isinstance(bb, int) and n == 1 and bb == 0 and half == 0:
                        dve.wait_ge(*spent["v"])
                    if n == 1:
                        hi, dst = halves(tn1[:, HI, :, :], half), halves(tn1[:, LO, :, :], half)
                    else:
                        hi, dst = tn2[:, HI, :, :], tn2[:, LO, :, :]
                    nc.vector.tensor_tensor(dst, halves(xc, half), hi.bitcast(F32), ALU.subtract).then_inc(lo_done[n], 1)

            def rest():
                dve.wait_ge(*spent["nf4"])
                nc.vector.memset(ctx_sb[:, :, :], 0.0).then_inc(ctx_cleared, 1)
                iterations(dve, step)

            return step, rest

        def gpsimd(pool):
            def norm_sum(b, job, part):
                j = job_index(b, job)
                n, bb, half = norm_of(b, job)
                if part == 6:
                    pool.wait_ge(eps_added, j + 1)
                    nc.gpsimd.tensor_tensor(rstd[:, :], var_eps[:, :], neg_half[:, :], ALU.pow).then_inc(rstd_ready, 1)
                    return
                src = sq[:, :, :] if part >= 3 else halves(t2 if n == 2 else xc, half)
                if part == 0:
                    if n == 2:
                        pool.wait_ge(evacuated["O"], 8 * bb + 4 * (half + 1))
                    else:
                        pool.wait_ge(xc_loaded[half], 16 * (bb + 1))
                    wait(pool, var_ready, j)
                elif part == 3:
                    pool.wait_ge(squared, j + 1)
                    pool.wait_ge(mean_ready, j + 1)
                else:
                    late = 2 if isinstance(b, int) and b == B and job == FFN1 else 0
                    pool.wait_ge(pool_chain, 4 * j + part - part // 3 - late)
                if part % 3 == 0:
                    ins = nc.gpsimd.tensor_tensor(total[:, :], src[:, 0, :], src[:, 1, :], ALU.add)
                else:
                    ins = nc.gpsimd.tensor_tensor(total[:, :], total[:, :], src[:, part % 3 + 1, :], ALU.add)
                ins.then_inc({2: total_ready, 5: sq_total_ready}.get(part, pool_chain), 1)

            def step(s, b):
                if s[0] == "INIT":
                    pool.wait_ge(const_made, 1)
                elif s[0] == "SUM":
                    norm_sum(b, s[1], s[2])
                elif s[0] == "MEAN" and not (isinstance(b, int) and b < 0):
                    for part in range(7) if not (isinstance(b, int) and b == B) else (0, 1, 2, 6):
                        norm_sum(b, s[1], part)

            def rest():
                iterations(pool, step)

            return step, rest

    return {"sync": sync, "tensor": tensor, "scalar": scalar, "vector": vector, "gpsimd": gpsimd}, late_res


def program(nc, x, w_qk_t, w_v_t, w_proj_t, b_v0, vectors0, group_mean,
            w_kv_t, w_q, w_out_t, w_ffn_t, qidx, scales, b_v1, vectors1, consts, t_dram, w_lora_dram, out):
    with ExitStack() as ctx:
        def sem(name):
            return ctx.enter_context(nc.semaphore(name))

        first, spent = layer0(nc, sem, x, w_qk_t, w_v_t, w_proj_t, b_v0, vectors0, group_mean, qidx, scales, t_dram, w_lora_dram)
        second, late_res = layer1(nc, sem, spent, t_dram, w_kv_t, w_q, w_out_t, w_ffn_t, w_lora_dram, b_v1, vectors1, consts, out)
        block = ctx.enter_context(nc.Block())

        @block.sync
        def _(sp):
            loads1, rest1 = second["sync"](sp)
            first["sync"](sp, loads1, late_res)
            rest1()

        @block.tensor
        def _(pe):
            step1, rest1 = second["tensor"](pe)
            first["tensor"](pe, step1)
            rest1()

        @block.scalar
        def _(act):
            step1, rest1 = second["scalar"](act)
            first["scalar"](act, step1)
            rest1()

        @block.vector
        def _(dve):
            step1, rest1 = second["vector"](dve)
            first["vector"](dve, step1, late_res)
            rest1()

        @block.gpsimd
        def _(pool):
            step1, rest1 = second["gpsimd"](pool)
            first["gpsimd"](pool, step1)
            rest1()


def kernel(**inputs):
    import concourse.bacc as bacc
    from concourse.bass_utils import run_bass_kernel_spmd

    def columns(*vs):
        return np.ascontiguousarray(np.stack([v.reshape(CH, P).T for v in vs], axis=1))

    a = {k: np.asarray(v) for k, v in inputs.items()}
    w0 = a["L0_conv_w_qkv"].reshape(HEADS, 3, HD, C)
    b0 = a["L0_conv_b_qkv"].reshape(HEADS, 3, HD)
    wq0, wk0, wv0 = (w0[:, i].reshape(C, C) for i in range(3))
    bq0, bk0, bv0 = (b0[:, i].reshape(C) for i in range(3))
    w1, b1 = a["L1_attn_W_qkv"], a["L1_attn_b_qkv"]
    same_group = np.arange(P)[:, None] // (C // GROUPS) == np.arange(P)[None, :] // (C // GROUPS)
    arrays = {
        "x": a["x"].reshape(B, C, L),
        "w_qk_t": np.concatenate([wq0.T, wk0.T], axis=1),
        "w_v_t": wv0.T,
        "w_proj_t": a["L0_conv_w_proj"].T,
        "b_v0": bv0,
        "vectors0": columns(bq0, bk0, a["L0_conv_b_proj"], a["L0_conv_gn_w"], a["L0_conv_gn_b"]),
        "group_mean": np.where(same_group, np.float32(GROUPS / C), np.float32(0)),
        "w_kv_t": w1[C:].T,
        "w_q": w1[:C],
        "w_out_t": a["L1_attn_W_out"].T,
        "w_ffn_t": a["L1_ffn_W"].T,
        "qidx": a["L1_ffn_qidx"].reshape(B, P, NF4_W),
        "scales": a["L1_ffn_scales"].reshape(B, P, NF4_W // 64),
        "b_v1": b1[2 * C:],
        "vectors1": columns(b1[:C], b1[C:2 * C], a["L1_attn_b_out"]),
        "consts": np.ascontiguousarray(np.stack(
            [np.full((P, P), 1 / C, np.float32), np.ones((P, P), np.float32), np.eye(P, dtype=np.float32)], axis=1)),
    }
    arrays = {f"in_{k}": np.ascontiguousarray(v) for k, v in arrays.items()}

    nc = bacc.Bacc("TRN2", target_bir_lowering=False, num_devices=1)
    args = [nc.dram_tensor(k, v.shape, mybir.dt.from_np(v.dtype), kind="ExternalInput").ap() for k, v in arrays.items()]
    args.append(nc.dram_tensor("t_between", (B, C, L), F32).ap())
    args.append(nc.dram_tensor("w_lora", (B, P, NF4_W), F32).ap())
    args.append(nc.dram_tensor("out_0", (B, C, L), F32, kind="ExternalOutput").ap())
    program(nc, *args)
    r = run_bass_kernel_spmd(nc, [arrays], core_ids=[0])
    return r.results[0]["out_0"].reshape(B, C, 32, 32)
```
